# Optimizing a Trainium2 kernel written in Bass

```python
import numpy as np
import jax
import jax.numpy as jnp

def _softmax(x, axis=-1):
    return jax.nn.softmax(x, axis=axis)

def _gelu(x):
    return jax.nn.gelu(x, approximate=True)

def _silu(x):
    return jax.nn.silu(x)

def _sigmoid(x):
    return jax.nn.sigmoid(x)

def _layernorm(x, axis=-1, eps=1e-05):
    m = jnp.mean(x, axis=axis, keepdims=True)
    v = jnp.var(x, axis=axis, keepdims=True)
    return (x - m) / jnp.sqrt(v + eps)

def _scatter_add(tgt, idx, src, axis=0):
    return tgt.at[idx].add(src)

def _segment_sum(src, seg, n):
    return jax.ops.segment_sum(src, seg, n)
kernel_name = 'mk_decoder_preln_d1_seqx_r4_de9f5f'

def setup_inputs(seed: int=0):
    np.random.seed(seed)
    _w = jnp.asarray

    def _rec_inputs():
        import jax
        import jax.numpy as jnp
        _rk = jax.random.key(seed)
        x = -0.0003929 + 0.9999 * jax.random.normal(jax.random.fold_in(_rk, 1), (16, 128, 256), jnp.float32)
        _lenS = 128 - jax.random.randint(jax.random.fold_in(_rk, 7), (16,), 0, max(1, 128 // 4) + 1, jnp.int32)
        _lenS2 = 128 - jax.random.randint(jax.random.fold_in(_rk, 8), (16,), 0, max(1, 128 // 4) + 1, jnp.int32)
        _ctx_512P = jax.random.normal(jax.random.fold_in(_rk, 11), (16, 16, 128), jnp.float32)
        _ctx_512c = jax.random.dirichlet(jax.random.fold_in(_rk, 511), 0.3 * jnp.ones((16,), jnp.float32), (16, 128))
        _ctx_512t = jnp.einsum('bsk,bkd->bsd', _ctx_512c, _ctx_512P)
        _ctx_512t = _ctx_512t * jax.lax.rsqrt(jnp.mean(jnp.square(_ctx_512t)) + 1e-12) * 0.953939
        ctx_512 = -1.39393e-06 + 0.999914 * (_ctx_512t + 0.3 * jax.random.normal(jax.random.fold_in(_rk, 611), (16, 128, 128), jnp.float32))
        return (x, ctx_512)
    x, ctx_512 = _rec_inputs()

    def _L0_attn_setup():
        import jax, jax.numpy as jnp
        import numpy as np
        B, H, D, K, F = (8, 16, 256, 64, 1024)
        N, S = (4, 1024)
        LN_EPS = 1e-06

        def _layer_norm(x, scale, bias):
            m = jnp.mean(x, axis=-1, keepdims=True)
            v = jnp.mean(jnp.square(x - m), axis=-1, keepdims=True)
            return (x - m) * jax.lax.rsqrt(v + LN_EPS) * scale + bias

        def _feature_map(x):
            return jax.nn.elu(x) + 1.0
        key = jax.random.key(seed)
        ks = jax.random.split(key, 9)
        w = lambda k, shape: jax.random.normal(k, shape, jnp.float32) * 0.02
        return {'x': jax.random.normal(ks[0], (N, S, D), jnp.float32), 'Wq': w(ks[1], (B, H, D, K)), 'bq': jnp.zeros((B, H, K), jnp.float32), 'Wk': w(ks[2], (B, H, D, K)), 'bk': jnp.zeros((B, H, K), jnp.float32), 'Wv': w(ks[3], (B, H, D, K)), 'bv': jnp.zeros((B, H, K), jnp.float32), 'Wo': w(ks[4], (B, H * K, D)), 'bo': jnp.zeros((B, D), jnp.float32), 'ln1_s': jnp.ones((B, D), jnp.float32), 'ln1_b': jnp.zeros((B, D), jnp.float32), 'W1': w(ks[5], (B, D, F)), 'b1': jnp.zeros((B, F), jnp.float32), 'W2': w(ks[6], (B, F, D)), 'b2': jnp.zeros((B, D), jnp.float32), 'ln2_s': jnp.ones((B, D), jnp.float32), 'ln2_b': jnp.zeros((B, D), jnp.float32)}
    _L0_attn_all = _L0_attn_setup()
    _L0_attn_in = {k: v for k, v in _L0_attn_all.items() if k in ('Wq', 'bq', 'Wk', 'bk', 'Wv', 'bv', 'Wo', 'bo', 'ln1_s', 'ln1_b', 'W1', 'b1', 'W2', 'b2', 'ln2_s', 'ln2_b')}
    del _L0_attn_all

    def _L0_xattn_setup():
        import jax, jax.numpy as jnp
        import numpy as np
        HEADS = 16
        D_MODEL = 256
        IMG_MODEL = 128
        D_K = D_MODEL // HEADS
        key = jax.random.key(seed)
        ks = jax.random.split(key, 12)
        B, LQ, LKV = (8, 512, 256)
        s_dm = 1.0 / np.sqrt(D_MODEL)
        s_im = 1.0 / np.sqrt(IMG_MODEL)
        return {'q': jax.random.normal(ks[0], (B, LQ, D_MODEL), jnp.float32), 'k': jax.random.normal(ks[1], (B, LKV, IMG_MODEL), jnp.float32), 'v': jax.random.normal(ks[2], (B, LKV, IMG_MODEL), jnp.float32), 'Wq': jax.random.normal(ks[3], (D_MODEL, D_MODEL), jnp.float32) * s_dm, 'bq': jnp.zeros((D_MODEL,), jnp.float32), 'Wk': jax.random.normal(ks[4], (IMG_MODEL, D_MODEL), jnp.float32) * s_im, 'bk': jnp.zeros((D_MODEL,), jnp.float32), 'Wv': jax.random.normal(ks[5], (IMG_MODEL, D_MODEL), jnp.float32) * s_im, 'bv': jnp.zeros((D_MODEL,), jnp.float32), 'Wo': jax.random.normal(ks[6], (D_MODEL, D_MODEL), jnp.float32) * s_dm, 'bo': jnp.zeros((D_MODEL,), jnp.float32)}
    _L0_xattn_all = _L0_xattn_setup()
    _L0_xattn_in = {k: v for k, v in _L0_xattn_all.items() if k in ('Wq', 'bq', 'Wk', 'bk', 'Wv', 'bv', 'Wo', 'bo')}
    del _L0_xattn_all

    def _L0_ffn_setup():
        import jax, jax.numpy as jnp
        import numpy as np
        B, S, H, F, E = (1, 512, 256, 512, 8)

        def _swiglu(x, wg, wu, wd):
            return jax.nn.silu(x @ wg.T) * (x @ wu.T) @ wd.T
        key = jax.random.key(seed)
        ks = jax.random.split(key, 8)
        sc = 1.0 / np.sqrt(H)
        scf = 1.0 / np.sqrt(F)
        return {'hidden_states': jax.random.normal(ks[0], (B, S, H), jnp.float32), 'gate_w': jax.random.normal(ks[1], (E, H), jnp.float32) * sc, 'shared_gate': jax.random.normal(ks[2], (F, H), jnp.float32) * sc, 'shared_up': jax.random.normal(ks[3], (F, H), jnp.float32) * sc, 'shared_down': jax.random.normal(ks[4], (H, F), jnp.float32) * scf, 'r_gate': jax.random.normal(ks[5], (E, F, H), jnp.float32) * sc, 'r_up': jax.random.normal(ks[6], (E, F, H), jnp.float32) * sc, 'r_down': jax.random.normal(ks[7], (E, H, F), jnp.float32) * scf}
    _L0_ffn_all = _L0_ffn_setup()
    _L0_ffn_in = {k: v for k, v in _L0_ffn_all.items() if k in ('gate_w', 'shared_gate', 'shared_up', 'shared_down', 'r_gate', 'r_up', 'r_down')}
    del _L0_ffn_all
    return {'x': x, 'ctx_512': ctx_512, 'L0_attn_Wq': _L0_attn_in['Wq'], 'L0_attn_bq': _L0_attn_in['bq'], 'L0_attn_Wk': _L0_attn_in['Wk'], 'L0_attn_bk': _L0_attn_in['bk'], 'L0_attn_Wv': _L0_attn_in['Wv'], 'L0_attn_bv': _L0_attn_in['bv'], 'L0_attn_Wo': _L0_attn_in['Wo'], 'L0_attn_bo': _L0_attn_in['bo'], 'L0_attn_ln1_s': _L0_attn_in['ln1_s'], 'L0_attn_ln1_b': _L0_attn_in['ln1_b'], 'L0_attn_W1': _L0_attn_in['W1'], 'L0_attn_b1': _L0_attn_in['b1'], 'L0_attn_W2': _L0_attn_in['W2'], 'L0_attn_b2': _L0_attn_in['b2'], 'L0_attn_ln2_s': _L0_attn_in['ln2_s'], 'L0_attn_ln2_b': _L0_attn_in['ln2_b'], 'L0_xattn_Wq': _L0_xattn_in['Wq'], 'L0_xattn_bq': _L0_xattn_in['bq'], 'L0_xattn_Wk': _L0_xattn_in['Wk'], 'L0_xattn_bk': _L0_xattn_in['bk'], 'L0_xattn_Wv': _L0_xattn_in['Wv'], 'L0_xattn_bv': _L0_xattn_in['bv'], 'L0_xattn_Wo': _L0_xattn_in['Wo'], 'L0_xattn_bo': _L0_xattn_in['bo'], 'L0_ffn_gate_w': _L0_ffn_in['gate_w'], 'L0_ffn_shared_gate': _L0_ffn_in['shared_gate'], 'L0_ffn_shared_up': _L0_ffn_in['shared_up'], 'L0_ffn_shared_down': _L0_ffn_in['shared_down'], 'L0_ffn_r_gate': _L0_ffn_in['r_gate'], 'L0_ffn_r_up': _L0_ffn_in['r_up'], 'L0_ffn_r_down': _L0_ffn_in['r_down']}

def reference(x, ctx_512, L0_attn_Wq, L0_attn_bq, L0_attn_Wk, L0_attn_bk, L0_attn_Wv, L0_attn_bv, L0_attn_Wo, L0_attn_bo, L0_attn_ln1_s, L0_attn_ln1_b, L0_attn_W1, L0_attn_b1, L0_attn_W2, L0_attn_b2, L0_attn_ln2_s, L0_attn_ln2_b, L0_xattn_Wq, L0_xattn_bq, L0_xattn_Wk, L0_xattn_bk, L0_xattn_Wv, L0_xattn_bv, L0_xattn_Wo, L0_xattn_bo, L0_ffn_gate_w, L0_ffn_shared_gate, L0_ffn_shared_up, L0_ffn_shared_down, L0_ffn_r_gate, L0_ffn_r_up, L0_ffn_r_down):
    import jax
    import jax.numpy as jnp

    def _L0_attn_ref(x, Wq, bq, Wk, bk, Wv, bv, Wo, bo, ln1_s, ln1_b, W1, b1, W2, b2, ln2_s, ln2_b):
        import jax, jax.numpy as jnp
        import numpy as np
        B, H, D, K, F = (8, 16, 256, 64, 1024)
        N, S = (4, 1024)
        LN_EPS = 1e-06

        def _layer_norm(x, scale, bias):
            m = jnp.mean(x, axis=-1, keepdims=True)
            v = jnp.mean(jnp.square(x - m), axis=-1, keepdims=True)
            return (x - m) * jax.lax.rsqrt(v + LN_EPS) * scale + bias

        def _feature_map(x):
            return jax.nn.elu(x) + 1.0
        n, s, _ = x.shape
        for i in range(B):
            residual = x
            Q = _feature_map(jnp.einsum('nsd,hdk->nshk', x, Wq[i]) + bq[i])
            Kf = _feature_map(jnp.einsum('nsd,hdk->nshk', x, Wk[i]) + bk[i])
            V = jnp.einsum('nsd,hdk->nshk', x, Wv[i]) + bv[i]
            KV = jnp.sum(Kf * V, axis=1)
            sumK = jnp.sum(Kf, axis=1)
            Z = 1.0 / (Q * sumK[:, None] + 1e-06)
            att = Q * KV[:, None] * Z
            att = att.reshape(n, s, H * K)
            y = jax.nn.gelu(att @ Wo[i] + bo[i])
            x = _layer_norm(y + residual, ln1_s[i], ln1_b[i])
            residual = x
            h = jax.nn.gelu(x @ W1[i] + b1[i])
            h = jax.nn.gelu(h @ W2[i] + b2[i])
            x = _layer_norm(h + residual, ln2_s[i], ln2_b[i])
        return x

    def _L0_xattn_ref(q, k, v, Wq, bq, Wk, bk, Wv, bv, Wo, bo):
        import jax, jax.numpy as jnp
        import numpy as np
        HEADS = 16
        D_MODEL = 256
        IMG_MODEL = 128
        D_K = D_MODEL // HEADS
        B, LQ, _ = q.shape
        LKV = k.shape[1]
        qh = (q @ Wq + bq).reshape(B, LQ, HEADS, D_K).transpose(0, 2, 1, 3)
        kh = (k @ Wk + bk).reshape(B, LKV, HEADS, D_K).transpose(0, 2, 1, 3)
        vh = (v @ Wv + bv).reshape(B, LKV, HEADS, D_K).transpose(0, 2, 1, 3)
        scale = 1.0 / np.sqrt(D_K)
        scores = jnp.einsum('bhqd,bhkd->bhqk', qh, kh) * scale
        attn = jax.nn.softmax(scores, axis=-1)
        out = jnp.einsum('bhqk,bhkd->bhqd', attn, vh)
        concat = out.transpose(0, 2, 1, 3).reshape(B, LQ, D_MODEL)
        return concat @ Wo + bo

    def _L0_ffn_ref(hidden_states, gate_w, shared_gate, shared_up, shared_down, r_gate, r_up, r_down):
        import jax, jax.numpy as jnp
        import numpy as np
        B, S, H, F, E = (1, 512, 256, 512, 8)

        def _swiglu(x, wg, wu, wd):
            return jax.nn.silu(x @ wg.T) * (x @ wu.T) @ wd.T
        b, s, h = hidden_states.shape
        x = hidden_states.reshape(-1, h)
        shared_out = _swiglu(x, shared_gate, shared_up, shared_down)
        logits = x @ gate_w.T
        top_id = jnp.argmax(logits, axis=-1)
        score = jax.nn.sigmoid(jnp.max(logits, axis=-1))
        xs = x * score[:, None]

        def body(acc, ws):
            wg, wu, wd, e = ws
            xe = jnp.where((top_id == e)[:, None], xs, 0.0)
            return (acc + _swiglu(xe, wg, wu, wd), None)
        acc0 = jnp.zeros_like(x)
        routed_out, _ = jax.lax.scan(body, acc0, (r_gate, r_up, r_down, jnp.arange(E)))
        return (shared_out + routed_out).reshape(b, s, h)
    x = x + _L0_attn_ref(_layernorm(x, axis=-1), L0_attn_Wq, L0_attn_bq, L0_attn_Wk, L0_attn_bk, L0_attn_Wv, L0_attn_bv, L0_attn_Wo, L0_attn_bo, L0_attn_ln1_s, L0_attn_ln1_b, L0_attn_W1, L0_attn_b1, L0_attn_W2, L0_attn_b2, L0_attn_ln2_s, L0_attn_ln2_b)
    x = x + _L0_xattn_ref(_layernorm(x, axis=-1), ctx_512, ctx_512, L0_xattn_Wq, L0_xattn_bq, L0_xattn_Wk, L0_xattn_bk, L0_xattn_Wv, L0_xattn_bv, L0_xattn_Wo, L0_xattn_bo)
    x = x + _L0_ffn_ref(_layernorm(x, axis=-1), L0_ffn_gate_w, L0_ffn_shared_gate, L0_ffn_shared_up, L0_ffn_shared_down, L0_ffn_r_gate, L0_ffn_r_up, L0_ffn_r_down)
    return x

_drawn_inputs = setup_inputs


def setup_inputs(seed=0):
    import zlib

    import numpy as np

    out = dict(_drawn_inputs(seed))
    spreads = {'L0_attn_bq': (0.0, 2.0),
     'L0_attn_bk': (0.0, 2.0),
     'L0_attn_bv': (0.0, 0.1),
     'L0_attn_bo': (0.0, 0.1),
     'L0_attn_ln1_s': (1.0, 0.2),
     'L0_attn_ln1_b': (0.0, 0.1),
     'L0_attn_b1': (0.0, 0.1),
     'L0_attn_b2': (0.0, 0.1),
     'L0_attn_ln2_s': (1.0, 0.2),
     'L0_attn_ln2_b': (0.0, 0.1),
     'L0_xattn_bq': (0.0, 0.312),
     'L0_xattn_bk': (0.0, 2.0),
     'L0_xattn_bv': (0.0, 0.1),
     'L0_xattn_bo': (0.0, 0.1)}
    factors = {'L0_attn_Wq': 64.0, 'L0_attn_Wk': 4.121}
    for name, (base, spread) in spreads.items():
        noise = np.random.default_rng([zlib.crc32(name.encode()), seed]).standard_normal(out[name].shape)
        drawn = base * np.exp(spread * noise) if base else spread * noise
        out[name] = jnp.asarray(drawn.astype(out[name].dtype))
    for name, factor in factors.items():
        out[name] = (out[name] * factor).astype(out[name].dtype)
    return out
```

```python
from contextlib import ExitStack

import concourse.bass as bass
from concourse import mybir

F32 = mybir.dt.float32
F32R = mybir.dt.float32r
U32 = mybir.dt.uint32
I32 = mybir.dt.int32
ALU = mybir.AluOpType
ACT = mybir.ActivationFunctionType
AX = mybir.AxisListType

P = 128
SEQS, SEQ, D = 16, 128, 256
KD = D // P
LAYERS, HEADS, HK, F = 8, 16, 64, 1024
HC = F // P
TS = 4
TOK = TS * SEQ
TILES = SEQS // TS
LAST = LAYERS * TILES
EPS_ATT = 1e-6
TINY = 1e-30
PIECES = HC + HC // 2
RING = 3
PIECE = 3 * KD * P


def bcast(ap, n):
    return ap.unsqueeze(1).to_broadcast([ap.shape[0], n, ap.shape[1]])


def spread(ap, w):
    return ap.unsqueeze(2).to_broadcast([ap.shape[0], ap.shape[1], w])


def attention_stack(nc, X, ident, x, Wq, bq, Wk, bk, Wv, bv, Wo, bo, s1, c1, W1, b1, W2, b2, s2, c2):
    with ExitStack() as ctx:
        def sb(name, shape, dt=F32):
            return ctx.enter_context(nc.sbuf_tensor(name, shape, dt))

        def sem(name):
            return ctx.enter_context(nc.semaphore(name))

        WHI = sb("WHI", [P, HC, 3, KD, P], F32R)
        WLO = sb("WLO", [P, HC, 3, KD, P], F32R)
        W1HI = sb("W1HI", [P, HC, KD, P], F32R)
        W1LO = sb("W1LO", [P, HC, KD, P], F32R)
        WO = sb("WO", [P, HC, D])
        W2S = sb("W2S", [P, HC, D])
        STAGE = sb("STAGE", [P, RING, PIECE])
        BA = sb("BA", [P, 3, HC])
        BNEG = sb("BNEG", [P, 3, HC])
        BO = sb("BO", [P, KD])
        B1 = sb("B1", [P, HC])
        B2 = sb("B2", [P, KD])
        LN1P = sb("LN1P", [P, 2, D])
        LN2P = sb("LN2P", [P, 2, D])
        XTHI = sb("XTHI", [P, 2, KD, TOK], F32R)
        XTLO = sb("XTLO", [P, 2, KD, TOK], F32R)
        X1HI = sb("X1HI", [P, KD, TOK], F32R)
        X1LO = sb("X1LO", [P, KD, TOK], F32R)
        ATT = sb("ATT", [P, 2, HC, TOK])
        H = sb("H", [P, HC, TOK])
        EK = sb("EK", [P, 2, TOK])
        RK = sb("RK", [P, 2, TOK])
        EQ = sb("EQ", [P, 2, TOK])
        RQ = sb("RQ", [P, TOK])
        T = sb("T", [P, KD, TOK])
        R = sb("R", [P, TS, D])
        SUMK = sb("SUMK", [P, 2, TS])
        KVS = sb("KVS", [P, 2, TS])
        RSK = sb("RSK", [P, 2, TS])
        CC = sb("CC", [P, 2, TS])
        NES = sb("NES", [P, 2, TS])
        NCE = sb("NCE", [P, 2, TS])
        ST = sb("ST", [P, TS, 6])
        MV = sb("MV", [P, 2, TS, 2])
        RSTD = sb("RSTD", [P, 2, TS])
        ST0 = sb("ST0", [P, SEQS, 6])
        MV0 = sb("MV0", [P, SEQS, 2])
        RSTD0 = sb("RSTD0", [P, SEQS])
        HALF = sb("HALF", [P, SEQS])
        EPS0 = sb("EPS0", [P, TS])
        EPS1 = sb("EPS1", [P, TS])
        ONE = sb("ONE", [P, 1])
        CARRY = sb("CARRY", [P, 1])
        PS = ctx.enter_context(nc.psum_tensor("PS", [P, 6, TOK], F32))
        Y = ctx.enter_context(nc.psum_tensor("Y", [P, 2 * TOK], F32))
        Yfm = Y[:, :].rearrange("p (m t) -> p m t", m=KD)
        Ytm = Y[:, :].rearrange("p (b d) -> p b d", b=TS)

        x_in = [sem(f"x_in{t}") for t in range(TILES)]
        staged = [sem(f"staged{s}") for s in range(RING)]
        ba_in = [sem(f"ba_in{h}") for h in range(2)]
        bo_in, b1_in, b2_in, wo_in, w2_in, ln1_in, ln2_in = (
            sem(n) for n in ("bo_in", "b1_in", "b2_in", "wo_in", "w2_in", "ln1_in", "ln2_in"))
        k_mm, v_mm, q_mm, y_mm, yt_mm, x1t_mm, h_mm, z_mm, zt_mm, xt_mm = (
            sem(n) for n in ("k_mm", "v_mm", "q_mm", "y_mm", "yt_mm", "x1t_mm", "h_mm", "z_mm", "zt_mm", "xt_mm"))
        b_neg, nk, ek, rk, nq, eq, rq, y_act, x1_hi, h_act, z_act, xt_hi = (
            sem(n) for n in ("b_neg", "nk", "ek", "rk", "nq", "eq", "rq", "y_act", "x1_hi", "h_act", "z_act", "xt_hi"))
        k_exp, k_sum, kv_sum, stat, q_elu, denom, recip, att, xt_lo, x1_lo = (
            sem(n) for n in ("k_exp", "k_sum", "kv_sum", "stat", "q_elu", "denom", "recip", "att", "xt_lo", "x1_lo"))
        res1, st1, mv1, n1, x1s, x1, res2, st2, mv2, n2, st0, mv0 = (
            sem(n) for n in ("res1", "st1", "mv1", "n1", "x1s", "x1", "res2", "st2", "mv2", "n2", "st0", "mv0"))
        half_set, w_hi, w_lo, v1, r1, v2, r2, xn_s, xn, v0, r0 = (
            sem(n) for n in ("half_set", "w_hi", "w_lo", "v1", "r1", "v2", "r2", "xn_s", "xn", "v0", "r0"))

        def piece_incs(k):
            return 16 * (3 * KD if k < HC else 2)

        per_layer = [sum(piece_incs(k) for k in range(s, PIECES, RING)) for s in range(RING)]

        def staged_value(layer, k):
            return layer * per_layer[k % RING] + sum(piece_incs(j) for j in range(k % RING, k + 1, RING))

        block = ctx.enter_context(nc.Block())

        @block.sync
        def _(sp):
            def load_piece(layer, k, first):
                if not (first and k < RING):
                    sp.wait_ge(w_lo, layer * PIECES + (k - RING + 1))
                s = k % RING
                if k < HC:
                    for m, w in enumerate((Wk, Wv, Wq)):
                        dst = STAGE[:, s, m * KD * P:(m + 1) * KD * P]
                        for kc in range(KD):
                            src = w[layer, 2 * k:2 * k + 2, kc * P:(kc + 1) * P, :].rearrange("h p k -> p h k")
                            sp.dma_start(dst[:, kc * P:(kc + 1) * P].rearrange("p (h k) -> p h k", h=2),
                                         src).then_inc(staged[s], 16)
                else:
                    j = k - HC
                    for i in range(2):
                        m = 2 * j + i
                        sp.dma_start(STAGE[:, s, i * KD * P:(i + 1) * KD * P].rearrange("p (c n) -> p c n", c=KD),
                                     W1[layer, :, m * P:(m + 1) * P].rearrange("(c p) n -> p c n", p=P)
                                     ).then_inc(staged[s], 16)

            def load_ba(layer, half):
                cs = slice(half * HC // 2, (half + 1) * HC // 2)
                for m, b in enumerate((bk, bv, bq)):
                    src = b[layer, half * HEADS // 2:(half + 1) * HEADS // 2, :].rearrange("(c h) k -> (h k) c", h=2)
                    sp.dma_start(BA[:, m, cs], src, allow_slow_non_contiguous=True).then_inc(ba_in[half], 16)

            def load_ln(dst, scale, bias, layer, done):
                sp.dma_start(dst[:, 0, :], scale[bass.ds(layer, 1), :].to_broadcast([P, D])).then_inc(done, 16)
                sp.dma_start(dst[:, 1, :], bias[bass.ds(layer, 1), :].to_broadcast([P, D])).then_inc(done, 16)

            def load_fm(dst, b, layer, done):
                sp.dma_start(dst[:, :], b[layer, :].rearrange("(c p) -> p c", p=P),
                             allow_slow_non_contiguous=True).then_inc(done, 16)

            def load_wide(dst, w, layer, done):
                sp.dma_start(dst[:, :, :], w[layer, :, :].rearrange("(c p) n -> p c n", p=P)).then_inc(done, 16)

            def layer_loads(l):
                n = (l * TILES + TILES - 1) * HC
                for k in range(HC):
                    load_piece(l + 1, k, False)
                    if k % 4 == 3:
                        sp.wait_ge(rq, n + k + 1)
                        sp.wait_ge(kv_sum, n + k + 1)
                        load_ba(l + 1, k // 4)
                g = l * TILES + TILES
                sp.wait_ge(y_mm, g)
                load_wide(WO, Wo, l + 1, wo_in)
                sp.wait_ge(y_act, g)
                load_fm(BO, bo, l + 1, bo_in)
                sp.wait_ge(x1, g)
                load_ln(LN1P, s1, c1, l + 1, ln1_in)
                for k in range(HC, PIECES):
                    load_piece(l + 1, k, False)
                sp.wait_ge(h_act, g * HC)
                load_fm(B1, b1, l + 1, b1_in)
                sp.wait_ge(z_mm, g)
                load_wide(W2S, W2, l + 1, w2_in)
                sp.wait_ge(z_act, g)
                load_fm(B2, b2, l + 1, b2_in)
                sp.wait_ge(xn, g + TILES)
                load_ln(LN2P, s2, c2, l + 1, ln2_in)

            for t in range(TILES):
                sp.dma_start(X[:, t * TS:(t + 1) * TS, :],
                             x[t * TS:(t + 1) * TS, :, :].rearrange("b s d -> s b d")).then_inc(x_in[t], 16)
                if t < RING:
                    load_piece(0, t, True)
            load_ba(0, 0)
            load_ba(0, 1)
            load_wide(WO, Wo, 0, wo_in)
            load_fm(BO, bo, 0, bo_in)
            load_ln(LN1P, s1, c1, 0, ln1_in)
            load_fm(B1, b1, 0, b1_in)
            load_wide(W2S, W2, 0, w2_in)
            load_fm(B2, b2, 0, b2_in)
            load_ln(LN2P, s2, c2, 0, ln2_in)
            for k in range(RING, PIECES):
                load_piece(0, k, True)
            with sp.Fori(0, LAYERS - 1, 1) as l:
                layer_loads(l)

        @block.gpsimd
        def _(pool):
            def split_piece(layer, k, first):
                s = k % RING
                pool.wait_ge(staged[s], staged_value(layer, k))
                if k < HC:
                    hi, lo = (w[:, k, :, :, :].rearrange("p m c n -> p (m c n)") for w in (WHI, WLO))
                    if not first:
                        pool.wait_ge(q_mm, layer * TILES * HC + (k + 1 - HC))
                    src = STAGE[:, s, :]
                else:
                    m = 2 * (k - HC)
                    hi, lo = (w[:, m:m + 2, :, :].rearrange("p m c n -> p (m c n)") for w in (W1HI, W1LO))
                    if not first:
                        pool.wait_ge(h_mm, layer * TILES * HC + (m + 2 - HC))
                    src = STAGE[:, s, 0:2 * KD * P]
                nc.gpsimd.tensor_tensor(hi, src, ONE[:, :].to_broadcast(src.shape), ALU.mult).then_inc(w_hi, 1)
                pool.wait_ge(w_hi, layer * PIECES + (k + 1))
                nc.gpsimd.tensor_tensor(lo, src, hi.bitcast(F32), ALU.subtract).then_inc(w_lo, 1)

            def rstd(out, var, eps, var_sem, var_value, v_sem, r_sem, value):
                pool.wait_ge(var_sem, var_value)
                nc.gpsimd.tensor_tensor(out, var, eps[:, 0:out.shape[1]], ALU.add).then_inc(v_sem, 1)
                pool.wait_ge(v_sem, value)
                nc.gpsimd.tensor_tensor(out, out, HALF[:, 0:out.shape[1]], ALU.pow).then_inc(r_sem, 1)

            nc.gpsimd.memset(ONE[:, :], 1.0)
            nc.gpsimd.memset(EPS0[:, :], 1e-5)
            nc.gpsimd.memset(EPS1[:, :], 1e-6)
            nc.gpsimd.memset(HALF[:, :], -0.5).then_inc(half_set, 1)
            pool.wait_ge(half_set, 1)
            for t in range(TILES):
                bs = slice(t * TS, (t + 1) * TS)
                rstd(RSTD0[:, bs], MV0[:, bs, 1], EPS0, mv0, t + 1, v0, r0, t + 1)
                pool.wait_ge(r0, t + 1)
                for b in range(t * TS, (t + 1) * TS):
                    last = nc.gpsimd.tensor_scalar(X[:, b, :], X[:, b, :], MV0[:, b, 0:1], RSTD0[:, b:b + 1],
                                                   ALU.subtract, ALU.mult)
                last.then_inc(xn, 1)
            for k in range(PIECES):
                split_piece(0, k, True)

            def tile_steps(l, t, last):
                g = l * TILES + t
                if t == 2 and not last:
                    for k in range(3):
                        split_piece(l + 1, k, False)
                rstd(RSTD[:, 0, :], MV[:, 0, :, 1], EPS1, mv1, g + 1, v1, r1, g + 1)
                if t == 2 and not last:
                    for k in range(3, HC):
                        split_piece(l + 1, k, False)
                if t == 3 and not last:
                    for k in range(HC, PIECES):
                        split_piece(l + 1, k, False)
                rstd(RSTD[:, 1, :], MV[:, 1, :, 1], EPS1, mv2, g + 1, v2, r2, g + 1)
                pool.wait_ge(n2, g + 1)
                pool.wait_ge(ln2_in, (l + 1) * 32)
                nc.gpsimd.tensor_tensor(R[:, :, :], R[:, :, :], bcast(LN2P[:, 0, :], TS), ALU.mult).then_inc(xn_s, 1)
                pool.wait_ge(xn_s, g + 1)
                nc.gpsimd.tensor_tensor(X[:, t * TS:(t + 1) * TS, :], R[:, :, :], bcast(LN2P[:, 1, :], TS),
                                        ALU.add).then_inc(xn, 1)

            with pool.Fori(0, LAYERS - 1, 1) as l:
                for t in range(TILES):
                    tile_steps(l, t, False)
            for t in range(TILES):
                tile_steps(LAYERS - 1, t, True)

        @block.tensor
        def _(pe):
            def split_product(out, whi, wlo, xhi, xlo):
                for kc in range(KD):
                    nc.tensor.matmul(out, whi[:, kc, :], xhi[:, kc, :], start=(kc == 0), stop=False)
                    nc.tensor.matmul(out, whi[:, kc, :], xlo[:, kc, :], start=False, stop=False)
                    ins = nc.tensor.matmul(out, wlo[:, kc, :], xhi[:, kc, :], start=False, stop=(kc == KD - 1))
                return ins

            def project(l, t, c, free):
                g = l * TILES + t
                if c == 0:
                    pe.wait_ge(xt_hi, g + 1)
                    pe.wait_ge(xt_lo, g + 1)
                if t == 0:
                    pe.wait_ge(w_lo, l * PIECES + (c + 1))
                for m, done in enumerate((k_mm, v_mm, q_mm)):
                    for s, value in free[m:m + 1]:
                        pe.wait_ge(s, value)
                    split_product(PS[:, 3 * (c % 2) + m, :], WHI[:, c, m], WLO[:, c, m],
                                  XTHI[:, t % 2], XTLO[:, t % 2]).then_inc(done, 1)

            def after_chunk(n):
                return [(rk, n - 1), (kv_sum, n - 1), (rq, n - 1)]

            def input_fm(j, t):
                pe.wait_ge(xn, j + 1)
                for kc in range(KD):
                    for b in range(TS):
                        ins = nc.tensor.transpose(Yfm[:, kc, b * P:(b + 1) * P],
                                                  X[:, (t % TILES) * TS + b, kc * P:(kc + 1) * P], ident[:, :])
                ins.then_inc(xt_mm, 1)

            def to_tm(done, value, transposed):
                pe.wait_ge(done, value)
                for b in range(TS):
                    for kc in range(KD):
                        ins = nc.tensor.transpose(Ytm[:, b, kc * P:(kc + 1) * P], T[:, kc, b * P:(b + 1) * P],
                                                  ident[:, :])
                ins.then_inc(transposed, 1)

            def down(w, src, done):
                for m in range(KD):
                    for c in range(HC):
                        ins = nc.tensor.matmul(Yfm[:, m, :], w[:, c, m * P:(m + 1) * P], src[:, c, :],
                                               start=(c == 0), stop=(c == HC - 1))
                ins.then_inc(done, 1)

            def hidden(l, g, ms, half, free):
                for i, m in enumerate(ms):
                    if i < 3:
                        pe.wait_ge(*free[i])
                    else:
                        pe.wait_ge(h_act, g * HC + (ms[0] + 1))
                    split_product(PS[:, 3 * half + i % 3, :], W1HI[:, m], W1LO[:, m], X1HI, X1LO).then_inc(h_mm, 1)

            def tile_steps(l, t, last):
                g = l * TILES + t
                n = (g + 1) * HC
                nl, nt = (l, t + 1) if t < TILES - 1 else (l + 1, 0)
                more = not (last and t == TILES - 1)
                if more:
                    project(nl, nt, 1, after_chunk(n + 1))
                if not (last and t >= TILES - 2):
                    pe.wait_ge(res2, g + 1)
                    input_fm(g + 2, t + 2)
                if more:
                    project(nl, nt, 2, after_chunk(n + 2))
                inputs = LAST if last and t >= TILES - 2 else g + 3
                pe.wait_ge(xt_hi, inputs)
                pe.wait_ge(xt_lo, inputs)
                pe.wait_ge(res2, g + 1)
                pe.wait_ge(att, (g + 1) * HC)
                if t == 0:
                    pe.wait_ge(wo_in, (l + 1) * 16)
                down(WO, ATT[:, t % 2], y_mm)
                if more:
                    project(nl, nt, 3, after_chunk(n + 3))
                to_tm(y_act, g + 1, yt_mm)
                if more:
                    project(nl, nt, 4, after_chunk(n + 4))
                    project(nl, nt, 5, after_chunk(n + 5))
                pe.wait_ge(x1, g + 1)
                for kc in range(KD):
                    for b in range(TS):
                        ins = nc.tensor.transpose(Yfm[:, kc, b * P:(b + 1) * P], R[:, b, kc * P:(kc + 1) * P],
                                                  ident[:, :])
                ins.then_inc(x1t_mm, 1)
                if t == 0:
                    pe.wait_ge(w_lo, (l + 1) * PIECES)
                pe.wait_ge(x1_hi, g + 1)
                pe.wait_ge(x1_lo, g + 1)
                top = n + 5 if more else n
                hidden(l, g, (0, 1, 2, 3), 0, [(s, top) for s in (rk, kv_sum, rq)])
                h = g * HC
                if more:
                    project(nl, nt, 6, [(h_act, h + 4), (h_act, h + 2), (h_act, h + 3)])
                top = n + 6 if more else n
                hidden(l, g, (4, 5, 6, 7), 1, [(s, top) for s in (rk, kv_sum, rq)])
                if more:
                    project(nl, nt, 7, [(h_act, h + 8), (h_act, h + 6), (h_act, h + 7)])
                pe.wait_ge(h_act, h + HC)
                if t == 0:
                    pe.wait_ge(w2_in, (l + 1) * 16)
                down(W2S, H, z_mm)
                if not (last and t >= TILES - 2):
                    nl, nt = (l, t + 2) if t < TILES - 2 else (l + 1, t - 2)
                    project(nl, nt, 0, after_chunk(n + HC))
                to_tm(z_act, g + 1, zt_mm)

            input_fm(0, 0)
            pe.wait_ge(xt_hi, 1)
            pe.wait_ge(xt_lo, 1)
            input_fm(1, 1)
            for c in range(HC):
                project(0, 0, c, after_chunk(c) if c >= 2 else [])
            pe.wait_ge(xt_hi, 2)
            project(0, 1, 0, after_chunk(HC))
            with pe.Fori(0, LAYERS - 1, 1) as l:
                for t in range(TILES):
                    tile_steps(l, t, False)
            for t in range(TILES):
                tile_steps(LAYERS - 1, t, True)

        @block.scalar
        def _(act):
            def chunk(l, t, c):
                n = (l * TILES + t) * HC + c
                p, half = c % 2, 3 * (c % 2)
                if t == 0 and c % 4 == 0:
                    cs = slice(c, c + 4)
                    act.wait_ge(ba_in[c // 4], (l + 1) * 48)
                    nc.scalar.mul(BNEG[:, :, cs], BA[:, :, cs], -1.0).then_inc(b_neg, 1)
                    act.wait_ge(b_neg, 2 * l + (c // 4 + 1))
                act.wait_ge(k_mm, n + 1)
                if not (type(n) is int and n < 2):
                    act.wait_ge(kv_sum, n - 1)
                nc.scalar.activation(EK[:, p, :], PS[:, half, :], ACT.Relu, scale=-1.0,
                                     bias=BNEG[:, 0, c:c + 1]).then_inc(nk, 1)
                nc.scalar.activation(RK[:, p, :], PS[:, half, :], ACT.Relu, bias=BA[:, 0, c:c + 1]).then_inc(rk, 1)
                act.wait_ge(nk, n + 1)
                nc.scalar.activation(EK[:, p, :], EK[:, p, :], ACT.Exp, scale=-1.0).then_inc(ek, 1)
                act.wait_ge(q_mm, n + 1)
                if not (type(n) is int and n < 2):
                    act.wait_ge(att, n - 1)
                nc.scalar.activation(EQ[:, p, :], PS[:, half + 2, :], ACT.Relu, scale=-1.0,
                                     bias=BNEG[:, 2, c:c + 1]).then_inc(nq, 1)
                if not (type(n) is int and n < 1):
                    act.wait_ge(q_elu, n)
                nc.scalar.activation(RQ[:, :], PS[:, half + 2, :], ACT.Relu, bias=BA[:, 2, c:c + 1]).then_inc(rq, 1)
                act.wait_ge(nq, n + 1)
                nc.scalar.activation(EQ[:, p, :], EQ[:, p, :], ACT.Exp, scale=-1.0).then_inc(eq, 1)

            def input_hi(j, t):
                act.wait_ge(xt_mm, j + 1)
                nc.scalar.copy(XTHI[:, t % 2, :, :], Yfm[:, :, :]).then_inc(xt_hi, 1)

            def gelu_down(mm, bias, bias_in, done, l, t, g):
                if t == 0:
                    act.wait_ge(bias_in, (l + 1) * 16)
                act.wait_ge(mm, g + 1)
                for m in range(KD):
                    ins = nc.scalar.activation(T[:, m, :], Yfm[:, m, :], ACT.Gelu_apprx_tanh, bias=bias[:, m:m + 1])
                ins.then_inc(done, 1)

            def hidden(l, t, g, ms, half):
                if t == 0 and ms[0] == 0:
                    act.wait_ge(b1_in, (l + 1) * 16)
                for i, m in enumerate(ms):
                    act.wait_ge(h_mm, g * HC + (m + 1))
                    nc.scalar.activation(H[:, m, :], PS[:, 3 * half + i % 3, :], ACT.Gelu_apprx_tanh,
                                         bias=B1[:, m:m + 1]).then_inc(h_act, 1)

            def tile_steps(l, t, last):
                g = l * TILES + t
                nl, nt = (l, t + 1) if t < TILES - 1 else (l + 1, 0)
                more = not (last and t == TILES - 1)
                if more:
                    chunk(nl, nt, 1)
                if not (last and t >= TILES - 2):
                    input_hi(g + 2, t + 2)
                if more:
                    chunk(nl, nt, 2)
                gelu_down(y_mm, BO, bo_in, y_act, l, t, g)
                if more:
                    for c in (3, 4, 5):
                        chunk(nl, nt, c)
                act.wait_ge(x1t_mm, g + 1)
                nc.scalar.copy(X1HI[:, :, :], Yfm[:, :, :]).then_inc(x1_hi, 1)
                hidden(l, t, g, (0, 1, 2, 3), 0)
                if more:
                    chunk(nl, nt, 6)
                hidden(l, t, g, (4, 5, 6, 7), 1)
                if more:
                    chunk(nl, nt, 7)
                gelu_down(z_mm, B2, b2_in, z_act, l, t, g)
                if not (last and t >= TILES - 2):
                    nl, nt = (l, t + 2) if t < TILES - 2 else (l + 1, t - 2)
                    chunk(nl, nt, 0)

            input_hi(0, 0)
            input_hi(1, 1)
            for c in range(HC):
                chunk(0, 0, c)
            chunk(0, 1, 0)
            with act.Fori(0, LAYERS - 1, 1) as l:
                for t in range(TILES):
                    tile_steps(l, t, False)
            for t in range(TILES):
                tile_steps(LAYERS - 1, t, True)

        @block.vector
        def _(dve):
            def seq(b):
                return slice(b * SEQ, (b + 1) * SEQ)

            def features(l, t, c, parts=(0, 1)):
                n = (l * TILES + t) * HC + c
                prev = not (type(n) is int and n == 0)
                cur = not (type(n) is int and n == LAST * HC)
                p, o, half = c % 2, 1 - c % 2, 3 * (c % 2)
                pt, pc = (t, c - 1) if c else (t - 1, HC - 1)
                if 0 in parts:
                    if cur:
                        dve.wait_ge(ek, n + 1)
                        nc.vector.tensor_scalar(EK[:, p, :], EK[:, p, :], -1.0, 1.0, ALU.add, ALU.add).then_inc(k_exp, 1)
                    if prev:
                        dve.wait_ge(q_elu, n)
                        dve.wait_ge(stat, n * 5)
                        for b in range(TS):
                            ins = nc.vector.tensor_scalar(EQ[:, o, seq(b)], EQ[:, o, seq(b)], 1.0, NES[:, o, b:b + 1],
                                                          ALU.add, ALU.subtract)
                        ins.then_inc(denom, 1)
                    if cur:
                        dve.wait_ge(rk, n + 1)
                        dve.wait_ge(k_exp, n + 1)
                        for b in range(TS):
                            ins = nc.vector.scalar_tensor_tensor(RK[:, p, seq(b)], RK[:, p, seq(b)], 0.0, EK[:, p, seq(b)],
                                                                 ALU.add, ALU.add, accum_out=SUMK[:, p, b:b + 1])
                        ins.then_inc(k_sum, 1)
                    if prev:
                        dve.wait_ge(denom, n)
                        nc.vector.reciprocal(EQ[:, o, :], EQ[:, o, :]).then_inc(recip, 1)
                if 1 in parts:
                    if cur:
                        dve.wait_ge(k_sum, n + 1)
                        nc.vector.tensor_scalar(SUMK[:, p, :], SUMK[:, p, :], TINY, None, ALU.max).then_inc(stat, 1)
                        dve.wait_ge(v_mm, n + 1)
                        if t == 0 and c % 4 == 0:
                            dve.wait_ge(ba_in[c // 4], (l + 1) * 48)
                        for b in range(TS):
                            ins = nc.vector.scalar_tensor_tensor(EK[:, p, seq(b)], PS[:, half + 1, seq(b)], BA[:, 1, c:c + 1],
                                                                 RK[:, p, seq(b)], ALU.add, ALU.mult,
                                                                 accum_out=KVS[:, p, b:b + 1])
                        ins.then_inc(kv_sum, 1)
                        dve.wait_ge(stat, n * 5 + 1)
                        nc.vector.reciprocal(RSK[:, p, :], SUMK[:, p, :]).then_inc(stat, 1)
                    if prev:
                        dve.wait_ge(recip, n)
                        for b in range(TS):
                            ins = nc.vector.tensor_scalar(ATT[:, pt % 2, pc, seq(b)], EQ[:, o, seq(b)], NCE[:, o, b:b + 1],
                                                          CC[:, o, b:b + 1], ALU.mult, ALU.add)
                        ins.then_inc(att, 1)
                    if cur:
                        dve.wait_ge(stat, n * 5 + 2)
                        dve.wait_ge(kv_sum, n + 1)
                        nc.vector.tensor_tensor(CC[:, p, :], KVS[:, p, :], RSK[:, p, :], ALU.mult).then_inc(stat, 1)
                        nc.vector.tensor_scalar(NES[:, p, :], RSK[:, p, :], -EPS_ATT, None, ALU.mult).then_inc(stat, 1)
                        dve.wait_ge(eq, n + 1)
                        dve.wait_ge(rq, n + 1)
                        nc.vector.scalar_tensor_tensor(EQ[:, p, :], EQ[:, p, :], -1.0, RQ[:, :], ALU.add,
                                                       ALU.add).then_inc(q_elu, 1)
                        dve.wait_ge(stat, n * 5 + 4)
                        nc.vector.tensor_tensor(NCE[:, p, :], CC[:, p, :], NES[:, p, :], ALU.mult).then_inc(stat, 1)

            def input_lo(j, t):
                dve.wait_ge(xt_hi, j + 1)
                nc.vector.tensor_tensor(XTLO[:, t % 2, :, :], Yfm[:, :, :], XTHI[:, t % 2, :, :].bitcast(F32),
                                        ALU.subtract).then_inc(xt_lo, 1)

            def normed(i, g, stats, means, rstds, done, mm, add, res, value):
                dve.wait_ge(mm, g + 1)
                nc.vector.tensor_tensor(R[:, :, :], Ytm[:, :, :], add, ALU.add).then_inc(res, 1)
                dve.wait_ge(res, value)
                for b in range(TS):
                    ins = nc.vector.bn_stats(ST[:, b, :], R[:, b, :])
                ins.then_inc(stats, 1)
                dve.wait_ge(stats, g + 1)
                nc.vector.memset(CARRY[:, :], 0.0)
                for b in range(TS):
                    ins = nc.vector.bn_aggr(MV[:, i, b, :], ST[:, b, :])
                ins.then_inc(means, 1)
                dve.wait_ge(rstds, g + 1)
                dve.wait_ge(means, g + 1)
                for b in range(TS):
                    ins = nc.vector.tensor_scalar(R[:, b, :], R[:, b, :], MV[:, i, b, 0:1], RSTD[:, i, b:b + 1],
                                                  ALU.subtract, ALU.mult)
                ins.then_inc(done, 1)

            def tile_steps(l, t, last):
                g = l * TILES + t
                nl, nt = (l, t + 1) if t < TILES - 1 else (l + 1, 0)
                more = not (last and t == TILES - 1)
                if more:
                    features(nl, nt, 1)
                if not (last and t >= TILES - 2):
                    input_lo(g + 2, t + 2)
                if more:
                    features(nl, nt, 2)
                    features(nl, nt, 3)
                dve.wait_ge(xn, g + TILES)
                normed(0, g, st1, mv1, r1, n1, yt_mm, X[:, t * TS:(t + 1) * TS, :], res1, g + 1)
                dve.wait_ge(n1, g + 1)
                if t == 0:
                    dve.wait_ge(ln1_in, (l + 1) * 32)
                nc.vector.tensor_tensor(R[:, :, :], R[:, :, :], bcast(LN1P[:, 0, :], TS), ALU.mult).then_inc(x1s, 1)
                dve.wait_ge(x1s, g + 1)
                nc.vector.tensor_tensor(R[:, :, :], R[:, :, :], bcast(LN1P[:, 1, :], TS), ALU.add).then_inc(x1, 1)
                if more:
                    features(nl, nt, 4)
                dve.wait_ge(x1_hi, g + 1)
                nc.vector.tensor_tensor(X1LO[:, :, :], Yfm[:, :, :], X1HI[:, :, :].bitcast(F32),
                                        ALU.subtract).then_inc(x1_lo, 1)
                if more:
                    for c in (5, 6, 7):
                        features(nl, nt, c)
                if not (last and t >= TILES - 2):
                    n2l, n2t = (l, t + 2) if t < TILES - 2 else (l + 1, t - 2)
                    features(n2l, n2t, 0)
                elif more:
                    features(LAYERS, 0, 0)
                dve.wait_ge(x1, g + 1)
                normed(1, g, st2, mv2, r2, n2, zt_mm, R[:, :, :], res2, g + 2)

            for t in range(TILES):
                dve.wait_ge(x_in[t], 16)
                for b in range(t * TS, (t + 1) * TS):
                    ins = nc.vector.bn_stats(ST0[:, b, :], X[:, b, :])
                ins.then_inc(st0, 1)
                dve.wait_ge(st0, t + 1)
                for b in range(t * TS, (t + 1) * TS):
                    ins = nc.vector.bn_aggr(MV0[:, b, :], ST0[:, b, :])
                ins.then_inc(mv0, 1)
            input_lo(0, 0)
            input_lo(1, 1)
            for c in range(HC):
                features(0, 0, c)
            features(0, 1, 0)
            nc.vector.tensor_copy(ST0[:, 0, 0:1], MV0[:, 0, 0:1]).then_inc(res2, 1)
            with dve.Fori(0, LAYERS - 1, 1) as l:
                for t in range(TILES):
                    tile_steps(l, t, False)
            for t in range(TILES):
                tile_steps(LAYERS - 1, t, True)


XH, XK = 16, 16
CH = P // XK
CTX = 128


def cross_attention(nc, X, ident, x, ctx_in, Wq, bq, Wk, bk, Wv, bv, Wo, bo):
    with ExitStack() as ctx:
        def sb(name, shape, dt=F32):
            return ctx.enter_context(nc.sbuf_tensor(name, shape, dt))

        def sem(name):
            return ctx.enter_context(nc.semaphore(name))

        XIN = sb("XIN", [P, SEQS, D])
        CTXS = sb("CTXS", [P, SEQS, CTX])
        WQ = sb("XWQ", [P, KD, D])
        WK = sb("XWK", [P, D])
        WV = sb("XWV", [P, D])
        WOX = sb("XWO", [P, KD, D])
        BQ = sb("XBQ", [P, KD])
        BK = sb("XBK", [P, KD])
        BV = sb("XBV", [P, D])
        BOX = sb("XBO", [P, D])
        ONES = sb("XONES", [P, 1024])
        MASK = sb("XMASK", [P, CH, SEQ])
        HALF = sb("XHALF", [P, SEQS])
        ST = sb("XST", [P, SEQS, 6])
        MV = sb("XMV", [P, SEQS, 2])
        RSTD = sb("XRSTD", [P, SEQS])
        Z = sb("XZ", [P, 2, D])
        CSEQ = sb("XCSEQ", [P, 2, CTX])
        ZT = sb("XZT", [P, 2, KD, P])
        CT = sb("XCT", [P, 2, P])
        QT = sb("XQT", [P, 2, KD, P])
        KT = sb("XKT", [P, 2, KD, P])
        KX = sb("XKX", [P, 2, CH, SEQ])
        V1 = sb("XV1", [P, 2, XH, XK + 1])
        MX = sb("XMX", [P, 2, CH])
        E = sb("XE", [P, 2, CH, SEQ])
        ET = sb("XET", [P, 2, CH, SEQ])
        RD = sb("XRD", [P, 2, CH])
        O = sb("XO", [P, 2, D])
        OT = sb("XOT", [P, 2, KD, P])
        S = ctx.enter_context(nc.psum_tensor("XS", [P, 2, CH * SEQ], F32))
        PT = ctx.enter_context(nc.psum_tensor("XPT", [P, CH * SEQ], F32))
        A = ctx.enter_context(nc.psum_tensor("XA", [P, 512], F32))
        B = ctx.enter_context(nc.psum_tensor("XB", [P, 512], F32))

        x_in, c_in, w_in, bias_in = (sem(n) for n in ("xx_in", "xc_in", "xw_in", "xbias_in"))
        set0, ones_set, v0, r0, mask_set, kx = (sem(n) for n in ("xset0", "xones_set", "xv0", "xr0", "xmask_set", "xkx"))
        prep, z, mx, sh, rd, o, v1, ob, upd = (
            sem(n) for n in ("xprep", "xz", "xmx", "xsh", "xrd", "xo", "xv1", "xob", "xupd"))
        zct_mm, qk_mm, v_mm, s_mm, pt_mm, pv_mm, ot_mm, p_mm = (
            sem(n) for n in ("xzct_mm", "xqk_mm", "xv_mm", "xs_mm", "xpt_mm", "xpv_mm", "xot_mm", "xp_mm"))
        zct, qt, kt, e, et, ot = (sem(n) for n in ("xzct", "xqt", "xkt", "xe", "xet", "xot"))
        block = ctx.enter_context(nc.Block())

        @block.sync
        def _(sp):
            sp.dma_start(XIN[:, :, :], x.rearrange("b s d -> s b d")).then_inc(x_in, 16)
            sp.dma_start(CTXS[:, :, :], ctx_in.rearrange("b s d -> s b d")).then_inc(c_in, 16)
            sp.dma_start(WQ[:, :, :], Wq.rearrange("(c p) n -> p c n", p=P)).then_inc(w_in, 16)
            sp.dma_start(WK[:, :], Wk).then_inc(w_in, 16)
            sp.dma_start(WV[:, :], Wv).then_inc(w_in, 16)
            sp.dma_start(WOX[:, :, :], Wo.rearrange("(c p) n -> p c n", p=P)).then_inc(w_in, 16)
            sp.dma_start(BQ[:, :], bq.rearrange("(c p) -> p c", p=P), allow_slow_non_contiguous=True).then_inc(bias_in, 16)
            sp.dma_start(BK[:, :], bk.rearrange("(c p) -> p c", p=P), allow_slow_non_contiguous=True).then_inc(bias_in, 16)
            sp.dma_start(BV[:, :], bv.unsqueeze(0).to_broadcast([P, D])).then_inc(bias_in, 16)
            sp.dma_start(BOX[:, :], bo.unsqueeze(0).to_broadcast([P, D])).then_inc(bias_in, 16)

        @block.gpsimd
        def _(pool):
            nc.gpsimd.memset(HALF[:, :], -0.5).then_inc(set0, 1)
            nc.gpsimd.memset(MASK[:, :, :], 1.0).then_inc(set0, 1)
            nc.gpsimd.memset(V1[:, :, :, XK:XK + 1], 1.0).then_inc(ones_set, 1)
            pool.wait_ge(set0, 2)
            nc.gpsimd.affine_select(out=MASK[:, :, :], in_=MASK[:, :, :], compare_op=ALU.is_ge, fill=0.0, base=0,
                                    pattern=[[-XK, CH], [0, SEQ]], channel_multiplier=1).then_inc(mask_set, 1)
            pool.wait_ge(mask_set, 1)
            nc.gpsimd.affine_select(out=MASK[:, :, :], in_=MASK[:, :, :], compare_op=ALU.is_ge, fill=0.0, base=XK - 1,
                                    pattern=[[XK, CH], [0, SEQ]], channel_multiplier=-1).then_inc(mask_set, 1)
            pool.wait_ge(prep, 3)
            nc.gpsimd.tensor_scalar(RSTD[:, :], MV[:, :, 1], 1e-5, None, ALU.add).then_inc(v0, 1)
            pool.wait_ge(v0, 1)
            nc.gpsimd.tensor_tensor(RSTD[:, :], RSTD[:, :], HALF[:, :], ALU.pow).then_inc(r0, 1)
            pool.wait_ge(mask_set, 2)

            def unit(i, j, c):
                u = (2 * i + j) * KD + c
                pool.wait_ge(kt, 2 * i + (j + 1))
                if not (type(i) is int and u < 2):
                    pool.wait_ge(s_mm, u - 1)
                nc.gpsimd.tensor_tensor(KX[:, c, :, :], bcast(KT[:, j, c, :], CH), MASK[:, :, :], ALU.mult).then_inc(kx, 1)

            for j in range(2):
                for c in range(KD):
                    unit(0, j, c)
            with pool.Fori(1, SEQS // 2, 1) as i:
                for j in range(2):
                    for c in range(KD):
                        unit(i, j, c)

        @block.tensor
        def _(pe):
            def prepare(i, j):
                b = 2 * i + j
                pe.wait_ge(z, b + 1)
                if not (type(i) is int and b == 0):
                    pe.wait_ge(v1, b)
                for kc in range(KD):
                    nc.tensor.transpose(A[:, kc * P:(kc + 1) * P], Z[:, j, kc * P:(kc + 1) * P], ident[:, :])
                nc.tensor.transpose(A[:, 2 * P:3 * P], CSEQ[:, j, :], ident[:, :]).then_inc(zct_mm, 1)
                pe.wait_ge(zct, b + 1)
                for c in range(KD):
                    for kc in range(KD):
                        nc.tensor.matmul(A[:, c * P:(c + 1) * P], WQ[:, kc, c * P:(c + 1) * P], ZT[:, j, kc, :],
                                         start=(kc == 0), stop=(kc == KD - 1))
                for c in range(KD):
                    ins = nc.tensor.matmul(A[:, (2 + c) * P:(3 + c) * P], WK[:, c * P:(c + 1) * P], CT[:, j, :],
                                           start=True, stop=True)
                ins.then_inc(qk_mm, 1)
                pe.wait_ge(qt, b + 1)
                pe.wait_ge(kt, b + 1)
                nc.tensor.matmul(A[:, 0:D], CT[:, j, :], WV[:, :], start=True, stop=True).then_inc(v_mm, 1)

            def scores(i, j, c):
                u = (2 * i + j) * KD + c
                pe.wait_ge(kx, u + 1)
                if not (type(i) is int and u < 2):
                    pe.wait_ge(sh, u - 1)
                for hf in range(2):
                    ins = nc.tensor.matmul(S[:, c, hf * 512:(hf + 1) * 512], QT[:, j, c, :],
                                           KX[:, c, hf * 4:(hf + 1) * 4, :].rearrange("p h s -> p (h s)"),
                                           start=True, stop=True)
                ins.then_inc(s_mm, 1)

            def weigh(i, j, c):
                u = (2 * i + j) * KD + c
                pe.wait_ge(e, u + 1)
                if not (type(i) is int and u < 1):
                    pe.wait_ge(et, u)
                for h in range(CH):
                    ins = nc.tensor.transpose(PT[:, h * SEQ:(h + 1) * SEQ], E[:, c, h, :], ident[:, :])
                ins.then_inc(pt_mm, 1)
                pe.wait_ge(et, u + 1)
                pe.wait_ge(v1, 2 * i + (j + 1))
                if not (type(i) is int and u < 1):
                    pe.wait_ge(o, u)
                for h in range(CH):
                    ins = nc.tensor.matmul(B[:, h * (XK + 1):(h + 1) * (XK + 1)], ET[:, c, h, :], V1[:, j, c * CH + h, :],
                                           start=True, stop=True)
                ins.then_inc(pv_mm, 1)

            def project(i, j):
                b = 2 * i + j
                pe.wait_ge(o, (b + 1) * KD)
                for kc in range(KD):
                    ins = nc.tensor.transpose(B[:, 256 + kc * P:256 + (kc + 1) * P], O[:, j, kc * P:(kc + 1) * P],
                                              ident[:, :])
                ins.then_inc(ot_mm, 1)
                pe.wait_ge(ot, b + 1)
                for kc in range(KD):
                    ins = nc.tensor.matmul(B[:, 256:512], OT[:, j, kc, :], WOX[:, kc, :], start=(kc == 0),
                                           stop=(kc == KD - 1))
                ins.then_inc(p_mm, 1)
                pe.wait_ge(upd, b + 1)

            def seq_steps(i, j):
                prepare(i, j)
                for c in range(KD):
                    scores(i, j, c)
                for c in range(KD):
                    weigh(i, j, c)
                project(i, j)

            pe.wait_ge(w_in, 64)
            pe.wait_ge(ones_set, 1)
            for j in range(2):
                seq_steps(0, j)
            with pe.Fori(1, SEQS // 2, 1) as i:
                for j in range(2):
                    seq_steps(i, j)

        @block.scalar
        def _(act):
            def seq_steps(i, j):
                b = 2 * i + j
                act.wait_ge(zct_mm, b + 1)
                nc.scalar.copy(ZT[:, j, :, :], A[:, 0:2 * P].rearrange("p (c t) -> p c t", c=KD))
                nc.scalar.copy(CT[:, j, :], A[:, 2 * P:3 * P]).then_inc(zct, 1)
                act.wait_ge(qk_mm, b + 1)
                for c in range(KD):
                    ins = nc.scalar.activation(QT[:, j, c, :], A[:, c * P:(c + 1) * P], ACT.Identity, bias=BQ[:, c:c + 1])
                ins.then_inc(qt, 1)
                for c in range(KD):
                    ins = nc.scalar.activation(KT[:, j, c, :], A[:, (2 + c) * P:(3 + c) * P], ACT.Identity,
                                               bias=BK[:, c:c + 1])
                ins.then_inc(kt, 1)
                for c in range(KD):
                    u = b * KD + c
                    act.wait_ge(sh, u + 1)
                    nc.scalar.activation(E[:, c, :, :], E[:, c, :, :], ACT.Exp, scale=XK ** -0.5).then_inc(e, 1)
                for c in range(KD):
                    u = b * KD + c
                    act.wait_ge(pt_mm, u + 1)
                    nc.scalar.copy(ET[:, c, :, :], PT[:, :].rearrange("p (h s) -> p h s", h=CH)).then_inc(et, 1)
                act.wait_ge(ot_mm, b + 1)
                nc.scalar.copy(OT[:, j, :, :], B[:, 256:512].rearrange("p (c t) -> p c t", c=KD)).then_inc(ot, 1)

            act.wait_ge(bias_in, 64)
            with act.Fori(0, SEQS // 2, 1) as i:
                for j in range(2):
                    seq_steps(i, j)

        @block.vector
        def _(dve):
            dve.wait_ge(x_in, 16)
            nc.vector.tensor_tensor(X[:, :, :], X[:, :, :], XIN[:, :, :], ALU.add).then_inc(prep, 1)
            dve.wait_ge(prep, 1)
            for b in range(SEQS):
                ins = nc.vector.bn_stats(ST[:, b, :], X[:, b, :])
            ins.then_inc(prep, 1)
            dve.wait_ge(prep, 2)
            for b in range(SEQS):
                ins = nc.vector.bn_aggr(MV[:, b, :], ST[:, b, :])
            ins.then_inc(prep, 1)
            dve.wait_ge(r0, 1)
            dve.wait_ge(prep, 3)
            dve.wait_ge(bias_in, 64)
            dve.wait_ge(c_in, 16)

            def seq_steps(i, j):
                b = 2 * i + j
                nc.vector.tensor_copy(CSEQ[:, j, :], CTXS[:, b, :])
                nc.vector.tensor_scalar(Z[:, j, :], X[:, b, :], MV[:, b, 0:1], RSTD[:, bass.ds(b, 1)], ALU.subtract,
                                        ALU.mult).then_inc(z, 1)
                dve.wait_ge(v_mm, b + 1)
                nc.vector.tensor_tensor(V1[:, j, :, 0:XK], A[:, 0:D].rearrange("p (h k) -> p h k", h=XH),
                                        BV[:, :].rearrange("p (h k) -> p h k", h=XH), ALU.add).then_inc(v1, 1)
                for c in range(KD):
                    u = b * KD + c
                    dve.wait_ge(s_mm, u + 1)
                    scores = S[:, c, :].rearrange("p (h s) -> p h s", h=CH)
                    nc.vector.tensor_reduce(MX[:, c, :], scores, AX.X, ALU.max).then_inc(mx, 1)
                    dve.wait_ge(mx, u + 1)
                    nc.vector.tensor_tensor(E[:, c, :, :], scores, spread(MX[:, c, :], SEQ), ALU.subtract).then_inc(sh, 1)
                for c in range(KD):
                    u = b * KD + c
                    dve.wait_ge(pv_mm, u + 1)
                    out = B[:, 0:CH * (XK + 1)].rearrange("p (h k) -> p h k", h=CH)
                    nc.vector.reciprocal(RD[:, c, :], out[:, :, XK]).then_inc(rd, 1)
                    dve.wait_ge(rd, u + 1)
                    nc.vector.tensor_tensor(O[:, j, c * P:(c + 1) * P].rearrange("p (h k) -> p h k", h=CH),
                                            out[:, :, 0:XK], spread(RD[:, c, :], XK), ALU.mult).then_inc(o, 1)
                nc.vector.tensor_tensor(X[:, b, :], X[:, b, :], BOX[:, :], ALU.add).then_inc(ob, 1)
                dve.wait_ge(p_mm, b + 1)
                dve.wait_ge(ob, b + 1)
                nc.vector.tensor_tensor(X[:, b, :], X[:, b, :], B[:, 256:512], ALU.add).then_inc(upd, 1)

            with dve.Fori(0, SEQS // 2, 1) as i:
                for j in range(2):
                    seq_steps(i, j)


E, FF = 8, 512
FC = FF // P
SHARED = E
EA = E + 1
RT = SEQS + E
UNITS = SEQS + RT
ROWS = UNITS * P


def mixture(nc, X, ident, out, gate_w, shared, routed):
    rows_in = nc.dram_tensor("rows_in", (ROWS, D), F32, kind="Internal").ap()
    rows_out = nc.dram_tensor("rows_out", (ROWS, D), F32, kind="Internal").ap()
    with ExitStack() as ctx:
        def sb(name, shape, dt=F32):
            return ctx.enter_context(nc.sbuf_tensor(name, shape, dt))

        WGU = sb("WGU", [P, EA, 2, KD, FF])
        WD = sb("WD", [P, EA, FC, D])
        EID = sb("EID", [P, UNITS], I32)
        ROW = sb("ROW", [P, SEQS], U32)
        PSX = ctx.enter_context(nc.psum_tensor("PSX", [P, 8, 512], F32))
        route(nc, X, ident, gate_w, shared, routed, rows_in, WGU, WD, EID, ROW, PSX)
        experts(nc, ident, rows_in, rows_out, WGU, WD, EID, PSX)
        combine(nc, X, rows_out, ROW, out)


def route(nc, X, ident, gate_w, shared, routed, rows_in, WGU, WD, EID, ROW, PSX):
    with ExitStack() as ctx:
        def sb(name, shape, dt=F32):
            return ctx.enter_context(nc.sbuf_tensor(name, shape, dt))

        def sem(name):
            return ctx.enter_context(nc.semaphore(name))

        RAW = sb("RAW", [P, 3, 1024])
        ZERO = sb("ZERO", [P, D])
        ZN = sb("ZN", [P, SEQS, D])
        XS = sb("XSC", [P, SEQS, D])
        ZG = sb("ZG", [P, 2, KD, TOK])
        GW = sb("GW", [E, D])
        GT = sb("GT", [P, KD, E])
        ST = sb("RST", [P, SEQS, 6])
        MV = sb("RMV", [P, SEQS, 2])
        RSTD = sb("RRSTD", [P, SEQS])
        HALF = sb("RHALF", [P, SEQS])
        BEFORE = sb("BEFORE", [P, P])
        ONES = sb("RONES", [P, P])
        IOTE = sb("IOTE", [P, SEQS, E])
        IOT128 = sb("IOT128", [P, E, SEQS])
        IOTU = sb("IOTU", [P, RT, E])
        LG = sb("LG", [P, SEQS, E])
        MXL = sb("MXL", [P, SEQS])
        SC = sb("SC", [P, SEQS])
        PICK = sb("PICK", [P, SEQS, E])
        IDX = sb("IDX", [P, SEQS])
        OH = sb("OH", [P, SEQS, E])
        TOTS = sb("TOTS", [P, SEQS, E])
        BASE = sb("BASE", [P, SEQS + 1, E])
        MORE = sb("MORE", [P, E, SEQS])
        NT = sb("NT", [P, E])
        START = sb("START", [P, E + 1])
        PAST = sb("PAST", [P, RT, E])
        EIDF = sb("EIDF", [P, RT])
        RB = sb("RB", [P, E])
        POS = sb("POS", [P, SEQS, E])
        POSF = sb("POSF", [P, SEQS])

        raw_in = [sem(f"raw_in{i}") for i in range(3)]
        gw_in, zeroed, zn_out, scattered = (sem(n) for n in ("gw_in", "zeroed", "zn_out", "scattered"))
        consts, zero_set, before_set, v0, r0 = (sem(n) for n in ("rconsts", "zero_set", "before_set", "rv0", "rr0"))
        gt_mm, zt_mm, lg_mm, pre_mm = (sem(n) for n in ("gt_mm", "rzt_mm", "lg_mm", "pre_mm"))
        w_mm = [sem(f"w_mm{i}") for i in range(3)]
        w_sb = [sem(f"w_sb{i}") for i in range(3)]
        gt, zg, sc = (sem(n) for n in ("gt", "zg", "sc"))
        prep, zn, step, xs, oh, row, mxl = (sem(n) for n in ("rprep", "rzn", "rstep", "rxs", "roh", "rrow", "rmxl"))
        block = ctx.enter_context(nc.Block())

        @block.sync
        def _(sp):
            def load(k, mats):
                for i, w in enumerate(mats):
                    if not (type(k) is int and k == 0):
                        sp.wait_ge(w_mm[i], k)
                    sp.dma_start(RAW[:, i, :].rearrange("p (c n) -> p c n", n=w.shape[1]),
                                 w.rearrange("(c p) n -> p c n", p=P)).then_inc(raw_in[i], 16)

            sp.dma_start(GW[:, :], gate_w).then_inc(gw_in, 16)
            load(0, shared)
            sp.wait_ge(zero_set, 1)
            sp.dma_start(rows_in[SEQS * P:ROWS, :].rearrange("(u p) d -> p u d", p=P),
                         bcast(ZERO[:, :], RT)).then_inc(zeroed, 16)
            sp.wait_ge(zn, TILES)
            sp.dma_start(rows_in[0:SEQS * P, :].rearrange("(b p) d -> p b d", p=P), ZN[:, :, :]).then_inc(zn_out, 16)
            with sp.Fori(0, E, 1) as e:
                load(e + 1, [w[e, :, :] for w in routed])
            sp.wait_ge(zeroed, 16)
            sp.wait_ge(zn_out, 16)

        @block.gpsimd
        def _(pool):
            nc.gpsimd.memset(ZERO[:, :], 0.0).then_inc(zero_set, 1)
            nc.gpsimd.memset(HALF[:, :], -0.5)
            nc.gpsimd.memset(ONES[:, :], 1.0)
            nc.gpsimd.memset(BASE[:, 0, :], 0.0)
            nc.gpsimd.memset(START[:, 0:1], 0.0)
            nc.gpsimd.memset(EID[:, 0:SEQS], SHARED)
            nc.gpsimd.iota(IOTE[:, :, :], pattern=[[0, SEQS], [1, E]], base=0, channel_multiplier=0,
                           allow_small_or_imprecise_dtypes=True)
            nc.gpsimd.iota(IOT128[:, :, :], pattern=[[0, E], [P, SEQS]], base=0, channel_multiplier=0,
                           allow_small_or_imprecise_dtypes=True)
            nc.gpsimd.iota(IOTU[:, :, :], pattern=[[1, RT], [0, E]], base=0, channel_multiplier=0,
                           allow_small_or_imprecise_dtypes=True)
            nc.gpsimd.memset(BEFORE[:, :], 1.0).then_inc(consts, 1)
            pool.wait_ge(consts, 1)
            nc.gpsimd.affine_select(out=BEFORE[:, :], in_=BEFORE[:, :], compare_op=ALU.is_ge, fill=0.0, base=-1,
                                    pattern=[[1, P]], channel_multiplier=-1).then_inc(before_set, 1)
            pool.wait_ge(prep, 2)
            nc.gpsimd.tensor_scalar(RSTD[:, :], MV[:, :, 1], 1e-5, None, ALU.add).then_inc(v0, 1)
            pool.wait_ge(v0, 1)
            nc.gpsimd.tensor_tensor(RSTD[:, :], RSTD[:, :], HALF[:, :], ALU.pow).then_inc(r0, 1)
            pool.wait_ge(xs, 1)
            pool.wait_ge(row, 1)
            pool.wait_ge(zeroed, 16)
            for b in range(SEQS):
                pool.indirect_dma_start(out=rows_in[:, :], out_offset=bass.IndirectOffsetOnAxis(ROW[:, b:b + 1], 0),
                                        in_=XS[:, b, :], in_offset=None).then_inc(scattered, 16)
            pool.wait_ge(scattered, 16 * SEQS)

        def turned(i, out_chunks, in_chunks):
            return [(c, n, (n * in_chunks + c) * P) for n in range(out_chunks) for c in range(in_chunks)]

        @block.tensor
        def _(pe):
            def matrix(k, i):
                oc, icn = (KD, FC) if i < 2 else (FC, KD)
                pe.wait_ge(raw_in[i], 16 * k + 16)
                if not (type(k) is int and k == 0):
                    pe.wait_ge(w_sb[i], k)
                width = oc * P
                dst = PSX[:, 2 * i:2 * i + 2, :].rearrange("p b n -> p (b n)")
                for c, n, at in turned(i, oc, icn):
                    ins = nc.tensor.transpose(dst[:, at:at + P], RAW[:, i, c * width + n * P:c * width + (n + 1) * P],
                                              ident[:, :])
                ins.then_inc(w_mm[i], 1)

            pe.wait_ge(gw_in, 16)
            for kc in range(KD):
                ins = nc.tensor.transpose(PSX[:, 7, kc * E:(kc + 1) * E], GW[:, kc * P:(kc + 1) * P], ident[0:E, 0:E])
            ins.then_inc(gt_mm, 1)
            for q in range(TILES):
                pe.wait_ge(zn, q + 1)
                if q >= 2:
                    pe.wait_ge(zg, q - 1)
                for kc in range(KD):
                    for b in range(TS):
                        ins = nc.tensor.transpose(PSX[:, 2 * (q % 2) + kc, b * P:(b + 1) * P],
                                                  ZN[:, q * TS + b, kc * P:(kc + 1) * P], ident[:, :])
                ins.then_inc(zt_mm, 1)
                if q == 0:
                    pe.wait_ge(gt, 1)
                pe.wait_ge(zg, q + 1)
                for b in range(TS):
                    s = q * TS + b
                    for kc in range(KD):
                        ins = nc.tensor.matmul(PSX[:, 6, s * E:(s + 1) * E], ZG[:, q % 2, kc, b * P:(b + 1) * P],
                                               GT[:, kc, :], start=(kc == 0), stop=(kc == KD - 1))
            ins.then_inc(lg_mm, 1)
            for i in range(3):
                matrix(0, i)
            pe.wait_ge(before_set, 1)
            pe.wait_ge(oh, 1)
            ohs = OH[:, :, :].rearrange("p b e -> p (b e)")
            nc.tensor.matmul(PSX[:, 7, 0:P], BEFORE[:, :], ohs, start=True, stop=True)
            nc.tensor.matmul(PSX[:, 7, P:2 * P], ONES[:, :], ohs, start=True, stop=True).then_inc(pre_mm, 1)
            with pe.Fori(1, EA, 1) as k:
                for i in range(3):
                    matrix(k, i)

        @block.scalar
        def _(act):
            def matrix(k, place, i):
                act.wait_ge(w_mm[i], k + 1)
                src = PSX[:, 2 * i:2 * i + 2, :].rearrange("p b n -> p (b n)")
                dst = WGU[:, place, i, :, :].rearrange("p c n -> p (c n)") if i < 2 else \
                    WD[:, place, :, :].rearrange("p c n -> p (c n)")
                nc.scalar.copy(dst, src).then_inc(w_sb[i], 1)

            act.wait_ge(gt_mm, 1)
            nc.scalar.copy(GT[:, :, :], PSX[:, 7, 0:KD * E].rearrange("p (c e) -> p c e", c=KD)).then_inc(gt, 1)
            for q in range(TILES):
                act.wait_ge(zt_mm, q + 1)
                nc.scalar.copy(ZG[:, q % 2, :, :], PSX[:, 2 * (q % 2):2 * (q % 2) + 2, :]).then_inc(zg, 1)
            act.wait_ge(mxl, 1)
            nc.scalar.activation(SC[:, :], MXL[:, :], ACT.Sigmoid).then_inc(sc, 1)
            for i in range(3):
                matrix(0, SHARED, i)
            with act.Fori(0, E, 1) as e:
                for i in range(3):
                    matrix(e + 1, e, i)

        @block.vector
        def _(dve):
            for b in range(SEQS):
                ins = nc.vector.bn_stats(ST[:, b, :], X[:, b, :])
            ins.then_inc(prep, 1)
            dve.wait_ge(prep, 1)
            for b in range(SEQS):
                ins = nc.vector.bn_aggr(MV[:, b, :], ST[:, b, :])
            ins.then_inc(prep, 1)
            dve.wait_ge(r0, 1)
            dve.wait_ge(prep, 2)
            for q in range(TILES):
                for b in range(q * TS, (q + 1) * TS):
                    ins = nc.vector.tensor_scalar(ZN[:, b, :], X[:, b, :], MV[:, b, 0:1], RSTD[:, b:b + 1], ALU.subtract,
                                                  ALU.mult)
                ins.then_inc(zn, 1)
            steps = [0]

            def then(ins):
                steps[0] += 1
                ins.then_inc(step, 1)
                dve.wait_ge(step, steps[0])

            dve.wait_ge(consts, 1)
            dve.wait_ge(lg_mm, 1)
            then(nc.vector.tensor_copy(LG[:, :, :], PSX[:, 6, 0:P].rearrange("p (b e) -> p b e", e=E)))
            nc.vector.tensor_reduce(MXL[:, :], LG[:, :, :], AX.X, ALU.max).then_inc(mxl, 1)
            dve.wait_ge(mxl, 1)
            then(nc.vector.tensor_tensor(PICK[:, :, :], LG[:, :, :], spread(MXL[:, :], E), ALU.is_lt))
            then(nc.vector.scalar_tensor_tensor(PICK[:, :, :], PICK[:, :, :], float(E), IOTE[:, :, :], ALU.mult, ALU.add))
            then(nc.vector.tensor_reduce(IDX[:, :], PICK[:, :, :], AX.X, ALU.min))
            nc.vector.tensor_tensor(OH[:, :, :], IOTE[:, :, :], spread(IDX[:, :], E), ALU.is_equal).then_inc(oh, 1)
            dve.wait_ge(sc, 1)
            dve.wait_ge(zn, TILES)
            for b in range(SEQS):
                ins = nc.vector.tensor_scalar(XS[:, b, :], ZN[:, b, :], SC[:, b:b + 1], None, ALU.mult)
            ins.then_inc(xs, 1)
            dve.wait_ge(pre_mm, 1)
            then(nc.vector.tensor_copy(TOTS[:, :, :], PSX[:, 7, P:2 * P].rearrange("p (b e) -> p b e", e=E)))
            for b in range(SEQS):
                then(nc.vector.tensor_tensor(BASE[:, b + 1, :], BASE[:, b, :], TOTS[:, b, :], ALU.add))
            then(nc.vector.tensor_tensor(MORE[:, :, :], spread(BASE[:, SEQS, :], SEQS), IOT128[:, :, :], ALU.is_gt))
            then(nc.vector.tensor_reduce(NT[:, :], MORE[:, :, :], AX.X, ALU.add))
            for e in range(E):
                then(nc.vector.tensor_tensor(START[:, e + 1:e + 2], START[:, e:e + 1], NT[:, e:e + 1], ALU.add))
            then(nc.vector.tensor_tensor(PAST[:, :, :], bcast(START[:, 1:E + 1], RT), IOTU[:, :, :], ALU.is_le))
            then(nc.vector.tensor_reduce(EIDF[:, :], PAST[:, :, :], AX.X, ALU.add))
            then(nc.vector.tensor_scalar(EID[:, SEQS:UNITS], EIDF[:, :], float(E - 1), None, ALU.min))
            then(nc.vector.tensor_scalar(RB[:, :], START[:, 0:E], float(P), float(SEQS * P), ALU.mult, ALU.add))
            then(nc.vector.tensor_tensor(POS[:, :, :], BASE[:, 0:SEQS, :], bcast(RB[:, :], SEQS), ALU.add))
            then(nc.vector.tensor_tensor(POS[:, :, :], POS[:, :, :], PSX[:, 7, 0:P].rearrange("p (b e) -> p b e", e=E),
                                         ALU.add))
            dve.wait_ge(oh, 1)
            then(nc.vector.tensor_tensor(POS[:, :, :], POS[:, :, :], OH[:, :, :], ALU.mult))
            then(nc.vector.tensor_reduce(POSF[:, :], POS[:, :, :], AX.X, ALU.add))
            nc.vector.tensor_copy(ROW[:, :], POSF[:, :]).then_inc(row, 1)


def experts(nc, ident, rows_in, rows_out, WGU, WD, EID, PSX):
    with ExitStack() as ctx:
        def sb(name, shape, dt=F32):
            return ctx.enter_context(nc.sbuf_tensor(name, shape, dt))

        def sem(name):
            return ctx.enter_context(nc.semaphore(name))

        XU = sb("XU", [P, 2, D])
        XTU = sb("XTU", [P, 2, KD, P])
        SG = sb("SG", [P, 2, FF])
        AC = sb("AC", [P, 2, FF])
        AT = sb("AT", [P, 2, FC, P])
        OU = sb("OU", [P, 2, D])
        xu_in = [sem(f"xu_in{j}") for j in range(2)]
        stored = [sem(f"stored{j}") for j in range(2)]
        xt_mm, g_mm, u_mm, at_mm, o_mm = (sem(n) for n in ("uxt_mm", "g_mm", "u_mm", "at_mm", "o_mm"))
        xt, sg, ac, at, ou = (sem(n) for n in ("uxt", "sg", "ac", "at", "ou"))
        HALVES = UNITS // 2
        block = ctx.enter_context(nc.Block())

        @block.sync
        def _(sp):
            def load(i, j):
                u = 2 * i + j
                if not (type(i) is int and i == 0):
                    sp.wait_ge(xt_mm, u - 1)
                sp.dma_start(XU[:, j, :], rows_in[bass.ds(u * P, P), :]).then_inc(xu_in[j], 16)

            for j in range(2):
                load(0, j)
            with sp.Fori(1, HALVES, 1) as i:
                for j in range(2):
                    load(i, j)

        @block.gpsimd
        def _(pool):
            with pool.Fori(0, HALVES, 1) as i:
                for j in range(2):
                    u = 2 * i + j
                    pool.wait_ge(ou, u + 1)
                    pool.dma_start(rows_out[bass.ds(u * P, P), :], OU[:, j, :]).then_inc(stored[j], 16)
            for j in range(2):
                pool.wait_ge(stored[j], 16 * HALVES)

        @block.tensor
        def _(pe):
            def turn_input(i, j):
                u = 2 * i + j
                pe.wait_ge(xu_in[j], 16 * i + 16)
                if not (type(i) is int and u == 0):
                    pe.wait_ge(xt, u)
                for kc in range(KD):
                    ins = nc.tensor.transpose(PSX[:, 6, kc * P:(kc + 1) * P], XU[:, j, kc * P:(kc + 1) * P], ident[:, :])
                ins.then_inc(xt_mm, 1)

            def gate_up(i, j):
                u = 2 * i + j
                e = nc.tensor.value_load(EID[0:1, bass.ds(u, 1)], min_val=0, max_val=E)
                pe.wait_ge(xt, u + 1)
                for m, done in enumerate((g_mm, u_mm)):
                    if not (type(i) is int and i == 0):
                        pe.wait_ge((sg, ac)[m], u - 1)
                    for kc in range(KD):
                        ins = nc.tensor.matmul(PSX[:, 2 * m + j, :], XTU[:, j, kc, :], WGU[:, e, m, kc, :],
                                               start=(kc == 0), stop=(kc == KD - 1))
                    ins.then_inc(done, 1)

            def turn_hidden(i, j):
                u = 2 * i + j
                pe.wait_ge(ac, u + 1)
                if not (type(i) is int and u == 0):
                    pe.wait_ge(at, u)
                for c in range(FC):
                    ins = nc.tensor.transpose(PSX[:, 4, c * P:(c + 1) * P], AC[:, j, c * P:(c + 1) * P], ident[:, :])
                ins.then_inc(at_mm, 1)

            def down(i, j):
                u = 2 * i + j
                e = nc.tensor.value_load(EID[0:1, bass.ds(u, 1)], min_val=0, max_val=E)
                pe.wait_ge(at, u + 1)
                if not (type(i) is int and i == 0):
                    pe.wait_ge(ou, u - 1)
                for c in range(FC):
                    ins = nc.tensor.matmul(PSX[:, 5 + 2 * j, 0:D], AT[:, j, c, :], WD[:, e, c, :], start=(c == 0),
                                           stop=(c == FC - 1))
                ins.then_inc(o_mm, 1)

            def pair(i, more):
                turn_hidden(i, 0)
                gate_up(i, 1)
                if more:
                    turn_input(i + 1, 0)
                down(i, 0)
                turn_hidden(i, 1)
                if more:
                    gate_up(i + 1, 0)
                    turn_input(i + 1, 1)
                down(i, 1)

            turn_input(0, 0)
            turn_input(0, 1)
            gate_up(0, 0)
            pair(0, True)
            with pe.Fori(1, HALVES - 1, 1) as i:
                pair(i, True)
            pair(HALVES - 1, False)

        @block.scalar
        def _(act):
            def evac_input(i, j):
                act.wait_ge(xt_mm, 2 * i + (j + 1))
                nc.scalar.copy(XTU[:, j, :, :], PSX[:, 6, 0:D].rearrange("p (c t) -> p c t", c=KD)).then_inc(xt, 1)

            def silu(i, j):
                u = 2 * i + j
                act.wait_ge(g_mm, u + 1)
                nc.scalar.activation(SG[:, j, :], PSX[:, j, :], ACT.Silu).then_inc(sg, 1)

            def evac_hidden(i, j):
                act.wait_ge(at_mm, 2 * i + (j + 1))
                nc.scalar.copy(AT[:, j, :, :], PSX[:, 4, :].rearrange("p (c t) -> p c t", c=FC)).then_inc(at, 1)

            def pair(i, more):
                evac_hidden(i, 0)
                silu(i, 1)
                if more:
                    evac_input(i + 1, 0)
                evac_hidden(i, 1)
                if more:
                    silu(i + 1, 0)
                    evac_input(i + 1, 1)

            evac_input(0, 0)
            evac_input(0, 1)
            silu(0, 0)
            with act.Fori(0, HALVES - 1, 1) as i:
                pair(i, True)
            pair(HALVES - 1, False)

        @block.vector
        def _(dve):
            def product(i, j):
                u = 2 * i + j
                dve.wait_ge(sg, u + 1)
                dve.wait_ge(u_mm, u + 1)
                nc.vector.tensor_tensor(AC[:, j, :], SG[:, j, :], PSX[:, 2 + j, :], ALU.mult).then_inc(ac, 1)

            def result(i, j, first):
                u = 2 * i + j
                dve.wait_ge(o_mm, u + 1)
                if not first:
                    dve.wait_ge(stored[j], 16 * i)
                nc.vector.tensor_copy(OU[:, j, :], PSX[:, 5 + 2 * j, 0:D]).then_inc(ou, 1)

            def pair(i, first, more):
                product(i, 1)
                result(i, 0, first)
                if more:
                    product(i + 1, 0)
                result(i, 1, first)

            product(0, 0)
            pair(0, True, True)
            with dve.Fori(1, HALVES - 1, 1) as i:
                pair(i, False, True)
            pair(HALVES - 1, False, False)


def combine(nc, X, rows_out, ROW, out):
    with ExitStack() as ctx:
        def sem(name):
            return ctx.enter_context(nc.semaphore(name))

        SH = ctx.enter_context(nc.sbuf_tensor("SH", [P, SEQS, D], F32))
        RO = ctx.enter_context(nc.sbuf_tensor("RO", [P, SEQS, D], F32))
        sh_in = sem("sh_in")
        ro_in = [sem(f"ro_in{h}") for h in range(2)]
        added, ready, written = sem("added"), sem("ready"), sem("written")
        block = ctx.enter_context(nc.Block())

        @block.sync
        def _(sp):
            sp.dma_start(SH[:, :, :], rows_out[0:SEQS * P, :].rearrange("(b p) d -> p b d", p=P)).then_inc(sh_in, 16)
            for t in range(TILES):
                sp.wait_ge(ready, t + 1)
                sp.dma_start(out[t * TS:(t + 1) * TS, :, :].rearrange("b s d -> s b d"),
                             X[:, t * TS:(t + 1) * TS, :]).then_inc(written, 16)
            sp.wait_ge(written, 16 * TILES)

        @block.gpsimd
        def _(pool):
            for b in range(SEQS):
                pool.indirect_dma_start(out=RO[:, b, :], out_offset=None, in_=rows_out[:, :],
                                        in_offset=bass.IndirectOffsetOnAxis(ROW[:, b:b + 1], 0)
                                        ).then_inc(ro_in[b // (SEQS // 2)], 16)

        @block.vector
        def _(dve):
            dve.wait_ge(sh_in, 16)
            nc.vector.tensor_tensor(X[:, :, :], X[:, :, :], SH[:, :, :], ALU.add).then_inc(added, 1)
            dve.wait_ge(added, 1)
            for t in range(TILES):
                bs = slice(t * TS, (t + 1) * TS)
                dve.wait_ge(ro_in[t // 2], 16 * SEQS // 2)
                nc.vector.tensor_tensor(X[:, bs, :], X[:, bs, :], RO[:, bs, :], ALU.add).then_inc(ready, 1)


def decoder(nc, a, out):
    with ExitStack() as ctx:
        X = ctx.enter_context(nc.sbuf_tensor("X", [P, SEQS, D], F32))
        ident = ctx.enter_context(nc.sbuf_tensor("ident", [P, P], F32))
        ident_set = ctx.enter_context(nc.semaphore("ident_set"))
        with nc.Block() as block:
            @block.gpsimd
            def _(pool):
                nc.gpsimd.memset(ident[:, :], 0.0).then_inc(ident_set, 1)
                pool.wait_ge(ident_set, 1)
                nc.gpsimd.affine_select(out=ident[:, :], in_=ident[:, :], compare_op=ALU.not_equal, fill=1.0, base=0,
                                        pattern=[[-1, P]], channel_multiplier=1).then_inc(ident_set, 1)
                pool.wait_ge(ident_set, 2)
        attention_stack(nc, X, ident, a["x"], *(a["L0_attn_" + n] for n in (
            "Wq", "bq", "Wk", "bk", "Wv", "bv", "Wo", "bo", "ln1_s", "ln1_b", "W1", "b1", "W2", "b2", "ln2_s", "ln2_b")))
        cross_attention(nc, X, ident, a["x"], a["ctx_512"], *(a["L0_xattn_" + n] for n in (
            "Wq", "bq", "Wk", "bk", "Wv", "bv", "Wo", "bo")))
        mixture(nc, X, ident, out, a["L0_ffn_gate_w"], [a["L0_ffn_shared_" + n] for n in ("gate", "up", "down")],
                [a["L0_ffn_r_" + n] for n in ("gate", "up", "down")])


def kernel(**inputs):
    import numpy as np
    from concourse import bacc
    from concourse.bass_utils import run_bass_kernel_spmd

    nc = bacc.Bacc("TRN2", target_bir_lowering=False, num_devices=1)
    arrays = {name: np.ascontiguousarray(a) for name, a in inputs.items()}
    aps = {name: nc.dram_tensor(name, a.shape, mybir.dt.from_np(a.dtype), kind="ExternalInput").ap()
           for name, a in arrays.items()}
    out = nc.dram_tensor("out", (SEQS, SEQ, D), F32, kind="ExternalOutput").ap()
    decoder(nc, aps, out)
    return run_bass_kernel_spmd(nc, [arrays], core_ids=[0]).results[0]["out"]
```

```python
from contextlib import ExitStack

import concourse.bass as bass
from concourse import mybir

F32 = mybir.dt.float32
F32R = mybir.dt.float32r
U32 = mybir.dt.uint32
I32 = mybir.dt.int32
ALU = mybir.AluOpType
ACT = mybir.ActivationFunctionType
AX = mybir.AxisListType

P = 128
SEQS, SEQ, D = 16, 128, 256
KD = D // P
LAYERS, HEADS, HK, F = 8, 16, 64, 1024
HC = F // P
TS = 4
TOK = TS * SEQ
TILES = SEQS // TS
LAST = LAYERS * TILES
EPS_ATT = 1e-6
TINY = 1e-24
PIECES = HC + HC // 2
RING = 3
IRING = 4
PIECE = 3 * KD * P


def bcast(ap, n):
    return ap.unsqueeze(1).to_broadcast([ap.shape[0], n, ap.shape[1]])


def spread(ap, w):
    return ap.unsqueeze(2).to_broadcast([ap.shape[0], ap.shape[1], w])


def slot_of(l, t):
    return l + t // TILES, t % TILES


def exists(l, t):
    return type(l) is not int or l * TILES + t < LAST


def attention_stack(nc, X, ident, x, Wq, bq, Wk, bk, Wv, bv, Wo, bo, s1, c1, W1, b1, W2, b2, s2, c2):
    with ExitStack() as ctx:
        def sb(name, shape, dt=F32):
            return ctx.enter_context(nc.sbuf_tensor(name, shape, dt))

        def sem(name):
            return ctx.enter_context(nc.semaphore(name))

        WHI = sb("WHI", [P, HC, 3, KD, P], F32R)
        WLO = sb("WLO", [P, HC, 3, KD, P], F32R)
        W1HI = sb("W1HI", [P, HC, KD, P], F32R)
        W1LO = sb("W1LO", [P, HC, KD, P], F32R)
        WO = sb("WO", [P, HC, D])
        W2S = sb("W2S", [P, HC, D])
        STAGE = sb("STAGE", [P, RING, PIECE])
        BA = sb("BA", [P, 3, HC])
        BNEG = sb("BNEG", [P, 3, HC])
        BO = sb("BO", [P, KD])
        B1 = sb("B1", [P, HC])
        B2 = sb("B2", [P, KD])
        LN1P = sb("LN1P", [P, 2, D])
        LN2P = sb("LN2P", [P, 2, D])
        XTHI = sb("XTHI", [P, 2, KD, TOK], F32R)
        XTLO = sb("XTLO", [P, 2, KD, TOK], F32R)
        X1HI = sb("X1HI", [P, KD, TOK], F32R)
        X1LO = sb("X1LO", [P, KD, TOK], F32R)
        ATT = sb("ATT", [P, HC, TOK])
        H = sb("H", [P, HC, TOK])
        EK = sb("EK", [P, 2, TOK])
        RK = sb("RK", [P, 2, TOK])
        EQ = sb("EQ", [P, 2, TOK])
        RQ = sb("RQ", [P, 2, TOK])
        INV = sb("INV", [P, IRING, TOK])
        T = sb("T", [P, KD, TOK])
        R = sb("R", [P, 2, TS, D])
        SUMK = sb("SUMK", [P, 2, TS])
        KVS = sb("KVS", [P, 2, TS])
        RSK = sb("RSK", [P, 2, TS])
        CC = sb("CC", [P, IRING, TS])
        ES = sb("ES", [P, 2, TS])
        CE = sb("CE", [P, IRING, TS])
        ST = sb("ST", [P, TS, 6])
        MV = sb("MV", [P, 2, TS, 2])
        RSTD = sb("RSTD", [P, 2, TS])
        ST0 = sb("ST0", [P, SEQS, 6])
        MV0 = sb("MV0", [P, SEQS, 2])
        RSTD0 = sb("RSTD0", [P, SEQS])
        HALF = sb("HALF", [P, SEQS])
        EPS0 = sb("EPS0", [P, TS])
        EPS1 = sb("EPS1", [P, TS])
        ONE = sb("ONE", [P, 1])
        CARRY = sb("CARRY", [P, 1])
        PS = ctx.enter_context(nc.psum_tensor("PS", [P, 6, TOK], F32))
        Y = ctx.enter_context(nc.psum_tensor("Y", [P, 2 * TOK], F32))
        Yfm = Y[:, :].rearrange("p (m t) -> p m t", m=KD)
        Ytm = Y[:, :].rearrange("p (b d) -> p b d", b=TS)

        x_in = [sem(f"x_in{t}") for t in range(TILES // 2)]
        staged = [sem(f"staged{s}") for s in range(RING)]
        ba_in = [sem(f"ba_in{h}") for h in range(2)]
        bo_in, b1_in, b2_in, wo_in, w2_in, ln1_in, ln2_in = (
            sem(n) for n in ("bo_in", "b1_in", "b2_in", "wo_in", "w2_in", "ln1_in", "ln2_in"))
        k_mm, v_mm, q_mm, y_mm, yt_mm, x1t_mm, h_mm, z_mm, zt_mm, xt_mm = (
            sem(n) for n in ("k_mm", "v_mm", "q_mm", "y_mm", "yt_mm", "x1t_mm", "h_mm", "z_mm", "zt_mm", "xt_mm"))
        b_neg, nk, ek, rk, nq, eq, rq, y_act, x1_hi, h_act, z_act, xt_hi, log, inv = (
            sem(n) for n in ("b_neg", "nk", "ek", "rk", "nq", "eq", "rq", "y_act", "x1_hi", "h_act", "z_act", "xt_hi",
                             "log", "inv"))
        k_exp, k_sum, kv_sum, stat, q_exp, denom, residue, recip, xt_lo, x1_lo = (
            sem(n) for n in ("k_exp", "k_sum", "kv_sum", "stat", "q_exp", "denom", "residue", "recip", "xt_lo", "x1_lo"))
        res1, st1, mv1, n1, x1, res2, st2, mv2, n2, mv0 = (
            sem(n) for n in ("res1", "st1", "mv1", "n1", "x1", "res2", "st2", "mv2", "n2", "mv0"))
        half_set, att_s, att, w_hi, w_lo, r1, r2, xn_s, xn, r0 = (
            sem(n) for n in ("half_set", "att_s", "att", "w_hi", "w_lo", "r1", "r2", "xn_s", "xn", "r0"))

        def piece_incs(k):
            return 16 * (3 * KD if k < HC else 2)

        per_layer = [sum(piece_incs(k) for k in range(s, PIECES, RING)) for s in range(RING)]

        def staged_value(layer, k):
            return layer * per_layer[k % RING] + sum(piece_incs(j) for j in range(k % RING, k + 1, RING))

        block = ctx.enter_context(nc.Block())

        @block.sync
        def _(sp):
            def load_piece(layer, k, first):
                if not (first and k < RING):
                    sp.wait_ge(w_lo, layer * PIECES + (k - RING + 1))
                s = k % RING
                if k < HC:
                    for m, w in enumerate((Wk, Wv, Wq)):
                        dst = STAGE[:, s, m * KD * P:(m + 1) * KD * P]
                        for kc in range(KD):
                            src = w[layer, 2 * k:2 * k + 2, kc * P:(kc + 1) * P, :].rearrange("h p k -> p h k")
                            sp.dma_start(dst[:, kc * P:(kc + 1) * P].rearrange("p (h k) -> p h k", h=2),
                                         src).then_inc(staged[s], 16)
                else:
                    j = k - HC
                    for i in range(2):
                        m = 2 * j + i
                        sp.dma_start(STAGE[:, s, i * KD * P:(i + 1) * KD * P].rearrange("p (c n) -> p c n", c=KD),
                                     W1[layer, :, m * P:(m + 1) * P].rearrange("(c p) n -> p c n", p=P)
                                     ).then_inc(staged[s], 16)

            def load_ba(layer, half):
                cs = slice(half * HC // 2, (half + 1) * HC // 2)
                for m, b in enumerate((bk, bv, bq)):
                    src = b[layer, half * HEADS // 2:(half + 1) * HEADS // 2, :].rearrange("(c h) k -> (h k) c", h=2)
                    sp.dma_start(BA[:, m, cs], src, allow_slow_non_contiguous=True).then_inc(ba_in[half], 16)

            def load_ln(dst, scale, bias, layer, done):
                sp.dma_start(dst[:, 0, :], scale[bass.ds(layer, 1), :].to_broadcast([P, D])).then_inc(done, 16)
                sp.dma_start(dst[:, 1, :], bias[bass.ds(layer, 1), :].to_broadcast([P, D])).then_inc(done, 16)

            def load_fm(dst, b, layer, done):
                sp.dma_start(dst[:, :], b[layer, :].rearrange("(c p) -> p c", p=P),
                             allow_slow_non_contiguous=True).then_inc(done, 16)

            def load_wide(dst, w, layer, done):
                sp.dma_start(dst[:, :, :], w[layer, :, :].rearrange("(c p) n -> p c n", p=P)).then_inc(done, 16)

            def layer_loads(l):
                n = (l * TILES + TILES - 1) * HC
                for k in range(HC):
                    load_piece(l + 1, k, False)
                    if k % 4 == 3:
                        sp.wait_ge(rq, n + k + 1)
                        sp.wait_ge(kv_sum, n + k + 1)
                        load_ba(l + 1, k // 4)
                g = l * TILES + TILES
                sp.wait_ge(y_mm, g)
                load_wide(WO, Wo, l + 1, wo_in)
                sp.wait_ge(y_act, g)
                load_fm(BO, bo, l + 1, bo_in)
                sp.wait_ge(x1, g)
                load_ln(LN1P, s1, c1, l + 1, ln1_in)
                for k in range(HC, PIECES):
                    load_piece(l + 1, k, False)
                sp.wait_ge(h_act, g * HC)
                load_fm(B1, b1, l + 1, b1_in)
                sp.wait_ge(z_mm, g)
                load_wide(W2S, W2, l + 1, w2_in)
                sp.wait_ge(z_act, g)
                load_fm(B2, b2, l + 1, b2_in)
                sp.wait_ge(xn, g + TILES)
                load_ln(LN2P, s2, c2, l + 1, ln2_in)

            for t in range(TILES):
                sp.dma_start(X[:, t * TS:(t + 1) * TS, :],
                             x[t * TS:(t + 1) * TS, :, :].rearrange("b s d -> s b d")).then_inc(x_in[t // 2], 16)
                if t < RING:
                    load_piece(0, t, True)
            load_ba(0, 0)
            load_ba(0, 1)
            load_wide(WO, Wo, 0, wo_in)
            load_fm(BO, bo, 0, bo_in)
            load_ln(LN1P, s1, c1, 0, ln1_in)
            load_fm(B1, b1, 0, b1_in)
            load_wide(W2S, W2, 0, w2_in)
            load_fm(B2, b2, 0, b2_in)
            load_ln(LN2P, s2, c2, 0, ln2_in)
            for k in range(RING, PIECES):
                load_piece(0, k, True)
            with sp.Fori(0, LAYERS - 1, 1) as l:
                layer_loads(l)

        @block.gpsimd
        def _(pool):
            def split_piece(layer, k, first):
                s = k % RING
                pool.wait_ge(staged[s], staged_value(layer, k))
                if k < HC:
                    hi, lo = (w[:, k, :, :, :].rearrange("p m c n -> p (m c n)") for w in (WHI, WLO))
                    if not first:
                        pool.wait_ge(q_mm, layer * TILES * HC + (k + 1 - HC))
                    src = STAGE[:, s, :]
                else:
                    m = 2 * (k - HC)
                    hi, lo = (w[:, m:m + 2, :, :].rearrange("p m c n -> p (m c n)") for w in (W1HI, W1LO))
                    if not first:
                        pool.wait_ge(h_mm, layer * TILES * HC + (m + 2 - HC))
                    src = STAGE[:, s, 0:2 * KD * P]
                nc.gpsimd.tensor_tensor(hi, src, ONE[:, :].to_broadcast(src.shape), ALU.mult).then_inc(w_hi, 1)
                pool.wait_ge(w_hi, layer * PIECES + (k + 1))
                nc.gpsimd.tensor_tensor(lo, src, hi.bitcast(F32), ALU.subtract).then_inc(w_lo, 1)

            def rstd(out, var, eps, var_sem, var_value, done, value):
                pool.wait_ge(var_sem, var_value)
                nc.gpsimd.tensor_tensor(out, var, eps[:, 0:out.shape[1]], ALU.add).then_inc(done, 1)
                pool.wait_ge(done, 2 * value - 1)
                nc.gpsimd.tensor_tensor(out, out, HALF[:, 0:out.shape[1]], ALU.pow).then_inc(done, 1)

            nc.gpsimd.memset(ONE[:, :], 1.0)
            nc.gpsimd.memset(EPS0[:, :], 1e-5)
            nc.gpsimd.memset(EPS1[:, :], 1e-6)
            nc.gpsimd.memset(HALF[:, :], -0.5).then_inc(half_set, 1)
            pool.wait_ge(half_set, 1)
            for t in range(TILES):
                bs = slice(t * TS, (t + 1) * TS)
                rstd(RSTD0[:, bs], MV0[:, bs, 1], EPS0, mv0, 2 * t + 2, r0, t + 1)
                pool.wait_ge(r0, 2 * t + 2)
                for b in range(t * TS, (t + 1) * TS):
                    last = nc.gpsimd.tensor_scalar(X[:, b, :], X[:, b, :], MV0[:, b, 0:1], RSTD0[:, b:b + 1],
                                                   ALU.subtract, ALU.mult)
                last.then_inc(xn, 1)

            def attend(l, t, c):
                g, e = l * TILES + t, c % IRING
                n = g * HC + c
                pool.wait_ge(recip, n + 1)
                pool.wait_ge(stat, n * 5 + 5)
                r3 = INV[:, e, :].rearrange("p (b s) -> p b s", b=TS)
                nc.gpsimd.tensor_tensor(r3, r3, spread(CE[:, e, :], SEQ), ALU.mult).then_inc(att_s, 1)
                pool.wait_ge(att_s, n + 1)
                if c == 0 and not (type(g) is int and g == 0):
                    pool.wait_ge(y_mm, g)
                nc.gpsimd.tensor_tensor(ATT[:, c, :].rearrange("p (b s) -> p b s", b=TS), r3,
                                        spread(CC[:, e, :], SEQ), ALU.add).then_inc(att, 1)

            def slot(l, t, first=False, load=True):
                g = l * TILES + t
                tile = exists(l, t)
                nl, nt = slot_of(l, t + 1)
                more = exists(l, t + 1)
                splits = load and t == TILES - 2
                splits_w1 = load and t == TILES
                if splits:
                    split_piece(l + 1, 0, False)
                for c in range(1, HC):
                    if splits:
                        split_piece(l + 1, c, False)
                    if c == 3 and tile:
                        rstd(RSTD[:, 0, :], MV[:, 0, :, 1], EPS1, mv1, g + 1, r1, g + 1)
                    if c == 6 and not first:
                        rstd(RSTD[:, 1, :], MV[:, 1, :, 1], EPS1, mv2, g, r2, g)
                    if more:
                        attend(nl, nt, c - 1)
                    if splits_w1 and 2 <= c < 2 + PIECES - HC:
                        split_piece(l + 1, HC + c - 2, False)
                    if c == 6 and not first:
                        wl, w = slot_of(l, t - 1)
                        rw = R[:, w % 2, :, :]
                        pool.wait_ge(n2, g)
                        pool.wait_ge(ln2_in, (wl + 1) * 32)
                        nc.gpsimd.tensor_tensor(rw, rw, bcast(LN2P[:, 0, :], TS), ALU.mult).then_inc(xn_s, 1)
                        pool.wait_ge(xn_s, g)
                        nc.gpsimd.tensor_tensor(X[:, w * TS:(w + 1) * TS, :], rw, bcast(LN2P[:, 1, :], TS),
                                                ALU.add).then_inc(xn, 1)
                if exists(l, t + 1):
                    attend(nl, nt, HC - 1)

            split_piece(0, 0, True)
            split_piece(0, 1, True)
            for c in range(HC):
                if c + 2 < HC:
                    split_piece(0, c + 2, True)
                attend(0, 0, c)
            for k in range(HC, PIECES):
                split_piece(0, k, True)
            slot(0, 0, first=True)
            with pool.Fori(0, LAYERS - 1, 1) as l:
                for t in range(1, TILES + 1):
                    slot(l, t)
            for t in range(1, TILES + 1):
                slot(LAYERS - 1, t, load=False)

        @block.tensor
        def _(pe):
            def split_product(out, whi, wlo, xhi, xlo):
                for kc in range(KD):
                    nc.tensor.matmul(out, whi[:, kc, :], xhi[:, kc, :], start=(kc == 0), stop=False)
                    nc.tensor.matmul(out, whi[:, kc, :], xlo[:, kc, :], start=False, stop=False)
                    ins = nc.tensor.matmul(out, wlo[:, kc, :], xhi[:, kc, :], start=False, stop=(kc == KD - 1))
                return ins

            def project(l, t, c, free):
                g = l * TILES + t
                if c == 0:
                    pe.wait_ge(xt_hi, g + 1)
                    pe.wait_ge(xt_lo, g + 1)
                if t == 0:
                    pe.wait_ge(w_lo, l * PIECES + (c + 1))
                for m, done in enumerate((k_mm, v_mm, q_mm)):
                    for s, value in free[m:m + 1]:
                        pe.wait_ge(s, value)
                    split_product(PS[:, 3 * (c % 2) + m, :], WHI[:, c, m], WLO[:, c, m],
                                  XTHI[:, t % 2], XTLO[:, t % 2]).then_inc(done, 1)

            def after_chunk(n):
                return [(rk, n - 1), (kv_sum, n - 1), (rq, n - 1)]

            def input_fm(j, t):
                pe.wait_ge(xn, j + 1)
                for kc in range(KD):
                    for b in range(TS):
                        ins = nc.tensor.transpose(Yfm[:, kc, b * P:(b + 1) * P],
                                                  X[:, t * TS + b, kc * P:(kc + 1) * P], ident[:, :])
                ins.then_inc(xt_mm, 1)

            def to_tm(done, value, transposed):
                pe.wait_ge(done, value)
                for b in range(TS):
                    for kc in range(KD):
                        ins = nc.tensor.transpose(Ytm[:, b, kc * P:(kc + 1) * P], T[:, kc, b * P:(b + 1) * P],
                                                  ident[:, :])
                ins.then_inc(transposed, 1)

            def down(w, src, m):
                for c in range(HC):
                    ins = nc.tensor.matmul(Yfm[:, m, :], w[:, c, m * P:(m + 1) * P], src[:, c, :],
                                           start=(c == 0), stop=(c == HC - 1))
                return ins

            def hidden(l, t, g):
                if t == 0:
                    pe.wait_ge(w_lo, (l + 1) * PIECES)
                pe.wait_ge(x1_hi, g + 1)
                pe.wait_ge(x1_lo, g + 1)
                chunks = (g + 2) * HC if exists(l, t + 1) else LAST * HC
                for m in range(HC):
                    if m < 3:
                        pe.wait_ge((rk, kv_sum, rq)[m], chunks)
                    else:
                        pe.wait_ge(h_act, g * HC + (m - 2))
                    split_product(PS[:, 3 + m % 3, :], W1HI[:, m], W1LO[:, m], X1HI, X1LO).then_inc(h_mm, 1)

            def slot(l, t, first=False):
                g = l * TILES + t
                n = (g + 1) * HC
                tl, tt = slot_of(l, t)
                nl, nt = slot_of(l, t + 1)
                tile, more, after = exists(l, t), exists(l, t + 1), exists(l, t + 2)
                if more:
                    free = after_chunk(n + 1) if first else [(h_act, n - HC - 1), (h_act, n - HC), (h_act, n - HC - 2)]
                    project(nl, nt, 1, free)
                if tile:
                    inputs = g + 3 if after else LAST
                    pe.wait_ge(xt_hi, inputs)
                    pe.wait_ge(xt_lo, inputs)
                    pe.wait_ge(att, n)
                    if tt == 0:
                        pe.wait_ge(wo_in, (tl + 1) * 16)
                    down(WO, ATT, 0)
                if more:
                    project(nl, nt, 2, after_chunk(n + 2))
                if tile:
                    down(WO, ATT, 1).then_inc(y_mm, 1)
                if more:
                    project(nl, nt, 3, after_chunk(n + 3))
                if tile:
                    to_tm(y_act, g + 1, yt_mm)
                if more:
                    project(nl, nt, 4, after_chunk(n + 4))
                if not first:
                    if tile:
                        pe.wait_ge(res1, g + 1)
                    wl, w = slot_of(l, t - 1)
                    if w == 0:
                        pe.wait_ge(w2_in, (wl + 1) * 16)
                    pe.wait_ge(h_act, g * HC)
                    down(W2S, H, 0)
                if more:
                    project(nl, nt, 5, after_chunk(n + 5))
                if not first:
                    down(W2S, H, 1).then_inc(z_mm, 1)
                if more:
                    project(nl, nt, 6, after_chunk(n + 6))
                if not first:
                    to_tm(z_act, g, zt_mm)
                if more:
                    project(nl, nt, 7, after_chunk(n + 7))
                if tile:
                    pe.wait_ge(x1, g + 1)
                    if not first:
                        pe.wait_ge(res2, g)
                    for kc in range(KD):
                        for b in range(TS):
                            ins = nc.tensor.transpose(Yfm[:, kc, b * P:(b + 1) * P],
                                                      R[:, t % 2, b, kc * P:(kc + 1) * P], ident[:, :])
                    ins.then_inc(x1t_mm, 1)
                if after:
                    al, at = slot_of(l, t + 2)
                    project(al, at, 0, after_chunk(n + HC))
                if tile:
                    hidden(tl, tt, g)
                if exists(l, t + 3):
                    input_fm(g + 3, slot_of(l, t + 3)[1])

            for t in range(2):
                if t > 0:
                    pe.wait_ge(xt_hi, t)
                    pe.wait_ge(xt_lo, t)
                input_fm(t, t)
            for c in range(HC):
                project(0, 0, c, after_chunk(c) if c >= 2 else [])
            pe.wait_ge(xt_hi, 2)
            pe.wait_ge(xt_lo, 2)
            input_fm(2, 2)
            project(0, 1, 0, after_chunk(HC))
            slot(0, 0, first=True)
            with pe.Fori(0, LAYERS - 1, 1) as l:
                for t in range(1, TILES + 1):
                    slot(l, t)
            for t in range(1, TILES + 1):
                slot(LAYERS - 1, t)

        @block.scalar
        def _(act):
            def chunk(l, t, c):
                n = (l * TILES + t) * HC + c
                p, half = c % 2, 3 * (c % 2)
                if t == 0 and c % 4 == 0:
                    cs = slice(c, c + 4)
                    act.wait_ge(ba_in[c // 4], (l + 1) * 48)
                    nc.scalar.mul(BNEG[:, :, cs], BA[:, :, cs], -1.0).then_inc(b_neg, 1)
                    act.wait_ge(b_neg, 2 * l + (c // 4 + 1))
                act.wait_ge(k_mm, n + 1)
                if not (type(n) is int and n < 2):
                    act.wait_ge(kv_sum, n - 1)
                nc.scalar.activation(EK[:, p, :], PS[:, half, :], ACT.Relu, scale=-1.0,
                                     bias=BNEG[:, 0, c:c + 1]).then_inc(nk, 1)
                nc.scalar.activation(RK[:, p, :], PS[:, half, :], ACT.Relu, bias=BA[:, 0, c:c + 1]).then_inc(rk, 1)
                act.wait_ge(nk, n + 1)
                nc.scalar.activation(EK[:, p, :], EK[:, p, :], ACT.Exp, scale=-1.0).then_inc(ek, 1)
                act.wait_ge(q_mm, n + 1)
                if not (type(n) is int and n < 2):
                    act.wait_ge(recip, n - 1)
                nc.scalar.activation(EQ[:, p, :], PS[:, half + 2, :], ACT.Relu, scale=-1.0,
                                     bias=BNEG[:, 2, c:c + 1]).then_inc(nq, 1)
                if not (type(n) is int and n < 2):
                    act.wait_ge(denom, n - 1)
                nc.scalar.activation(RQ[:, p, :], PS[:, half + 2, :], ACT.Relu, bias=BA[:, 2, c:c + 1]).then_inc(rq, 1)
                act.wait_ge(nq, n + 1)
                nc.scalar.activation(EQ[:, p, :], EQ[:, p, :], ACT.Exp, scale=-1.0).then_inc(eq, 1)
                if not (type(n) is int and n < 1):
                    invert(n - 1, (c - 1) % HC)

            def invert(n, c):
                e = c % IRING
                act.wait_ge(denom, n + 1)
                if not (type(n) is int and n < IRING):
                    act.wait_ge(att, n - (IRING - 1))
                nc.scalar.activation(INV[:, e, :], EQ[:, c % 2, :], ACT.Ln).then_inc(log, 1)
                act.wait_ge(log, n + 1)
                nc.scalar.activation(INV[:, e, :], INV[:, e, :], ACT.Exp, scale=-1.0).then_inc(inv, 1)

            def attention_tables():
                nc.scalar.preload_act_table_set("natural_log_exp_and_others")

            def input_hi(j, t):
                act.wait_ge(xt_mm, j + 1)
                nc.scalar.copy(XTHI[:, t % 2, :, :], Yfm[:, :, :]).then_inc(xt_hi, 1)

            def gelu_down(mm, bias, bias_in, done, l, t, value):
                if t == 0:
                    act.wait_ge(bias_in, (l + 1) * 16)
                act.wait_ge(mm, value)
                for m in range(KD):
                    ins = nc.scalar.activation(T[:, m, :], Yfm[:, m, :], ACT.Gelu_apprx_tanh, bias=bias[:, m:m + 1])
                ins.then_inc(done, 1)

            def hidden(l, t, g):
                if t == 0:
                    act.wait_ge(b1_in, (l + 1) * 16)
                for m in range(HC):
                    act.wait_ge(h_mm, g * HC + (m + 1))
                    nc.scalar.activation(H[:, m, :], PS[:, 3 + m % 3, :], ACT.Gelu_apprx_tanh,
                                         bias=B1[:, m:m + 1]).then_inc(h_act, 1)

            def slot(l, t, first=False):
                g = l * TILES + t
                tl, tt = slot_of(l, t)
                nl, nt = slot_of(l, t + 1)
                tile, more = exists(l, t), exists(l, t + 1)
                if more:
                    chunk(nl, nt, 1)
                    chunk(nl, nt, 2)
                elif tile:
                    invert(LAST * HC - 1, HC - 1)
                if tile:
                    gelu_down(y_mm, BO, bo_in, y_act, tl, tt, g + 1)
                if more:
                    attention_tables()
                    for c in (3, 4, 5):
                        chunk(nl, nt, c)
                if not first:
                    wl, w = slot_of(l, t - 1)
                    gelu_down(z_mm, B2, b2_in, z_act, wl, w, g)
                if more:
                    if not first:
                        attention_tables()
                    for c in (6, 7):
                        chunk(nl, nt, c)
                if tile:
                    act.wait_ge(x1t_mm, g + 1)
                    nc.scalar.copy(X1HI[:, :, :], Yfm[:, :, :]).then_inc(x1_hi, 1)
                if exists(l, t + 2):
                    al, at = slot_of(l, t + 2)
                    chunk(al, at, 0)
                if tile:
                    hidden(tl, tt, g)
                if exists(l, t + 3):
                    input_hi(g + 3, t + 3)
                if more:
                    attention_tables()

            attention_tables()
            input_hi(0, 0)
            input_hi(1, 1)
            for c in range(HC):
                chunk(0, 0, c)
            input_hi(2, 2)
            chunk(0, 1, 0)
            slot(0, 0, first=True)
            with act.Fori(0, LAYERS - 1, 1) as l:
                for t in range(1, TILES + 1):
                    slot(l, t)
            for t in range(1, TILES + 1):
                slot(LAYERS - 1, t)

        @block.vector
        def _(dve):
            def seq(b):
                return slice(b * SEQ, (b + 1) * SEQ)

            def keys(l, t, c):
                n = (l * TILES + t) * HC + c
                p, e, half = c % 2, c % IRING, 3 * (c % 2)
                dve.wait_ge(ek, n + 1)
                nc.vector.tensor_scalar(EK[:, p, :], EK[:, p, :], -1.0, 1.0, ALU.add, ALU.add).then_inc(k_exp, 1)
                dve.wait_ge(rk, n + 1)
                dve.wait_ge(k_exp, n + 1)
                for b in range(TS):
                    ins = nc.vector.scalar_tensor_tensor(RK[:, p, seq(b)], RK[:, p, seq(b)], 0.0, EK[:, p, seq(b)],
                                                         ALU.add, ALU.add, accum_out=SUMK[:, p, b:b + 1])
                ins.then_inc(k_sum, 1)
                dve.wait_ge(v_mm, n + 1)
                if t == 0 and c % 4 == 0:
                    dve.wait_ge(ba_in[c // 4], (l + 1) * 48)
                dve.wait_ge(k_sum, n + 1)
                for b in range(TS):
                    ins = nc.vector.scalar_tensor_tensor(EK[:, p, seq(b)], PS[:, half + 1, seq(b)], BA[:, 1, c:c + 1],
                                                         RK[:, p, seq(b)], ALU.add, ALU.mult,
                                                         accum_out=KVS[:, p, b:b + 1])
                ins.then_inc(kv_sum, 1)
                nc.vector.tensor_scalar(SUMK[:, p, :], SUMK[:, p, :], TINY, None, ALU.max).then_inc(stat, 1)
                dve.wait_ge(stat, n * 5 + 1)
                nc.vector.reciprocal(RSK[:, p, :], SUMK[:, p, :]).then_inc(stat, 1)
                dve.wait_ge(stat, n * 5 + 2)
                nc.vector.tensor_scalar(ES[:, p, :], RSK[:, p, :], EPS_ATT, None, ALU.mult).then_inc(stat, 1)
                dve.wait_ge(kv_sum, n + 1)
                if not (type(n) is int and n < IRING):
                    dve.wait_ge(att, n - (IRING - 1))
                nc.vector.tensor_tensor(CC[:, e, :], KVS[:, p, :], RSK[:, p, :], ALU.mult).then_inc(stat, 1)
                dve.wait_ge(stat, n * 5 + 4)
                nc.vector.tensor_tensor(CE[:, e, :], CC[:, e, :], ES[:, p, :], ALU.mult).then_inc(stat, 1)

            def queries(l, t, c):
                n = (l * TILES + t) * HC + c
                p = c % 2
                dve.wait_ge(eq, n + 1)
                nc.vector.tensor_scalar(EQ[:, p, :], EQ[:, p, :], -1.0, 1.0, ALU.add, ALU.add).then_inc(q_exp, 1)
                if not (type(n) is int and n < 1):
                    residues(n - 1, (c - 1) % HC)
                dve.wait_ge(rq, n + 1)
                dve.wait_ge(q_exp, n + 1)
                dve.wait_ge(stat, n * 5 + 3)
                for b in range(TS):
                    ins = nc.vector.scalar_tensor_tensor(EQ[:, p, seq(b)], EQ[:, p, seq(b)], ES[:, p, b:b + 1],
                                                         RQ[:, p, seq(b)], ALU.add, ALU.add)
                ins.then_inc(denom, 1)
                if not (type(n) is int and n < 1):
                    inverses(n - 1, (c - 1) % HC)

            def residues(n, c):
                dve.wait_ge(inv, n + 1)
                nc.vector.tensor_tensor(EQ[:, c % 2, :], EQ[:, c % 2, :], INV[:, c % IRING, :],
                                        ALU.mult).then_inc(residue, 1)

            def inverses(n, c):
                e = c % IRING
                dve.wait_ge(residue, n + 1)
                nc.vector.scalar_tensor_tensor(INV[:, e, :], EQ[:, c % 2, :], 2.0, INV[:, e, :], ALU.subtract,
                                               ALU.mult).then_inc(recip, 1)

            def input_lo(j, t):
                dve.wait_ge(xt_hi, j + 1)
                nc.vector.tensor_tensor(XTLO[:, t % 2, :, :], Yfm[:, :, :], XTHI[:, t % 2, :, :].bitcast(F32),
                                        ALU.subtract).then_inc(xt_lo, 1)

            def residual(w, value, stats, means, mm, add, res, i):
                dve.wait_ge(mm, value)
                nc.vector.tensor_tensor(R[:, w, :, :], Ytm[:, :, :], add, ALU.add).then_inc(res, 1)
                dve.wait_ge(res, value)
                for b in range(TS):
                    ins = nc.vector.bn_stats(ST[:, b, :], R[:, w, b, :])
                ins.then_inc(stats, 1)
                dve.wait_ge(stats, value)
                nc.vector.memset(CARRY[:, :], 0.0)
                for b in range(TS):
                    ins = nc.vector.bn_aggr(MV[:, i, b, :], ST[:, b, :])
                ins.then_inc(means, 1)

            def normed(w, value, means, rstds, done, i):
                dve.wait_ge(rstds, 2 * value)
                dve.wait_ge(means, value)
                for b in range(TS):
                    ins = nc.vector.tensor_scalar(R[:, w, b, :], R[:, w, b, :], MV[:, i, b, 0:1], RSTD[:, i, b:b + 1],
                                                  ALU.subtract, ALU.mult)
                ins.then_inc(done, 1)

            def slot(l, t, first=False):
                g = l * TILES + t
                tl, tt = slot_of(l, t)
                nl, nt = slot_of(l, t + 1)
                tile, more = exists(l, t), exists(l, t + 1)
                if more:
                    for c in (1, 2):
                        keys(nl, nt, c)
                        queries(nl, nt, c)
                    keys(nl, nt, 3)
                elif tile:
                    residues(LAST * HC - 1, HC - 1)
                    inverses(LAST * HC - 1, HC - 1)
                if tile:
                    dve.wait_ge(xn, g + 3)
                    residual(t % 2, g + 1, st1, mv1, yt_mm, X[:, tt * TS:(tt + 1) * TS, :], res1, 0)
                if more:
                    queries(nl, nt, 3)
                    keys(nl, nt, 4)
                if tile:
                    normed(t % 2, g + 1, mv1, r1, n1, 0)
                if more:
                    queries(nl, nt, 4)
                if tile:
                    rt = R[:, t % 2, :, :]
                    dve.wait_ge(n1, 2 * g + 1)
                    if tt == 0:
                        dve.wait_ge(ln1_in, (tl + 1) * 32)
                    nc.vector.tensor_tensor(rt, rt, bcast(LN1P[:, 0, :], TS), ALU.mult).then_inc(n1, 1)
                    dve.wait_ge(n1, 2 * g + 2)
                    nc.vector.tensor_tensor(rt, rt, bcast(LN1P[:, 1, :], TS), ALU.add).then_inc(x1, 1)
                if more:
                    keys(nl, nt, 5)
                    queries(nl, nt, 5)
                    keys(nl, nt, 6)
                if not first:
                    w = (t - 1) % 2
                    residual(w, g, st2, mv2, zt_mm, R[:, w, :, :], res2, 1)
                if more:
                    queries(nl, nt, 6)
                    keys(nl, nt, 7)
                if not first:
                    normed(w, g, mv2, r2, n2, 1)
                if more:
                    queries(nl, nt, 7)
                if tile:
                    dve.wait_ge(x1_hi, g + 1)
                    nc.vector.tensor_tensor(X1LO[:, :, :], Yfm[:, :, :], X1HI[:, :, :].bitcast(F32),
                                            ALU.subtract).then_inc(x1_lo, 1)
                if exists(l, t + 2):
                    al, at = slot_of(l, t + 2)
                    keys(al, at, 0)
                    queries(al, at, 0)
                if exists(l, t + 3):
                    input_lo(g + 3, t + 3)

            for t in range(TILES):
                if t % 2 == 0:
                    dve.wait_ge(x_in[t // 2], 32)
                for b in range(t * TS, (t + 1) * TS):
                    ins = nc.vector.bn_stats(ST0[:, b, :], X[:, b, :])
                ins.then_inc(mv0, 1)
                dve.wait_ge(mv0, 2 * t + 1)
                for b in range(t * TS, (t + 1) * TS):
                    ins = nc.vector.bn_aggr(MV0[:, b, :], ST0[:, b, :])
                ins.then_inc(mv0, 1)
            input_lo(0, 0)
            input_lo(1, 1)
            for c in range(HC):
                keys(0, 0, c)
                queries(0, 0, c)
            input_lo(2, 2)
            keys(0, 1, 0)
            queries(0, 1, 0)
            slot(0, 0, first=True)
            with dve.Fori(0, LAYERS - 1, 1) as l:
                for t in range(1, TILES + 1):
                    slot(l, t)
            for t in range(1, TILES + 1):
                slot(LAYERS - 1, t)


XH, XK = 16, 16
CH = P // XK
CTX = 128


def cross_attention(nc, X, ident, x, ctx_in, Wq, bq, Wk, bk, Wv, bv, Wo, bo):
    with ExitStack() as ctx:
        def sb(name, shape, dt=F32):
            return ctx.enter_context(nc.sbuf_tensor(name, shape, dt))

        def sem(name):
            return ctx.enter_context(nc.semaphore(name))

        XIN = sb("XIN", [P, SEQS, D])
        CTXS = sb("CTXS", [P, SEQS, CTX])
        WQ = sb("XWQ", [P, KD, D])
        WK = sb("XWK", [P, D])
        WV = sb("XWV", [P, D])
        WOX = sb("XWO", [P, KD, D])
        BQ = sb("XBQ", [P, KD])
        BK = sb("XBK", [P, KD])
        BV = sb("XBV", [P, D])
        BOX = sb("XBO", [P, D])
        ONES = sb("XONES", [P, 1024])
        MASK = sb("XMASK", [P, CH, SEQ])
        HALF = sb("XHALF", [P, SEQS])
        ST = sb("XST", [P, SEQS, 6])
        MV = sb("XMV", [P, SEQS, 2])
        RSTD = sb("XRSTD", [P, SEQS])
        Z = sb("XZ", [P, 2, D])
        CSEQ = sb("XCSEQ", [P, 2, CTX])
        ZT = sb("XZT", [P, 2, KD, P])
        CT = sb("XCT", [P, 2, P])
        QT = sb("XQT", [P, 2, KD, P])
        KT = sb("XKT", [P, 2, KD, P])
        KX = sb("XKX", [P, 2, CH, SEQ])
        V1 = sb("XV1", [P, 2, XH, XK + 1])
        MX = sb("XMX", [P, 2, CH])
        E = sb("XE", [P, 2, CH, SEQ])
        ET = sb("XET", [P, 2, CH, SEQ])
        RD = sb("XRD", [P, 2, CH])
        O = sb("XO", [P, 2, D])
        OT = sb("XOT", [P, 2, KD, P])
        S = ctx.enter_context(nc.psum_tensor("XS", [P, 2, CH * SEQ], F32))
        PT = ctx.enter_context(nc.psum_tensor("XPT", [P, CH * SEQ], F32))
        A = ctx.enter_context(nc.psum_tensor("XA", [P, 512], F32))
        B = ctx.enter_context(nc.psum_tensor("XB", [P, 512], F32))

        x_in, c_in, w_in, bias_in = (sem(n) for n in ("xx_in", "xc_in", "xw_in", "xbias_in"))
        set0, ones_set, v0, r0, mask_set, kx = (sem(n) for n in ("xset0", "xones_set", "xv0", "xr0", "xmask_set", "xkx"))
        prep, z, mx, sh, rd, o, v1, ob, upd = (
            sem(n) for n in ("xprep", "xz", "xmx", "xsh", "xrd", "xo", "xv1", "xob", "xupd"))
        zct_mm, qk_mm, v_mm, s_mm, pt_mm, pv_mm, ot_mm, p_mm = (
            sem(n) for n in ("xzct_mm", "xqk_mm", "xv_mm", "xs_mm", "xpt_mm", "xpv_mm", "xot_mm", "xp_mm"))
        zct, qt, kt, e, et, ot = (sem(n) for n in ("xzct", "xqt", "xkt", "xe", "xet", "xot"))
        block = ctx.enter_context(nc.Block())

        @block.sync
        def _(sp):
            sp.dma_start(XIN[:, :, :], x.rearrange("b s d -> s b d")).then_inc(x_in, 16)
            sp.dma_start(CTXS[:, :, :], ctx_in.rearrange("b s d -> s b d")).then_inc(c_in, 16)
            sp.dma_start(WQ[:, :, :], Wq.rearrange("(c p) n -> p c n", p=P)).then_inc(w_in, 16)
            sp.dma_start(WK[:, :], Wk).then_inc(w_in, 16)
            sp.dma_start(WV[:, :], Wv).then_inc(w_in, 16)
            sp.dma_start(WOX[:, :, :], Wo.rearrange("(c p) n -> p c n", p=P)).then_inc(w_in, 16)
            sp.dma_start(BQ[:, :], bq.rearrange("(c p) -> p c", p=P), allow_slow_non_contiguous=True).then_inc(bias_in, 16)
            sp.dma_start(BK[:, :], bk.rearrange("(c p) -> p c", p=P), allow_slow_non_contiguous=True).then_inc(bias_in, 16)
            sp.dma_start(BV[:, :], bv.unsqueeze(0).to_broadcast([P, D])).then_inc(bias_in, 16)
            sp.dma_start(BOX[:, :], bo.unsqueeze(0).to_broadcast([P, D])).then_inc(bias_in, 16)

        @block.gpsimd
        def _(pool):
            nc.gpsimd.memset(HALF[:, :], -0.5).then_inc(set0, 1)
            nc.gpsimd.memset(MASK[:, :, :], 1.0).then_inc(set0, 1)
            nc.gpsimd.memset(V1[:, :, :, XK:XK + 1], 1.0).then_inc(ones_set, 1)
            pool.wait_ge(set0, 2)
            nc.gpsimd.affine_select(out=MASK[:, :, :], in_=MASK[:, :, :], compare_op=ALU.is_ge, fill=0.0, base=0,
                                    pattern=[[-XK, CH], [0, SEQ]], channel_multiplier=1).then_inc(mask_set, 1)
            pool.wait_ge(mask_set, 1)
            nc.gpsimd.affine_select(out=MASK[:, :, :], in_=MASK[:, :, :], compare_op=ALU.is_ge, fill=0.0, base=XK - 1,
                                    pattern=[[XK, CH], [0, SEQ]], channel_multiplier=-1).then_inc(mask_set, 1)
            pool.wait_ge(prep, 3)
            nc.gpsimd.tensor_scalar(RSTD[:, :], MV[:, :, 1], 1e-5, None, ALU.add).then_inc(v0, 1)
            pool.wait_ge(v0, 1)
            nc.gpsimd.tensor_tensor(RSTD[:, :], RSTD[:, :], HALF[:, :], ALU.pow).then_inc(r0, 1)
            pool.wait_ge(mask_set, 2)

            def unit(i, j, c):
                u = (2 * i + j) * KD + c
                pool.wait_ge(kt, 2 * i + (j + 1))
                if not (type(i) is int and u < 2):
                    pool.wait_ge(s_mm, u - 1)
                nc.gpsimd.tensor_tensor(KX[:, c, :, :], bcast(KT[:, j, c, :], CH), MASK[:, :, :], ALU.mult).then_inc(kx, 1)

            for j in range(2):
                for c in range(KD):
                    unit(0, j, c)
            with pool.Fori(1, SEQS // 2, 1) as i:
                for j in range(2):
                    for c in range(KD):
                        unit(i, j, c)

        @block.tensor
        def _(pe):
            def prepare(i, j):
                b = 2 * i + j
                pe.wait_ge(z, b + 1)
                if not (type(i) is int and b == 0):
                    pe.wait_ge(v1, b)
                for kc in range(KD):
                    nc.tensor.transpose(A[:, kc * P:(kc + 1) * P], Z[:, j, kc * P:(kc + 1) * P], ident[:, :])
                nc.tensor.transpose(A[:, 2 * P:3 * P], CSEQ[:, j, :], ident[:, :]).then_inc(zct_mm, 1)
                pe.wait_ge(zct, b + 1)
                for c in range(KD):
                    for kc in range(KD):
                        nc.tensor.matmul(A[:, c * P:(c + 1) * P], WQ[:, kc, c * P:(c + 1) * P], ZT[:, j, kc, :],
                                         start=(kc == 0), stop=(kc == KD - 1))
                for c in range(KD):
                    ins = nc.tensor.matmul(A[:, (2 + c) * P:(3 + c) * P], WK[:, c * P:(c + 1) * P], CT[:, j, :],
                                           start=True, stop=True)
                ins.then_inc(qk_mm, 1)
                pe.wait_ge(qt, b + 1)
                pe.wait_ge(kt, b + 1)
                nc.tensor.matmul(A[:, 0:D], CT[:, j, :], WV[:, :], start=True, stop=True).then_inc(v_mm, 1)

            def scores(i, j, c):
                u = (2 * i + j) * KD + c
                pe.wait_ge(kx, u + 1)
                if not (type(i) is int and u < 2):
                    pe.wait_ge(sh, u - 1)
                for hf in range(2):
                    ins = nc.tensor.matmul(S[:, c, hf * 512:(hf + 1) * 512], QT[:, j, c, :],
                                           KX[:, c, hf * 4:(hf + 1) * 4, :].rearrange("p h s -> p (h s)"),
                                           start=True, stop=True)
                ins.then_inc(s_mm, 1)

            def weigh(i, j, c):
                u = (2 * i + j) * KD + c
                pe.wait_ge(e, u + 1)
                if not (type(i) is int and u < 1):
                    pe.wait_ge(et, u)
                for h in range(CH):
                    ins = nc.tensor.transpose(PT[:, h * SEQ:(h + 1) * SEQ], E[:, c, h, :], ident[:, :])
                ins.then_inc(pt_mm, 1)
                pe.wait_ge(et, u + 1)
                pe.wait_ge(v1, 2 * i + (j + 1))
                if not (type(i) is int and u < 1):
                    pe.wait_ge(o, u)
                for h in range(CH):
                    ins = nc.tensor.matmul(B[:, h * (XK + 1):(h + 1) * (XK + 1)], ET[:, c, h, :], V1[:, j, c * CH + h, :],
                                           start=True, stop=True)
                ins.then_inc(pv_mm, 1)

            def project(i, j):
                b = 2 * i + j
                pe.wait_ge(o, (b + 1) * KD)
                for kc in range(KD):
                    ins = nc.tensor.transpose(B[:, 256 + kc * P:256 + (kc + 1) * P], O[:, j, kc * P:(kc + 1) * P],
                                              ident[:, :])
                ins.then_inc(ot_mm, 1)
                pe.wait_ge(ot, b + 1)
                for kc in range(KD):
                    ins = nc.tensor.matmul(B[:, 256:512], OT[:, j, kc, :], WOX[:, kc, :], start=(kc == 0),
                                           stop=(kc == KD - 1))
                ins.then_inc(p_mm, 1)
                pe.wait_ge(upd, b + 1)

            def seq_steps(i, j):
                prepare(i, j)
                for c in range(KD):
                    scores(i, j, c)
                for c in range(KD):
                    weigh(i, j, c)
                project(i, j)

            pe.wait_ge(w_in, 64)
            pe.wait_ge(ones_set, 1)
            for j in range(2):
                seq_steps(0, j)
            with pe.Fori(1, SEQS // 2, 1) as i:
                for j in range(2):
                    seq_steps(i, j)

        @block.scalar
        def _(act):
            def seq_steps(i, j):
                b = 2 * i + j
                act.wait_ge(zct_mm, b + 1)
                nc.scalar.copy(ZT[:, j, :, :], A[:, 0:2 * P].rearrange("p (c t) -> p c t", c=KD))
                nc.scalar.copy(CT[:, j, :], A[:, 2 * P:3 * P]).then_inc(zct, 1)
                act.wait_ge(qk_mm, b + 1)
                for c in range(KD):
                    ins = nc.scalar.activation(QT[:, j, c, :], A[:, c * P:(c + 1) * P], ACT.Identity, bias=BQ[:, c:c + 1])
                ins.then_inc(qt, 1)
                for c in range(KD):
                    ins = nc.scalar.activation(KT[:, j, c, :], A[:, (2 + c) * P:(3 + c) * P], ACT.Identity,
                                               bias=BK[:, c:c + 1])
                ins.then_inc(kt, 1)
                for c in range(KD):
                    u = b * KD + c
                    act.wait_ge(sh, u + 1)
                    nc.scalar.activation(E[:, c, :, :], E[:, c, :, :], ACT.Exp, scale=XK ** -0.5).then_inc(e, 1)
                for c in range(KD):
                    u = b * KD + c
                    act.wait_ge(pt_mm, u + 1)
                    nc.scalar.copy(ET[:, c, :, :], PT[:, :].rearrange("p (h s) -> p h s", h=CH)).then_inc(et, 1)
                act.wait_ge(ot_mm, b + 1)
                nc.scalar.copy(OT[:, j, :, :], B[:, 256:512].rearrange("p (c t) -> p c t", c=KD)).then_inc(ot, 1)

            act.wait_ge(bias_in, 64)
            with act.Fori(0, SEQS // 2, 1) as i:
                for j in range(2):
                    seq_steps(i, j)

        @block.vector
        def _(dve):
            dve.wait_ge(x_in, 16)
            nc.vector.tensor_tensor(X[:, :, :], X[:, :, :], XIN[:, :, :], ALU.add).then_inc(prep, 1)
            dve.wait_ge(prep, 1)
            for b in range(SEQS):
                ins = nc.vector.bn_stats(ST[:, b, :], X[:, b, :])
            ins.then_inc(prep, 1)
            dve.wait_ge(prep, 2)
            for b in range(SEQS):
                ins = nc.vector.bn_aggr(MV[:, b, :], ST[:, b, :])
            ins.then_inc(prep, 1)
            dve.wait_ge(r0, 1)
            dve.wait_ge(prep, 3)
            dve.wait_ge(bias_in, 64)
            dve.wait_ge(c_in, 16)

            def seq_steps(i, j):
                b = 2 * i + j
                nc.vector.tensor_copy(CSEQ[:, j, :], CTXS[:, b, :])
                nc.vector.tensor_scalar(Z[:, j, :], X[:, b, :], MV[:, b, 0:1], RSTD[:, bass.ds(b, 1)], ALU.subtract,
                                        ALU.mult).then_inc(z, 1)
                dve.wait_ge(v_mm, b + 1)
                nc.vector.tensor_tensor(V1[:, j, :, 0:XK], A[:, 0:D].rearrange("p (h k) -> p h k", h=XH),
                                        BV[:, :].rearrange("p (h k) -> p h k", h=XH), ALU.add).then_inc(v1, 1)
                for c in range(KD):
                    u = b * KD + c
                    dve.wait_ge(s_mm, u + 1)
                    scores = S[:, c, :].rearrange("p (h s) -> p h s", h=CH)
                    nc.vector.tensor_reduce(MX[:, c, :], scores, AX.X, ALU.max).then_inc(mx, 1)
                    dve.wait_ge(mx, u + 1)
                    nc.vector.tensor_tensor(E[:, c, :, :], scores, spread(MX[:, c, :], SEQ), ALU.subtract).then_inc(sh, 1)
                for c in range(KD):
                    u = b * KD + c
                    dve.wait_ge(pv_mm, u + 1)
                    out = B[:, 0:CH * (XK + 1)].rearrange("p (h k) -> p h k", h=CH)
                    nc.vector.reciprocal(RD[:, c, :], out[:, :, XK]).then_inc(rd, 1)
                    dve.wait_ge(rd, u + 1)
                    nc.vector.tensor_tensor(O[:, j, c * P:(c + 1) * P].rearrange("p (h k) -> p h k", h=CH),
                                            out[:, :, 0:XK], spread(RD[:, c, :], XK), ALU.mult).then_inc(o, 1)
                nc.vector.tensor_tensor(X[:, b, :], X[:, b, :], BOX[:, :], ALU.add).then_inc(ob, 1)
                dve.wait_ge(p_mm, b + 1)
                dve.wait_ge(ob, b + 1)
                nc.vector.tensor_tensor(X[:, b, :], X[:, b, :], B[:, 256:512], ALU.add).then_inc(upd, 1)

            with dve.Fori(0, SEQS // 2, 1) as i:
                for j in range(2):
                    seq_steps(i, j)


E, FF = 8, 512
FC = FF // P
SHARED = E
EA = E + 1
RT = SEQS + E
UNITS = SEQS + RT
ROWS = UNITS * P


def mixture(nc, X, ident, out, gate_w, shared, routed):
    rows_in = nc.dram_tensor("rows_in", (ROWS, D), F32, kind="Internal").ap()
    rows_out = nc.dram_tensor("rows_out", (ROWS, D), F32, kind="Internal").ap()
    with ExitStack() as ctx:
        def sb(name, shape, dt=F32):
            return ctx.enter_context(nc.sbuf_tensor(name, shape, dt))

        WGU = sb("WGU", [P, EA, 2, KD, FF])
        WD = sb("WD", [P, EA, FC, D])
        EID = sb("EID", [P, UNITS], I32)
        ROW = sb("ROW", [P, SEQS], U32)
        PSX = ctx.enter_context(nc.psum_tensor("PSX", [P, 8, 512], F32))
        route(nc, X, ident, gate_w, shared, routed, rows_in, WGU, WD, EID, ROW, PSX)
        experts(nc, ident, rows_in, rows_out, WGU, WD, EID, PSX)
        combine(nc, X, rows_out, ROW, out)


def route(nc, X, ident, gate_w, shared, routed, rows_in, WGU, WD, EID, ROW, PSX):
    with ExitStack() as ctx:
        def sb(name, shape, dt=F32):
            return ctx.enter_context(nc.sbuf_tensor(name, shape, dt))

        def sem(name):
            return ctx.enter_context(nc.semaphore(name))

        RAW = sb("RAW", [P, 3, 1024])
        ZERO = sb("ZERO", [P, D])
        ZN = sb("ZN", [P, SEQS, D])
        XS = sb("XSC", [P, SEQS, D])
        ZG = sb("ZG", [P, 2, KD, TOK])
        GW = sb("GW", [E, D])
        GT = sb("GT", [P, KD, E])
        ST = sb("RST", [P, SEQS, 6])
        MV = sb("RMV", [P, SEQS, 2])
        RSTD = sb("RRSTD", [P, SEQS])
        HALF = sb("RHALF", [P, SEQS])
        BEFORE = sb("BEFORE", [P, P])
        ONES = sb("RONES", [P, P])
        IOTE = sb("IOTE", [P, SEQS, E])
        IOT128 = sb("IOT128", [P, E, SEQS])
        IOTU = sb("IOTU", [P, RT, E])
        LG = sb("LG", [P, SEQS, E])
        MXL = sb("MXL", [P, SEQS])
        SC = sb("SC", [P, SEQS])
        PICK = sb("PICK", [P, SEQS, E])
        IDX = sb("IDX", [P, SEQS])
        OH = sb("OH", [P, SEQS, E])
        TOTS = sb("TOTS", [P, SEQS, E])
        BASE = sb("BASE", [P, SEQS + 1, E])
        MORE = sb("MORE", [P, E, SEQS])
        NT = sb("NT", [P, E])
        START = sb("START", [P, E + 1])
        PAST = sb("PAST", [P, RT, E])
        EIDF = sb("EIDF", [P, RT])
        RB = sb("RB", [P, E])
        POS = sb("POS", [P, SEQS, E])
        POSF = sb("POSF", [P, SEQS])

        raw_in = [sem(f"raw_in{i}") for i in range(3)]
        gw_in, zeroed, zn_out, scattered = (sem(n) for n in ("gw_in", "zeroed", "zn_out", "scattered"))
        consts, zero_set, before_set, v0, r0 = (sem(n) for n in ("rconsts", "zero_set", "before_set", "rv0", "rr0"))
        gt_mm, zt_mm, lg_mm, pre_mm = (sem(n) for n in ("gt_mm", "rzt_mm", "lg_mm", "pre_mm"))
        w_mm = [sem(f"w_mm{i}") for i in range(3)]
        w_sb = [sem(f"w_sb{i}") for i in range(3)]
        gt, zg, sc = (sem(n) for n in ("gt", "zg", "sc"))
        prep, zn, step, xs, oh, row, mxl = (sem(n) for n in ("rprep", "rzn", "rstep", "rxs", "roh", "rrow", "rmxl"))
        block = ctx.enter_context(nc.Block())

        @block.sync
        def _(sp):
            def load(k, mats):
                for i, w in enumerate(mats):
                    if not (type(k) is int and k == 0):
                        sp.wait_ge(w_mm[i], k)
                    sp.dma_start(RAW[:, i, :].rearrange("p (c n) -> p c n", n=w.shape[1]),
                                 w.rearrange("(c p) n -> p c n", p=P)).then_inc(raw_in[i], 16)

            sp.dma_start(GW[:, :], gate_w).then_inc(gw_in, 16)
            load(0, shared)
            sp.wait_ge(zero_set, 1)
            sp.dma_start(rows_in[SEQS * P:ROWS, :].rearrange("(u p) d -> p u d", p=P),
                         bcast(ZERO[:, :], RT)).then_inc(zeroed, 16)
            sp.wait_ge(zn, TILES)
            sp.dma_start(rows_in[0:SEQS * P, :].rearrange("(b p) d -> p b d", p=P), ZN[:, :, :]).then_inc(zn_out, 16)
            with sp.Fori(0, E, 1) as e:
                load(e + 1, [w[e, :, :] for w in routed])
            sp.wait_ge(zeroed, 16)
            sp.wait_ge(zn_out, 16)

        @block.gpsimd
        def _(pool):
            nc.gpsimd.memset(ZERO[:, :], 0.0).then_inc(zero_set, 1)
            nc.gpsimd.memset(HALF[:, :], -0.5)
            nc.gpsimd.memset(ONES[:, :], 1.0)
            nc.gpsimd.memset(BASE[:, 0, :], 0.0)
            nc.gpsimd.memset(START[:, 0:1], 0.0)
            nc.gpsimd.memset(EID[:, 0:SEQS], SHARED)
            nc.gpsimd.iota(IOTE[:, :, :], pattern=[[0, SEQS], [1, E]], base=0, channel_multiplier=0,
                           allow_small_or_imprecise_dtypes=True)
            nc.gpsimd.iota(IOT128[:, :, :], pattern=[[0, E], [P, SEQS]], base=0, channel_multiplier=0,
                           allow_small_or_imprecise_dtypes=True)
            nc.gpsimd.iota(IOTU[:, :, :], pattern=[[1, RT], [0, E]], base=0, channel_multiplier=0,
                           allow_small_or_imprecise_dtypes=True)
            nc.gpsimd.memset(BEFORE[:, :], 1.0).then_inc(consts, 1)
            pool.wait_ge(consts, 1)
            nc.gpsimd.affine_select(out=BEFORE[:, :], in_=BEFORE[:, :], compare_op=ALU.is_ge, fill=0.0, base=-1,
                                    pattern=[[1, P]], channel_multiplier=-1).then_inc(before_set, 1)
            pool.wait_ge(prep, 2)
            nc.gpsimd.tensor_scalar(RSTD[:, :], MV[:, :, 1], 1e-5, None, ALU.add).then_inc(v0, 1)
            pool.wait_ge(v0, 1)
            nc.gpsimd.tensor_tensor(RSTD[:, :], RSTD[:, :], HALF[:, :], ALU.pow).then_inc(r0, 1)
            pool.wait_ge(xs, 1)
            pool.wait_ge(row, 1)
            pool.wait_ge(zeroed, 16)
            for b in range(SEQS):
                pool.indirect_dma_start(out=rows_in[:, :], out_offset=bass.IndirectOffsetOnAxis(ROW[:, b:b + 1], 0),
                                        in_=XS[:, b, :], in_offset=None).then_inc(scattered, 16)
            pool.wait_ge(scattered, 16 * SEQS)

        def turned(i, out_chunks, in_chunks):
            return [(c, n, (n * in_chunks + c) * P) for n in range(out_chunks) for c in range(in_chunks)]

        @block.tensor
        def _(pe):
            def matrix(k, i):
                oc, icn = (KD, FC) if i < 2 else (FC, KD)
                pe.wait_ge(raw_in[i], 16 * k + 16)
                if not (type(k) is int and k == 0):
                    pe.wait_ge(w_sb[i], k)
                width = oc * P
                dst = PSX[:, 2 * i:2 * i + 2, :].rearrange("p b n -> p (b n)")
                for c, n, at in turned(i, oc, icn):
                    ins = nc.tensor.transpose(dst[:, at:at + P], RAW[:, i, c * width + n * P:c * width + (n + 1) * P],
                                              ident[:, :])
                ins.then_inc(w_mm[i], 1)

            pe.wait_ge(gw_in, 16)
            for kc in range(KD):
                ins = nc.tensor.transpose(PSX[:, 7, kc * E:(kc + 1) * E], GW[:, kc * P:(kc + 1) * P], ident[0:E, 0:E])
            ins.then_inc(gt_mm, 1)
            for q in range(TILES):
                pe.wait_ge(zn, q + 1)
                if q >= 2:
                    pe.wait_ge(zg, q - 1)
                for kc in range(KD):
                    for b in range(TS):
                        ins = nc.tensor.transpose(PSX[:, 2 * (q % 2) + kc, b * P:(b + 1) * P],
                                                  ZN[:, q * TS + b, kc * P:(kc + 1) * P], ident[:, :])
                ins.then_inc(zt_mm, 1)
                if q == 0:
                    pe.wait_ge(gt, 1)
                pe.wait_ge(zg, q + 1)
                for b in range(TS):
                    s = q * TS + b
                    for kc in range(KD):
                        ins = nc.tensor.matmul(PSX[:, 6, s * E:(s + 1) * E], ZG[:, q % 2, kc, b * P:(b + 1) * P],
                                               GT[:, kc, :], start=(kc == 0), stop=(kc == KD - 1))
            ins.then_inc(lg_mm, 1)
            for i in range(3):
                matrix(0, i)
            pe.wait_ge(before_set, 1)
            pe.wait_ge(oh, 1)
            ohs = OH[:, :, :].rearrange("p b e -> p (b e)")
            nc.tensor.matmul(PSX[:, 7, 0:P], BEFORE[:, :], ohs, start=True, stop=True)
            nc.tensor.matmul(PSX[:, 7, P:2 * P], ONES[:, :], ohs, start=True, stop=True).then_inc(pre_mm, 1)
            with pe.Fori(1, EA, 1) as k:
                for i in range(3):
                    matrix(k, i)

        @block.scalar
        def _(act):
            def matrix(k, place, i):
                act.wait_ge(w_mm[i], k + 1)
                src = PSX[:, 2 * i:2 * i + 2, :].rearrange("p b n -> p (b n)")
                dst = WGU[:, place, i, :, :].rearrange("p c n -> p (c n)") if i < 2 else \
                    WD[:, place, :, :].rearrange("p c n -> p (c n)")
                nc.scalar.copy(dst, src).then_inc(w_sb[i], 1)

            act.wait_ge(gt_mm, 1)
            nc.scalar.copy(GT[:, :, :], PSX[:, 7, 0:KD * E].rearrange("p (c e) -> p c e", c=KD)).then_inc(gt, 1)
            for q in range(TILES):
                act.wait_ge(zt_mm, q + 1)
                nc.scalar.copy(ZG[:, q % 2, :, :], PSX[:, 2 * (q % 2):2 * (q % 2) + 2, :]).then_inc(zg, 1)
            act.wait_ge(mxl, 1)
            nc.scalar.activation(SC[:, :], MXL[:, :], ACT.Sigmoid).then_inc(sc, 1)
            for i in range(3):
                matrix(0, SHARED, i)
            with act.Fori(0, E, 1) as e:
                for i in range(3):
                    matrix(e + 1, e, i)

        @block.vector
        def _(dve):
            for b in range(SEQS):
                ins = nc.vector.bn_stats(ST[:, b, :], X[:, b, :])
            ins.then_inc(prep, 1)
            dve.wait_ge(prep, 1)
            for b in range(SEQS):
                ins = nc.vector.bn_aggr(MV[:, b, :], ST[:, b, :])
            ins.then_inc(prep, 1)
            dve.wait_ge(r0, 1)
            dve.wait_ge(prep, 2)
            for q in range(TILES):
                for b in range(q * TS, (q + 1) * TS):
                    ins = nc.vector.tensor_scalar(ZN[:, b, :], X[:, b, :], MV[:, b, 0:1], RSTD[:, b:b + 1], ALU.subtract,
                                                  ALU.mult)
                ins.then_inc(zn, 1)
            steps = [0]

            def then(ins):
                steps[0] += 1
                ins.then_inc(step, 1)
                dve.wait_ge(step, steps[0])

            dve.wait_ge(consts, 1)
            dve.wait_ge(lg_mm, 1)
            then(nc.vector.tensor_copy(LG[:, :, :], PSX[:, 6, 0:P].rearrange("p (b e) -> p b e", e=E)))
            nc.vector.tensor_reduce(MXL[:, :], LG[:, :, :], AX.X, ALU.max).then_inc(mxl, 1)
            dve.wait_ge(mxl, 1)
            then(nc.vector.tensor_tensor(PICK[:, :, :], LG[:, :, :], spread(MXL[:, :], E), ALU.is_lt))
            then(nc.vector.scalar_tensor_tensor(PICK[:, :, :], PICK[:, :, :], float(E), IOTE[:, :, :], ALU.mult, ALU.add))
            then(nc.vector.tensor_reduce(IDX[:, :], PICK[:, :, :], AX.X, ALU.min))
            nc.vector.tensor_tensor(OH[:, :, :], IOTE[:, :, :], spread(IDX[:, :], E), ALU.is_equal).then_inc(oh, 1)
            dve.wait_ge(sc, 1)
            dve.wait_ge(zn, TILES)
            for b in range(SEQS):
                ins = nc.vector.tensor_scalar(XS[:, b, :], ZN[:, b, :], SC[:, b:b + 1], None, ALU.mult)
            ins.then_inc(xs, 1)
            dve.wait_ge(pre_mm, 1)
            then(nc.vector.tensor_copy(TOTS[:, :, :], PSX[:, 7, P:2 * P].rearrange("p (b e) -> p b e", e=E)))
            for b in range(SEQS):
                then(nc.vector.tensor_tensor(BASE[:, b + 1, :], BASE[:, b, :], TOTS[:, b, :], ALU.add))
            then(nc.vector.tensor_tensor(MORE[:, :, :], spread(BASE[:, SEQS, :], SEQS), IOT128[:, :, :], ALU.is_gt))
            then(nc.vector.tensor_reduce(NT[:, :], MORE[:, :, :], AX.X, ALU.add))
            for e in range(E):
                then(nc.vector.tensor_tensor(START[:, e + 1:e + 2], START[:, e:e + 1], NT[:, e:e + 1], ALU.add))
            then(nc.vector.tensor_tensor(PAST[:, :, :], bcast(START[:, 1:E + 1], RT), IOTU[:, :, :], ALU.is_le))
            then(nc.vector.tensor_reduce(EIDF[:, :], PAST[:, :, :], AX.X, ALU.add))
            then(nc.vector.tensor_scalar(EID[:, SEQS:UNITS], EIDF[:, :], float(E - 1), None, ALU.min))
            then(nc.vector.tensor_scalar(RB[:, :], START[:, 0:E], float(P), float(SEQS * P), ALU.mult, ALU.add))
            then(nc.vector.tensor_tensor(POS[:, :, :], BASE[:, 0:SEQS, :], bcast(RB[:, :], SEQS), ALU.add))
            then(nc.vector.tensor_tensor(POS[:, :, :], POS[:, :, :], PSX[:, 7, 0:P].rearrange("p (b e) -> p b e", e=E),
                                         ALU.add))
            dve.wait_ge(oh, 1)
            then(nc.vector.tensor_tensor(POS[:, :, :], POS[:, :, :], OH[:, :, :], ALU.mult))
            then(nc.vector.tensor_reduce(POSF[:, :], POS[:, :, :], AX.X, ALU.add))
            nc.vector.tensor_copy(ROW[:, :], POSF[:, :]).then_inc(row, 1)


def experts(nc, ident, rows_in, rows_out, WGU, WD, EID, PSX):
    with ExitStack() as ctx:
        def sb(name, shape, dt=F32):
            return ctx.enter_context(nc.sbuf_tensor(name, shape, dt))

        def sem(name):
            return ctx.enter_context(nc.semaphore(name))

        XU = sb("XU", [P, 2, D])
        XTU = sb("XTU", [P, 2, KD, P])
        SG = sb("SG", [P, 2, FF])
        AC = sb("AC", [P, 2, FF])
        AT = sb("AT", [P, 2, FC, P])
        OU = sb("OU", [P, 2, D])
        xu_in = [sem(f"xu_in{j}") for j in range(2)]
        stored = [sem(f"stored{j}") for j in range(2)]
        xt_mm, g_mm, u_mm, at_mm, o_mm = (sem(n) for n in ("uxt_mm", "g_mm", "u_mm", "at_mm", "o_mm"))
        xt, sg, ac, at, ou = (sem(n) for n in ("uxt", "sg", "ac", "at", "ou"))
        HALVES = UNITS // 2
        block = ctx.enter_context(nc.Block())

        @block.sync
        def _(sp):
            def load(i, j):
                u = 2 * i + j
                if not (type(i) is int and i == 0):
                    sp.wait_ge(xt_mm, u - 1)
                sp.dma_start(XU[:, j, :], rows_in[bass.ds(u * P, P), :]).then_inc(xu_in[j], 16)

            for j in range(2):
                load(0, j)
            with sp.Fori(1, HALVES, 1) as i:
                for j in range(2):
                    load(i, j)

        @block.gpsimd
        def _(pool):
            with pool.Fori(0, HALVES, 1) as i:
                for j in range(2):
                    u = 2 * i + j
                    pool.wait_ge(ou, u + 1)
                    pool.dma_start(rows_out[bass.ds(u * P, P), :], OU[:, j, :]).then_inc(stored[j], 16)
            for j in range(2):
                pool.wait_ge(stored[j], 16 * HALVES)

        @block.tensor
        def _(pe):
            def turn_input(i, j):
                u = 2 * i + j
                pe.wait_ge(xu_in[j], 16 * i + 16)
                if not (type(i) is int and u == 0):
                    pe.wait_ge(xt, u)
                for kc in range(KD):
                    ins = nc.tensor.transpose(PSX[:, 6, kc * P:(kc + 1) * P], XU[:, j, kc * P:(kc + 1) * P], ident[:, :])
                ins.then_inc(xt_mm, 1)

            def gate_up(i, j):
                u = 2 * i + j
                e = nc.tensor.value_load(EID[0:1, bass.ds(u, 1)], min_val=0, max_val=E)
                pe.wait_ge(xt, u + 1)
                for m, done in enumerate((g_mm, u_mm)):
                    if not (type(i) is int and i == 0):
                        pe.wait_ge((sg, ac)[m], u - 1)
                    for kc in range(KD):
                        ins = nc.tensor.matmul(PSX[:, 2 * m + j, :], XTU[:, j, kc, :], WGU[:, e, m, kc, :],
                                               start=(kc == 0), stop=(kc == KD - 1))
                    ins.then_inc(done, 1)

            def turn_hidden(i, j):
                u = 2 * i + j
                pe.wait_ge(ac, u + 1)
                if not (type(i) is int and u == 0):
                    pe.wait_ge(at, u)
                for c in range(FC):
                    ins = nc.tensor.transpose(PSX[:, 4, c * P:(c + 1) * P], AC[:, j, c * P:(c + 1) * P], ident[:, :])
                ins.then_inc(at_mm, 1)

            def down(i, j):
                u = 2 * i + j
                e = nc.tensor.value_load(EID[0:1, bass.ds(u, 1)], min_val=0, max_val=E)
                pe.wait_ge(at, u + 1)
                if not (type(i) is int and i == 0):
                    pe.wait_ge(ou, u - 1)
                for c in range(FC):
                    ins = nc.tensor.matmul(PSX[:, 5 + 2 * j, 0:D], AT[:, j, c, :], WD[:, e, c, :], start=(c == 0),
                                           stop=(c == FC - 1))
                ins.then_inc(o_mm, 1)

            def pair(i, more):
                turn_hidden(i, 0)
                gate_up(i, 1)
                if more:
                    turn_input(i + 1, 0)
                down(i, 0)
                turn_hidden(i, 1)
                if more:
                    gate_up(i + 1, 0)
                    turn_input(i + 1, 1)
                down(i, 1)

            turn_input(0, 0)
            turn_input(0, 1)
            gate_up(0, 0)
            pair(0, True)
            with pe.Fori(1, HALVES - 1, 1) as i:
                pair(i, True)
            pair(HALVES - 1, False)

        @block.scalar
        def _(act):
            def evac_input(i, j):
                act.wait_ge(xt_mm, 2 * i + (j + 1))
                nc.scalar.copy(XTU[:, j, :, :], PSX[:, 6, 0:D].rearrange("p (c t) -> p c t", c=KD)).then_inc(xt, 1)

            def silu(i, j):
                u = 2 * i + j
                act.wait_ge(g_mm, u + 1)
                nc.scalar.activation(SG[:, j, :], PSX[:, j, :], ACT.Silu).then_inc(sg, 1)

            def evac_hidden(i, j):
                act.wait_ge(at_mm, 2 * i + (j + 1))
                nc.scalar.copy(AT[:, j, :, :], PSX[:, 4, :].rearrange("p (c t) -> p c t", c=FC)).then_inc(at, 1)

            def pair(i, more):
                evac_hidden(i, 0)
                silu(i, 1)
                if more:
                    evac_input(i + 1, 0)
                evac_hidden(i, 1)
                if more:
                    silu(i + 1, 0)
                    evac_input(i + 1, 1)

            evac_input(0, 0)
            evac_input(0, 1)
            silu(0, 0)
            with act.Fori(0, HALVES - 1, 1) as i:
                pair(i, True)
            pair(HALVES - 1, False)

        @block.vector
        def _(dve):
            def product(i, j):
                u = 2 * i + j
                dve.wait_ge(sg, u + 1)
                dve.wait_ge(u_mm, u + 1)
                nc.vector.tensor_tensor(AC[:, j, :], SG[:, j, :], PSX[:, 2 + j, :], ALU.mult).then_inc(ac, 1)

            def result(i, j, first):
                u = 2 * i + j
                dve.wait_ge(o_mm, u + 1)
                if not first:
                    dve.wait_ge(stored[j], 16 * i)
                nc.vector.tensor_copy(OU[:, j, :], PSX[:, 5 + 2 * j, 0:D]).then_inc(ou, 1)

            def pair(i, first, more):
                product(i, 1)
                result(i, 0, first)
                if more:
                    product(i + 1, 0)
                result(i, 1, first)

            product(0, 0)
            pair(0, True, True)
            with dve.Fori(1, HALVES - 1, 1) as i:
                pair(i, False, True)
            pair(HALVES - 1, False, False)


def combine(nc, X, rows_out, ROW, out):
    with ExitStack() as ctx:
        def sem(name):
            return ctx.enter_context(nc.semaphore(name))

        SH = ctx.enter_context(nc.sbuf_tensor("SH", [P, SEQS, D], F32))
        RO = ctx.enter_context(nc.sbuf_tensor("RO", [P, SEQS, D], F32))
        sh_in = sem("sh_in")
        ro_in = [sem(f"ro_in{h}") for h in range(2)]
        added, ready, written = sem("added"), sem("ready"), sem("written")
        block = ctx.enter_context(nc.Block())

        @block.sync
        def _(sp):
            sp.dma_start(SH[:, :, :], rows_out[0:SEQS * P, :].rearrange("(b p) d -> p b d", p=P)).then_inc(sh_in, 16)
            for t in range(TILES):
                sp.wait_ge(ready, t + 1)
                sp.dma_start(out[t * TS:(t + 1) * TS, :, :].rearrange("b s d -> s b d"),
                             X[:, t * TS:(t + 1) * TS, :]).then_inc(written, 16)
            sp.wait_ge(written, 16 * TILES)

        @block.gpsimd
        def _(pool):
            for b in range(SEQS):
                pool.indirect_dma_start(out=RO[:, b, :], out_offset=None, in_=rows_out[:, :],
                                        in_offset=bass.IndirectOffsetOnAxis(ROW[:, b:b + 1], 0)
                                        ).then_inc(ro_in[b // (SEQS // 2)], 16)

        @block.vector
        def _(dve):
            dve.wait_ge(sh_in, 16)
            nc.vector.tensor_tensor(X[:, :, :], X[:, :, :], SH[:, :, :], ALU.add).then_inc(added, 1)
            dve.wait_ge(added, 1)
            for t in range(TILES):
                bs = slice(t * TS, (t + 1) * TS)
                dve.wait_ge(ro_in[t // 2], 16 * SEQS // 2)
                nc.vector.tensor_tensor(X[:, bs, :], X[:, bs, :], RO[:, bs, :], ALU.add).then_inc(ready, 1)


def decoder(nc, a, out):
    with ExitStack() as ctx:
        X = ctx.enter_context(nc.sbuf_tensor("X", [P, SEQS, D], F32))
        ident = ctx.enter_context(nc.sbuf_tensor("ident", [P, P], F32))
        ident_set = ctx.enter_context(nc.semaphore("ident_set"))
        with nc.Block() as block:
            @block.gpsimd
            def _(pool):
                nc.gpsimd.memset(ident[:, :], 0.0).then_inc(ident_set, 1)
                pool.wait_ge(ident_set, 1)
                nc.gpsimd.affine_select(out=ident[:, :], in_=ident[:, :], compare_op=ALU.not_equal, fill=1.0, base=0,
                                        pattern=[[-1, P]], channel_multiplier=1).then_inc(ident_set, 1)
                pool.wait_ge(ident_set, 2)
        attention_stack(nc, X, ident, a["x"], *(a["L0_attn_" + n] for n in (
            "Wq", "bq", "Wk", "bk", "Wv", "bv", "Wo", "bo", "ln1_s", "ln1_b", "W1", "b1", "W2", "b2", "ln2_s", "ln2_b")))
        cross_attention(nc, X, ident, a["x"], a["ctx_512"], *(a["L0_xattn_" + n] for n in (
            "Wq", "bq", "Wk", "bk", "Wv", "bv", "Wo", "bo")))
        mixture(nc, X, ident, out, a["L0_ffn_gate_w"], [a["L0_ffn_shared_" + n] for n in ("gate", "up", "down")],
                [a["L0_ffn_r_" + n] for n in ("gate", "up", "down")])


def kernel(**inputs):
    import numpy as np
    from concourse import bacc
    from concourse.bass_utils import run_bass_kernel_spmd

    nc = bacc.Bacc("TRN2", target_bir_lowering=False, num_devices=1)
    arrays = {name: np.ascontiguousarray(a) for name, a in inputs.items()}
    aps = {name: nc.dram_tensor(name, a.shape, mybir.dt.from_np(a.dtype), kind="ExternalInput").ap()
           for name, a in arrays.items()}
    out = nc.dram_tensor("out", (SEQS, SEQ, D), F32, kind="ExternalOutput").ap()
    decoder(nc, aps, out)
    return run_bass_kernel_spmd(nc, [arrays], core_ids=[0]).results[0]["out"]
```

```python
from contextlib import ExitStack

import concourse.bass as bass
from concourse import mybir

F32 = mybir.dt.float32
F32R = mybir.dt.float32r
U32 = mybir.dt.uint32
I32 = mybir.dt.int32
ALU = mybir.AluOpType
ACT = mybir.ActivationFunctionType
AX = mybir.AxisListType

P = 128
SEQS, SEQ, D = 16, 128, 256
KD = D // P
LAYERS, HEADS, HK, F = 8, 16, 64, 1024
HC = F // P
TS = 4
TOK = TS * SEQ
TILES = SEQS // TS
LAST = LAYERS * TILES
EPS_ATT = 1e-6
TINY = 1e-24
PIECES = HC + HC // 2
RING = 3
IRING = 4
PIECE = 3 * KD * P


def bcast(ap, n):
    return ap.unsqueeze(1).to_broadcast([ap.shape[0], n, ap.shape[1]])


def spread(ap, w):
    return ap.unsqueeze(2).to_broadcast([ap.shape[0], ap.shape[1], w])


def slot_of(l, t):
    return l + t // TILES, t % TILES


def exists(l, t):
    return type(l) is not int or l * TILES + t < LAST


def attention_stack(nc, X, ident, x, Wq, bq, Wk, bk, Wv, bv, Wo, bo, s1, c1, W1, b1, W2, b2, s2, c2):
    with ExitStack() as ctx:
        def sb(name, shape, dt=F32):
            return ctx.enter_context(nc.sbuf_tensor(name, shape, dt))

        def sem(name):
            return ctx.enter_context(nc.semaphore(name))

        WHI = sb("WHI", [P, HC, 3, KD, P], F32R)
        WLO = sb("WLO", [P, HC, 3, KD, P], F32R)
        W1HI = sb("W1HI", [P, HC, KD, P], F32R)
        W1LO = sb("W1LO", [P, HC, KD, P], F32R)
        WO = sb("WO", [P, HC, D])
        W2S = sb("W2S", [P, HC, D])
        STAGE = sb("STAGE", [P, RING, PIECE])
        BA = sb("BA", [P, 3, HC])
        BNEG = sb("BNEG", [P, 3, HC])
        BO = sb("BO", [P, KD])
        B1 = sb("B1", [P, HC])
        B2 = sb("B2", [P, KD])
        LN1P = sb("LN1P", [P, 2, D])
        LN2P = sb("LN2P", [P, 2, D])
        XTHI = sb("XTHI", [P, 2, KD, TOK], F32R)
        XTLO = sb("XTLO", [P, 2, KD, TOK], F32R)
        X1HI = sb("X1HI", [P, KD, TOK], F32R)
        X1LO = sb("X1LO", [P, KD, TOK], F32R)
        ATT = sb("ATT", [P, HC, TOK])
        H = sb("H", [P, HC, TOK])
        EK = sb("EK", [P, 2, TOK])
        RK = sb("RK", [P, 2, TOK])
        EQ = sb("EQ", [P, IRING, TOK])
        RQ = sb("RQ", [P, 2, TOK])
        INV = sb("INV", [P, IRING, TOK])
        T = sb("T", [P, KD, TOK])
        R = sb("R", [P, 2, TS, D])
        SUMK = sb("SUMK", [P, 2, TS])
        KVS = sb("KVS", [P, 2, TS])
        RSK = sb("RSK", [P, 2, TS])
        CC = sb("CC", [P, IRING, TS])
        ES = sb("ES", [P, 2, TS])
        CE = sb("CE", [P, IRING, TS])
        ST = sb("ST", [P, TS, 6])
        MV = sb("MV", [P, 2, TS, 2])
        RSTD = sb("RSTD", [P, 2, TS])
        ST0 = sb("ST0", [P, SEQS, 6])
        MV0 = sb("MV0", [P, SEQS, 2])
        RSTD0 = sb("RSTD0", [P, SEQS])
        HALF = sb("HALF", [P, SEQS])
        EPS0 = sb("EPS0", [P, TS])
        EPS1 = sb("EPS1", [P, TS])
        ONE = sb("ONE", [P, 1])
        CARRY = sb("CARRY", [P, 1])
        PS = ctx.enter_context(nc.psum_tensor("PS", [P, 6, TOK], F32))
        Y = ctx.enter_context(nc.psum_tensor("Y", [P, 2 * TOK], F32))
        Yfm = Y[:, :].rearrange("p (m t) -> p m t", m=KD)
        Ytm = Y[:, :].rearrange("p (b d) -> p b d", b=TS)

        x_in = [sem(f"x_in{t}") for t in range(TILES // 2)]
        staged = [sem(f"staged{s}") for s in range(RING)]
        ba_in = [sem(f"ba_in{h}") for h in range(2)]
        bo_in, b1_in, b2_in, wo_in, w2_in, ln1_in, ln2_in = (
            sem(n) for n in ("bo_in", "b1_in", "b2_in", "wo_in", "w2_in", "ln1_in", "ln2_in"))
        k_mm, v_mm, q_mm, y_mm, yt_mm, x1t_mm, h_mm, z_mm, zt_mm, xt_mm = (
            sem(n) for n in ("k_mm", "v_mm", "q_mm", "y_mm", "yt_mm", "x1t_mm", "h_mm", "z_mm", "zt_mm", "xt_mm"))
        b_neg, nk, ek, rk, nq, eq, rq, y_act, x1_hi, h_act, z_act, xt_hi, log, inv = (
            sem(n) for n in ("b_neg", "nk", "ek", "rk", "nq", "eq", "rq", "y_act", "x1_hi", "h_act", "z_act", "xt_hi",
                             "log", "inv"))
        k_exp, k_sum, kv_sum, stat, q_exp, denom, residue, recip, xt_lo, x1_lo = (
            sem(n) for n in ("k_exp", "k_sum", "kv_sum", "stat", "q_exp", "denom", "residue", "recip", "xt_lo", "x1_lo"))
        res1, st1, mv1, n1, x1, res2, st2, mv2, n2, mv0 = (
            sem(n) for n in ("res1", "st1", "mv1", "n1", "x1", "res2", "st2", "mv2", "n2", "mv0"))
        half_set, att_s, att, w_hi, w_lo, r1, r2, xn_s, xn, r0 = (
            sem(n) for n in ("half_set", "att_s", "att", "w_hi", "w_lo", "r1", "r2", "xn_s", "xn", "r0"))

        def piece_incs(k):
            return 16 * (3 * KD if k < HC else 2)

        per_layer = [sum(piece_incs(k) for k in range(s, PIECES, RING)) for s in range(RING)]

        def staged_value(layer, k):
            return layer * per_layer[k % RING] + sum(piece_incs(j) for j in range(k % RING, k + 1, RING))

        block = ctx.enter_context(nc.Block())

        @block.sync
        def _(sp):
            def load_piece(layer, k, first):
                if not (first and k < RING):
                    sp.wait_ge(w_lo, layer * PIECES + (k - RING + 1))
                s = k % RING
                if k < HC:
                    for m, w in enumerate((Wk, Wv, Wq)):
                        dst = STAGE[:, s, m * KD * P:(m + 1) * KD * P]
                        for kc in range(KD):
                            src = w[layer, 2 * k:2 * k + 2, kc * P:(kc + 1) * P, :].rearrange("h p k -> p h k")
                            sp.dma_start(dst[:, kc * P:(kc + 1) * P].rearrange("p (h k) -> p h k", h=2),
                                         src).then_inc(staged[s], 16)
                else:
                    j = k - HC
                    for i in range(2):
                        m = 2 * j + i
                        sp.dma_start(STAGE[:, s, i * KD * P:(i + 1) * KD * P].rearrange("p (c n) -> p c n", c=KD),
                                     W1[layer, :, m * P:(m + 1) * P].rearrange("(c p) n -> p c n", p=P)
                                     ).then_inc(staged[s], 16)

            def load_ba(layer, half):
                cs = slice(half * HC // 2, (half + 1) * HC // 2)
                for m, b in enumerate((bk, bv, bq)):
                    src = b[layer, half * HEADS // 2:(half + 1) * HEADS // 2, :].rearrange("(c h) k -> (h k) c", h=2)
                    sp.dma_start(BA[:, m, cs], src, allow_slow_non_contiguous=True).then_inc(ba_in[half], 16)

            def load_ln(dst, scale, bias, layer, done):
                sp.dma_start(dst[:, 0, :], scale[bass.ds(layer, 1), :].to_broadcast([P, D])).then_inc(done, 16)
                sp.dma_start(dst[:, 1, :], bias[bass.ds(layer, 1), :].to_broadcast([P, D])).then_inc(done, 16)

            def load_fm(dst, b, layer, done):
                sp.dma_start(dst[:, :], b[layer, :].rearrange("(c p) -> p c", p=P),
                             allow_slow_non_contiguous=True).then_inc(done, 16)

            def load_wide(dst, w, layer, done):
                sp.dma_start(dst[:, :, :], w[layer, :, :].rearrange("(c p) n -> p c n", p=P)).then_inc(done, 16)

            def layer_loads(l):
                n = (l * TILES + TILES - 1) * HC
                for k in range(HC):
                    load_piece(l + 1, k, False)
                    if k % 4 == 3:
                        sp.wait_ge(rq, n + k + 1)
                        sp.wait_ge(kv_sum, n + k + 1)
                        load_ba(l + 1, k // 4)
                g = l * TILES + TILES
                sp.wait_ge(y_mm, g)
                load_wide(WO, Wo, l + 1, wo_in)
                sp.wait_ge(y_act, g)
                load_fm(BO, bo, l + 1, bo_in)
                sp.wait_ge(x1, g)
                load_ln(LN1P, s1, c1, l + 1, ln1_in)
                for k in range(HC, PIECES):
                    load_piece(l + 1, k, False)
                sp.wait_ge(h_act, g * HC)
                load_fm(B1, b1, l + 1, b1_in)
                sp.wait_ge(z_mm, g)
                load_wide(W2S, W2, l + 1, w2_in)
                sp.wait_ge(z_act, g)
                load_fm(B2, b2, l + 1, b2_in)
                sp.wait_ge(xn, g + TILES)
                load_ln(LN2P, s2, c2, l + 1, ln2_in)

            for t in range(TILES):
                sp.dma_start(X[:, t * TS:(t + 1) * TS, :],
                             x[t * TS:(t + 1) * TS, :, :].rearrange("b s d -> s b d")).then_inc(x_in[t // 2], 16)
                if t == 0:
                    load_piece(0, 0, True)
                if t == 1:
                    load_ba(0, 0)
                    load_piece(0, 1, True)
            load_piece(0, 2, True)
            load_ba(0, 1)
            for k in range(RING, HC):
                load_piece(0, k, True)
            load_wide(WO, Wo, 0, wo_in)
            load_fm(BO, bo, 0, bo_in)
            load_ln(LN1P, s1, c1, 0, ln1_in)
            load_fm(B1, b1, 0, b1_in)
            load_wide(W2S, W2, 0, w2_in)
            load_fm(B2, b2, 0, b2_in)
            load_ln(LN2P, s2, c2, 0, ln2_in)
            for k in range(HC, PIECES):
                load_piece(0, k, True)
            with sp.Fori(0, LAYERS - 1, 1) as l:
                layer_loads(l)

        @block.gpsimd
        def _(pool):
            def split_piece(layer, k, first):
                s = k % RING
                pool.wait_ge(staged[s], staged_value(layer, k))
                if k < HC:
                    hi, lo = (w[:, k, :, :, :].rearrange("p m c n -> p (m c n)") for w in (WHI, WLO))
                    if not first:
                        pool.wait_ge(q_mm, layer * TILES * HC + (k + 1 - HC))
                    src = STAGE[:, s, :]
                else:
                    m = 2 * (k - HC)
                    hi, lo = (w[:, m:m + 2, :, :].rearrange("p m c n -> p (m c n)") for w in (W1HI, W1LO))
                    if not first:
                        pool.wait_ge(h_mm, layer * TILES * HC + (m + 2 - HC))
                    src = STAGE[:, s, 0:2 * KD * P]
                nc.gpsimd.tensor_tensor(hi, src, ONE[:, :].to_broadcast(src.shape), ALU.mult).then_inc(w_hi, 1)
                pool.wait_ge(w_hi, layer * PIECES + (k + 1))
                nc.gpsimd.tensor_tensor(lo, src, hi.bitcast(F32), ALU.subtract).then_inc(w_lo, 1)

            def rstd(out, var, eps, var_sem, var_value, done, value):
                pool.wait_ge(var_sem, var_value)
                nc.gpsimd.tensor_tensor(out, var, eps[:, 0:out.shape[1]], ALU.add).then_inc(done, 1)
                pool.wait_ge(done, 2 * value - 1)
                nc.gpsimd.tensor_tensor(out, out, HALF[:, 0:out.shape[1]], ALU.pow).then_inc(done, 1)

            nc.gpsimd.memset(ONE[:, :], 1.0)
            nc.gpsimd.memset(EPS0[:, :], 1e-5)
            nc.gpsimd.memset(EPS1[:, :], 1e-6)
            nc.gpsimd.memset(HALF[:, :], -0.5).then_inc(half_set, 1)
            pool.wait_ge(half_set, 1)

            def norm_input(t):
                bs = slice(t * TS, (t + 1) * TS)
                rstd(RSTD0[:, bs], MV0[:, bs, 1], EPS0, mv0, 2 * t + 2, r0, t + 1)
                pool.wait_ge(r0, 2 * t + 2)
                for b in range(t * TS, (t + 1) * TS):
                    last = nc.gpsimd.tensor_scalar(X[:, b, :], X[:, b, :], MV0[:, b, 0:1], RSTD0[:, b:b + 1],
                                                   ALU.subtract, ALU.mult)
                last.then_inc(xn, 1)

            def attend(l, t, c):
                g, e = l * TILES + t, c % IRING
                n = g * HC + c
                pool.wait_ge(recip, n + 1)
                pool.wait_ge(stat, n * 5 + 5)
                r3 = INV[:, e, :].rearrange("p (b s) -> p b s", b=TS)
                nc.gpsimd.tensor_tensor(r3, r3, spread(CE[:, e, :], SEQ), ALU.mult).then_inc(att_s, 1)
                pool.wait_ge(att_s, n + 1)
                if c == 0 and not (type(g) is int and g == 0):
                    pool.wait_ge(y_mm, g)
                nc.gpsimd.tensor_tensor(ATT[:, c, :].rearrange("p (b s) -> p b s", b=TS), r3,
                                        spread(CC[:, e, :], SEQ), ALU.add).then_inc(att, 1)

            def slot(l, t, first=False, load=True):
                g = l * TILES + t
                tile = exists(l, t)
                nl, nt = slot_of(l, t + 1)
                more = exists(l, t + 1)
                splits = load and t == TILES - 2
                splits_w1 = load and t == TILES
                if splits:
                    split_piece(l + 1, 0, False)
                for c in range(1, HC):
                    if splits:
                        split_piece(l + 1, c, False)
                    if c == 3 and tile:
                        rstd(RSTD[:, 0, :], MV[:, 0, :, 1], EPS1, mv1, g + 1, r1, g + 1)
                    if c == 6 and not first:
                        rstd(RSTD[:, 1, :], MV[:, 1, :, 1], EPS1, mv2, g, r2, g)
                    if more:
                        attend(nl, nt, c - 1)
                    if splits_w1 and 2 <= c < 2 + PIECES - HC:
                        split_piece(l + 1, HC + c - 2, False)
                    if c == 6 and not first:
                        wl, w = slot_of(l, t - 1)
                        rw = R[:, w % 2, :, :]
                        pool.wait_ge(n2, g)
                        pool.wait_ge(ln2_in, (wl + 1) * 32)
                        nc.gpsimd.tensor_tensor(rw, rw, bcast(LN2P[:, 0, :], TS), ALU.mult).then_inc(xn_s, 1)
                        pool.wait_ge(xn_s, g)
                        nc.gpsimd.tensor_tensor(X[:, w * TS:(w + 1) * TS, :], rw, bcast(LN2P[:, 1, :], TS),
                                                ALU.add).then_inc(xn, 1)
                if more:
                    attend(nl, nt, HC - 1)

            split_piece(0, 0, True)
            norm_input(0)
            split_piece(0, 1, True)
            norm_input(1)
            for c in range(HC):
                if c + 2 < HC:
                    split_piece(0, c + 2, True)
                if c in (1, 3):
                    norm_input(2 + c // 2)
                attend(0, 0, c)
            for k in range(HC, PIECES):
                split_piece(0, k, True)
            slot(0, 0, first=True)
            with pool.Fori(0, LAYERS - 1, 1) as l:
                for t in range(1, TILES + 1):
                    slot(l, t)
            for t in range(1, TILES + 1):
                slot(LAYERS - 1, t, load=False)

        @block.tensor
        def _(pe):
            def split_product(out, whi, wlo, xhi, xlo):
                for kc in range(KD):
                    nc.tensor.matmul(out, whi[:, kc, :], xhi[:, kc, :], start=(kc == 0), stop=False)
                    nc.tensor.matmul(out, whi[:, kc, :], xlo[:, kc, :], start=False, stop=False)
                    ins = nc.tensor.matmul(out, wlo[:, kc, :], xhi[:, kc, :], start=False, stop=(kc == KD - 1))
                return ins

            def project(l, t, c, free, which=(0, 1, 2)):
                g = l * TILES + t
                if c == 0:
                    pe.wait_ge(xt_hi, g + 1)
                    pe.wait_ge(xt_lo, g + 1)
                if t == 0:
                    pe.wait_ge(w_lo, l * PIECES + (c + 1))
                for m in which:
                    done = (k_mm, v_mm, q_mm)[m]
                    for s, value in free[m:m + 1]:
                        pe.wait_ge(s, value)
                    split_product(PS[:, 3 * (c % 2) + m, :], WHI[:, c, m], WLO[:, c, m],
                                  XTHI[:, t % 2], XTLO[:, t % 2]).then_inc(done, 1)

            def after_chunk(n):
                return [(rk, n - 1), (kv_sum, n - 1), (rq, n - 1)]

            def input_fm(j, t):
                pe.wait_ge(xn, j + 1)
                for kc in range(KD):
                    for b in range(TS):
                        ins = nc.tensor.transpose(Yfm[:, kc, b * P:(b + 1) * P],
                                                  X[:, t * TS + b, kc * P:(kc + 1) * P], ident[:, :])
                ins.then_inc(xt_mm, 1)

            def to_tm(done, value, transposed):
                pe.wait_ge(done, value)
                for b in range(TS):
                    for kc in range(KD):
                        ins = nc.tensor.transpose(Ytm[:, b, kc * P:(kc + 1) * P], T[:, kc, b * P:(b + 1) * P],
                                                  ident[:, :])
                ins.then_inc(transposed, 1)

            def down(w, src, m):
                for c in range(HC):
                    ins = nc.tensor.matmul(Yfm[:, m, :], w[:, c, m * P:(m + 1) * P], src[:, c, :],
                                           start=(c == 0), stop=(c == HC - 1))
                return ins

            def hidden(l, t, g):
                if t == 0:
                    pe.wait_ge(w_lo, (l + 1) * PIECES)
                pe.wait_ge(x1_hi, g + 1)
                pe.wait_ge(x1_lo, g + 1)
                chunks = (g + 2) * HC - 1 if exists(l, t + 1) else LAST * HC
                for m in range(HC):
                    if m < 3:
                        pe.wait_ge((rk, kv_sum, rq)[m], chunks)
                    else:
                        pe.wait_ge(h_act, g * HC + (m - 2))
                    split_product(PS[:, m % 3, :], W1HI[:, m], W1LO[:, m], X1HI, X1LO).then_inc(h_mm, 1)

            def slot(l, t, first=False):
                g = l * TILES + t
                n = (g + 1) * HC
                tl, tt = slot_of(l, t)
                nl, nt = slot_of(l, t + 1)
                tile, more, after = exists(l, t), exists(l, t + 1), exists(l, t + 2)
                if more:
                    project(nl, nt, 1, after_chunk(n + 1))
                if tile:
                    inputs = g + 3 if after else LAST
                    pe.wait_ge(xt_hi, inputs)
                    pe.wait_ge(xt_lo, inputs)
                    pe.wait_ge(att, n)
                    if tt == 0:
                        pe.wait_ge(wo_in, (tl + 1) * 16)
                    down(WO, ATT, 0)
                if more:
                    project(nl, nt, 2, after_chunk(n + 2))
                if tile:
                    down(WO, ATT, 1).then_inc(y_mm, 1)
                if more:
                    project(nl, nt, 3, after_chunk(n + 3))
                if tile:
                    to_tm(y_act, g + 1, yt_mm)
                if more:
                    project(nl, nt, 4, after_chunk(n + 4))
                if not first:
                    if tile:
                        pe.wait_ge(res1, g + 1)
                    wl, w = slot_of(l, t - 1)
                    if w == 0:
                        pe.wait_ge(w2_in, (wl + 1) * 16)
                    pe.wait_ge(h_act, g * HC)
                    down(W2S, H, 0)
                if more:
                    project(nl, nt, 5, after_chunk(n + 5))
                if not first:
                    down(W2S, H, 1).then_inc(z_mm, 1)
                if more:
                    project(nl, nt, 6, after_chunk(n + 6))
                if not first:
                    to_tm(z_act, g, zt_mm)
                if more:
                    project(nl, nt, 7, after_chunk(n + 7), (0, 1))
                if tile:
                    pe.wait_ge(x1, g + 1)
                    if not first:
                        pe.wait_ge(res2, g)
                    for kc in range(KD):
                        for b in range(TS):
                            ins = nc.tensor.transpose(Yfm[:, kc, b * P:(b + 1) * P],
                                                      R[:, t % 2, b, kc * P:(kc + 1) * P], ident[:, :])
                    ins.then_inc(x1t_mm, 1)
                if more:
                    project(nl, nt, 7, after_chunk(n + 7), (2,))
                if tile:
                    hidden(tl, tt, g)
                if exists(l, t + 3):
                    input_fm(g + 3, slot_of(l, t + 3)[1])
                if after:
                    al, at = slot_of(l, t + 2)
                    project(al, at, 0, [(h_act, n - 1), (h_act, n), (h_act, n - 2)])

            for t in range(2):
                if t > 0:
                    pe.wait_ge(xt_hi, t)
                    pe.wait_ge(xt_lo, t)
                input_fm(t, t)
            for c in range(HC):
                project(0, 0, c, after_chunk(c) if c >= 2 else [])
            pe.wait_ge(xt_hi, 2)
            pe.wait_ge(xt_lo, 2)
            input_fm(2, 2)
            project(0, 1, 0, after_chunk(HC))
            slot(0, 0, first=True)
            with pe.Fori(0, LAYERS - 1, 1) as l:
                for t in range(1, TILES + 1):
                    slot(l, t)
            for t in range(1, TILES + 1):
                slot(LAYERS - 1, t)

        @block.scalar
        def _(act):
            def chunk(l, t, c):
                n = (l * TILES + t) * HC + c
                p, half = c % 2, 3 * (c % 2)
                if t == 0 and c % 4 == 0:
                    cs = slice(c, c + 4)
                    act.wait_ge(ba_in[c // 4], (l + 1) * 48)
                    nc.scalar.mul(BNEG[:, :, cs], BA[:, :, cs], -1.0).then_inc(b_neg, 1)
                    act.wait_ge(b_neg, 2 * l + (c // 4 + 1))
                act.wait_ge(k_mm, n + 1)
                if not (type(n) is int and n < 2):
                    act.wait_ge(kv_sum, n - 1)
                nc.scalar.activation(EK[:, p, :], PS[:, half, :], ACT.Relu, scale=-1.0,
                                     bias=BNEG[:, 0, c:c + 1]).then_inc(nk, 1)
                nc.scalar.activation(RK[:, p, :], PS[:, half, :], ACT.Relu, bias=BA[:, 0, c:c + 1]).then_inc(rk, 1)
                act.wait_ge(nk, n + 1)
                nc.scalar.activation(EK[:, p, :], EK[:, p, :], ACT.Exp, scale=-1.0).then_inc(ek, 1)
                act.wait_ge(q_mm, n + 1)
                if not (type(n) is int and n < IRING):
                    act.wait_ge(recip, n - (IRING - 1))
                nc.scalar.activation(EQ[:, c % IRING, :], PS[:, half + 2, :], ACT.Relu, scale=-1.0,
                                     bias=BNEG[:, 2, c:c + 1]).then_inc(nq, 1)
                if not (type(n) is int and n < 2):
                    act.wait_ge(denom, n - 1)
                nc.scalar.activation(RQ[:, p, :], PS[:, half + 2, :], ACT.Relu, bias=BA[:, 2, c:c + 1]).then_inc(rq, 1)
                act.wait_ge(nq, n + 1)
                nc.scalar.activation(EQ[:, c % IRING, :], EQ[:, c % IRING, :], ACT.Exp, scale=-1.0).then_inc(eq, 1)

            def invert(l, t, c):
                n, e = (l * TILES + t) * HC + c, c % IRING
                act.wait_ge(denom, n + 1)
                if not (type(n) is int and n < IRING):
                    act.wait_ge(att, n - (IRING - 1))
                nc.scalar.activation(INV[:, e, :], EQ[:, e, :], ACT.Ln).then_inc(log, 1)
                act.wait_ge(log, n + 1)
                nc.scalar.activation(INV[:, e, :], INV[:, e, :], ACT.Exp, scale=-1.0).then_inc(inv, 1)

            def attention_tables():
                nc.scalar.preload_act_table_set("natural_log_exp_and_others")

            def input_hi(j, t):
                act.wait_ge(xt_mm, j + 1)
                nc.scalar.copy(XTHI[:, t % 2, :, :], Yfm[:, :, :]).then_inc(xt_hi, 1)

            def gelu_down(mm, bias, bias_in, done, l, t, value):
                if t == 0:
                    act.wait_ge(bias_in, (l + 1) * 16)
                act.wait_ge(mm, value)
                for m in range(KD):
                    ins = nc.scalar.activation(T[:, m, :], Yfm[:, m, :], ACT.Gelu_apprx_tanh, bias=bias[:, m:m + 1])
                ins.then_inc(done, 1)

            def hidden(l, t, g):
                if t == 0:
                    act.wait_ge(b1_in, (l + 1) * 16)
                for m in range(HC):
                    act.wait_ge(h_mm, g * HC + (m + 1))
                    nc.scalar.activation(H[:, m, :], PS[:, m % 3, :], ACT.Gelu_apprx_tanh,
                                         bias=B1[:, m:m + 1]).then_inc(h_act, 1)

            def slot(l, t, first=False):
                g = l * TILES + t
                tl, tt = slot_of(l, t)
                nl, nt = slot_of(l, t + 1)
                tile, more = exists(l, t), exists(l, t + 1)
                if more:
                    chunk(nl, nt, 1)
                    invert(nl, nt, 0)
                    chunk(nl, nt, 2)
                    invert(nl, nt, 1)
                elif tile:
                    invert(LAYERS - 1, TILES - 1, HC - 1)
                if tile:
                    gelu_down(y_mm, BO, bo_in, y_act, tl, tt, g + 1)
                if more:
                    attention_tables()
                    for c in (3, 4, 5):
                        chunk(nl, nt, c)
                        invert(nl, nt, c - 1)
                if False:
                    invert(nl, nt, 5)
                if not first:
                    wl, w = slot_of(l, t - 1)
                    gelu_down(z_mm, B2, b2_in, z_act, wl, w, g)
                if more:
                    if not first:
                        attention_tables()
                    chunk(nl, nt, 6)
                    if True:
                        invert(nl, nt, 5)
                if tile:
                    act.wait_ge(x1t_mm, g + 1)
                    nc.scalar.copy(X1HI[:, :, :], Yfm[:, :, :]).then_inc(x1_hi, 1)
                if more:
                    chunk(nl, nt, 7)
                if tile:
                    hidden(tl, tt, g)
                if more:
                    attention_tables()
                    invert(nl, nt, 6)
                if exists(l, t + 3):
                    input_hi(g + 3, t + 3)
                if exists(l, t + 2):
                    invert(nl, nt, 7)
                    al, at = slot_of(l, t + 2)
                    chunk(al, at, 0)

            attention_tables()
            input_hi(0, 0)
            input_hi(1, 1)
            for c in range(HC):
                chunk(0, 0, c)
                if c > 0:
                    invert(0, 0, c - 1)
            input_hi(2, 2)
            chunk(0, 1, 0)
            invert(0, 0, HC - 1)
            slot(0, 0, first=True)
            with act.Fori(0, LAYERS - 1, 1) as l:
                for t in range(1, TILES + 1):
                    slot(l, t)
            for t in range(1, TILES + 1):
                slot(LAYERS - 1, t)

        @block.vector
        def _(dve):
            def seq(b):
                return slice(b * SEQ, (b + 1) * SEQ)

            def keys(l, t, c):
                n = (l * TILES + t) * HC + c
                p, e, half = c % 2, c % IRING, 3 * (c % 2)
                dve.wait_ge(ek, n + 1)
                nc.vector.tensor_scalar(EK[:, p, :], EK[:, p, :], -1.0, 1.0, ALU.add, ALU.add).then_inc(k_exp, 1)
                dve.wait_ge(rk, n + 1)
                dve.wait_ge(k_exp, n + 1)
                for b in range(TS):
                    ins = nc.vector.scalar_tensor_tensor(RK[:, p, seq(b)], RK[:, p, seq(b)], 0.0, EK[:, p, seq(b)],
                                                         ALU.add, ALU.add, accum_out=SUMK[:, p, b:b + 1])
                ins.then_inc(k_sum, 1)
                dve.wait_ge(v_mm, n + 1)
                if t == 0 and c % 4 == 0:
                    dve.wait_ge(ba_in[c // 4], (l + 1) * 48)
                dve.wait_ge(k_sum, n + 1)
                for b in range(TS):
                    ins = nc.vector.scalar_tensor_tensor(EK[:, p, seq(b)], PS[:, half + 1, seq(b)], BA[:, 1, c:c + 1],
                                                         RK[:, p, seq(b)], ALU.add, ALU.mult,
                                                         accum_out=KVS[:, p, b:b + 1])
                ins.then_inc(kv_sum, 1)
                nc.vector.tensor_scalar(SUMK[:, p, :], SUMK[:, p, :], TINY, None, ALU.max).then_inc(stat, 1)
                dve.wait_ge(stat, n * 5 + 1)
                nc.vector.reciprocal(RSK[:, p, :], SUMK[:, p, :]).then_inc(stat, 1)
                dve.wait_ge(stat, n * 5 + 2)
                nc.vector.tensor_scalar(ES[:, p, :], RSK[:, p, :], EPS_ATT, None, ALU.mult).then_inc(stat, 1)
                dve.wait_ge(kv_sum, n + 1)
                if not (type(n) is int and n < IRING):
                    dve.wait_ge(att, n - (IRING - 1))
                nc.vector.tensor_tensor(CC[:, e, :], KVS[:, p, :], RSK[:, p, :], ALU.mult).then_inc(stat, 1)
                dve.wait_ge(stat, n * 5 + 4)
                nc.vector.tensor_tensor(CE[:, e, :], CC[:, e, :], ES[:, p, :], ALU.mult).then_inc(stat, 1)

            def queries(l, t, c, before=True):
                n = (l * TILES + t) * HC + c
                p, e = c % 2, c % IRING
                dve.wait_ge(eq, n + 1)
                nc.vector.tensor_scalar(EQ[:, e, :], EQ[:, e, :], -1.0, 1.0, ALU.add, ALU.add).then_inc(q_exp, 1)
                if before and not (type(n) is int and n < 1):
                    residues(n - 1, (c - 1) % HC)
                dve.wait_ge(rq, n + 1)
                dve.wait_ge(q_exp, n + 1)
                dve.wait_ge(stat, n * 5 + 3)
                for b in range(TS):
                    ins = nc.vector.scalar_tensor_tensor(EQ[:, e, seq(b)], EQ[:, e, seq(b)], ES[:, p, b:b + 1],
                                                         RQ[:, p, seq(b)], ALU.add, ALU.add)
                ins.then_inc(denom, 1)
                if before and not (type(n) is int and n < 1):
                    inverses(n - 1, (c - 1) % HC)

            def residues(n, c):
                e = c % IRING
                dve.wait_ge(inv, n + 1)
                nc.vector.tensor_tensor(EQ[:, e, :], EQ[:, e, :], INV[:, e, :], ALU.mult).then_inc(residue, 1)

            def inverses(n, c):
                e = c % IRING
                dve.wait_ge(residue, n + 1)
                nc.vector.scalar_tensor_tensor(INV[:, e, :], EQ[:, e, :], 2.0, INV[:, e, :], ALU.subtract,
                                               ALU.mult).then_inc(recip, 1)

            def input_lo(j, t):
                dve.wait_ge(xt_hi, j + 1)
                nc.vector.tensor_tensor(XTLO[:, t % 2, :, :], Yfm[:, :, :], XTHI[:, t % 2, :, :].bitcast(F32),
                                        ALU.subtract).then_inc(xt_lo, 1)

            def residual(w, value, mm, add, res):
                dve.wait_ge(mm, value)
                nc.vector.tensor_tensor(R[:, w, :, :], Ytm[:, :, :], add, ALU.add).then_inc(res, 1)

            def statistics(w, value, stats, means, res, i):
                dve.wait_ge(res, value)
                for b in range(TS):
                    ins = nc.vector.bn_stats(ST[:, b, :], R[:, w, b, :])
                ins.then_inc(stats, 1)
                dve.wait_ge(stats, value)
                nc.vector.memset(CARRY[:, :], 0.0)
                for b in range(TS):
                    ins = nc.vector.bn_aggr(MV[:, i, b, :], ST[:, b, :])
                ins.then_inc(means, 1)

            def normed(w, value, means, rstds, done, i):
                dve.wait_ge(rstds, 2 * value)
                dve.wait_ge(means, value)
                for b in range(TS):
                    ins = nc.vector.tensor_scalar(R[:, w, b, :], R[:, w, b, :], MV[:, i, b, 0:1], RSTD[:, i, b:b + 1],
                                                  ALU.subtract, ALU.mult)
                ins.then_inc(done, 1)

            def slot(l, t, first=False):
                g = l * TILES + t
                tl, tt = slot_of(l, t)
                nl, nt = slot_of(l, t + 1)
                tile, more = exists(l, t), exists(l, t + 1)
                if more:
                    for c in (1, 2):
                        keys(nl, nt, c)
                        queries(nl, nt, c)
                    keys(nl, nt, 3)
                elif tile:
                    for c in (HC - 2, HC - 1):
                        residues((LAST - 1) * HC + c, c)
                        inverses((LAST - 1) * HC + c, c)
                if tile:
                    dve.wait_ge(xn, g + 3)
                    residual(t % 2, g + 1, yt_mm, X[:, tt * TS:(tt + 1) * TS, :], res1)
                    statistics(t % 2, g + 1, st1, mv1, res1, 0)
                if more:
                    queries(nl, nt, 3)
                    keys(nl, nt, 4)
                if tile:
                    normed(t % 2, g + 1, mv1, r1, n1, 0)
                if more:
                    queries(nl, nt, 4)
                if tile:
                    rt = R[:, t % 2, :, :]
                    dve.wait_ge(n1, 2 * g + 1)
                    if tt == 0:
                        dve.wait_ge(ln1_in, (tl + 1) * 32)
                    nc.vector.tensor_tensor(rt, rt, bcast(LN1P[:, 0, :], TS), ALU.mult).then_inc(n1, 1)
                    dve.wait_ge(n1, 2 * g + 2)
                    nc.vector.tensor_tensor(rt, rt, bcast(LN1P[:, 1, :], TS), ALU.add).then_inc(x1, 1)
                if more:
                    keys(nl, nt, 5)
                    queries(nl, nt, 5)
                if not first:
                    w = (t - 1) % 2
                    residual(w, g, zt_mm, R[:, w, :, :], res2)
                if more:
                    keys(nl, nt, 6)
                if tile:
                    dve.wait_ge(x1_hi, g + 1)
                    nc.vector.tensor_tensor(X1LO[:, :, :], Yfm[:, :, :], X1HI[:, :, :].bitcast(F32),
                                            ALU.subtract).then_inc(x1_lo, 1)
                if not first:
                    statistics(w, g, st2, mv2, res2, 1)
                if more:
                    queries(nl, nt, 6)
                if not first:
                    normed(w, g, mv2, r2, n2, 1)
                if more:
                    keys(nl, nt, 7)
                    queries(nl, nt, 7, False)
                if exists(l, t + 2):
                    al, at = slot_of(l, t + 2)
                    n = (g + 2) * HC
                    residues(n - 2, HC - 2)
                    inverses(n - 2, HC - 2)
                    residues(n - 1, HC - 1)
                    inverses(n - 1, HC - 1)
                if exists(l, t + 3):
                    input_lo(g + 3, t + 3)
                if exists(l, t + 2):
                    keys(al, at, 0)
                if exists(l, t + 2):
                    queries(al, at, 0, False)

            for t in range(TILES):
                if t % 2 == 0:
                    dve.wait_ge(x_in[t // 2], 32)
                for b in range(t * TS, (t + 1) * TS):
                    ins = nc.vector.bn_stats(ST0[:, b, :], X[:, b, :])
                ins.then_inc(mv0, 1)
                dve.wait_ge(mv0, 2 * t + 1)
                for b in range(t * TS, (t + 1) * TS):
                    ins = nc.vector.bn_aggr(MV0[:, b, :], ST0[:, b, :])
                ins.then_inc(mv0, 1)
            input_lo(0, 0)
            input_lo(1, 1)
            for c in range(HC):
                keys(0, 0, c)
                queries(0, 0, c)
            input_lo(2, 2)
            keys(0, 1, 0)
            queries(0, 1, 0)
            slot(0, 0, first=True)
            with dve.Fori(0, LAYERS - 1, 1) as l:
                for t in range(1, TILES + 1):
                    slot(l, t)
            for t in range(1, TILES + 1):
                slot(LAYERS - 1, t)


XH, XK = 16, 16
CH = P // XK
CTX = 128


def cross_attention(nc, X, ident, x, ctx_in, Wq, bq, Wk, bk, Wv, bv, Wo, bo):
    with ExitStack() as ctx:
        def sb(name, shape, dt=F32):
            return ctx.enter_context(nc.sbuf_tensor(name, shape, dt))

        def sem(name):
            return ctx.enter_context(nc.semaphore(name))

        XIN = sb("XIN", [P, SEQS, D])
        CTXS = sb("CTXS", [P, SEQS, CTX])
        WQ = sb("XWQ", [P, KD, D])
        WK = sb("XWK", [P, D])
        WV = sb("XWV", [P, D])
        WOX = sb("XWO", [P, KD, D])
        BQ = sb("XBQ", [P, KD])
        BK = sb("XBK", [P, KD])
        BV = sb("XBV", [P, D])
        BOX = sb("XBO", [P, D])
        ONES = sb("XONES", [P, 1024])
        MASK = sb("XMASK", [P, CH, SEQ])
        HALF = sb("XHALF", [P, SEQS])
        ST = sb("XST", [P, SEQS, 6])
        MV = sb("XMV", [P, SEQS, 2])
        RSTD = sb("XRSTD", [P, SEQS])
        Z = sb("XZ", [P, 2, D])
        CSEQ = sb("XCSEQ", [P, 2, CTX])
        ZT = sb("XZT", [P, 2, KD, P])
        CT = sb("XCT", [P, 2, P])
        QT = sb("XQT", [P, 2, KD, P])
        KT = sb("XKT", [P, 2, KD, P])
        KX = sb("XKX", [P, 2, CH, SEQ])
        V1 = sb("XV1", [P, 2, XH, XK + 1])
        MX = sb("XMX", [P, 2, CH])
        E = sb("XE", [P, 2, CH, SEQ])
        ET = sb("XET", [P, 2, CH, SEQ])
        RD = sb("XRD", [P, 2, CH])
        O = sb("XO", [P, 2, D])
        OT = sb("XOT", [P, 2, KD, P])
        S = ctx.enter_context(nc.psum_tensor("XS", [P, 2, CH * SEQ], F32))
        PT = ctx.enter_context(nc.psum_tensor("XPT", [P, CH * SEQ], F32))
        A = ctx.enter_context(nc.psum_tensor("XA", [P, 512], F32))
        B = ctx.enter_context(nc.psum_tensor("XB", [P, 512], F32))

        x_in, c_in, w_in, bias_in = (sem(n) for n in ("xx_in", "xc_in", "xw_in", "xbias_in"))
        set0, ones_set, v0, r0, mask_set, kx = (sem(n) for n in ("xset0", "xones_set", "xv0", "xr0", "xmask_set", "xkx"))
        prep, z, mx, sh, rd, o, v1, ob, upd = (
            sem(n) for n in ("xprep", "xz", "xmx", "xsh", "xrd", "xo", "xv1", "xob", "xupd"))
        zct_mm, qk_mm, v_mm, s_mm, pt_mm, pv_mm, ot_mm, p_mm = (
            sem(n) for n in ("xzct_mm", "xqk_mm", "xv_mm", "xs_mm", "xpt_mm", "xpv_mm", "xot_mm", "xp_mm"))
        zct, qt, kt, e, et, ot = (sem(n) for n in ("xzct", "xqt", "xkt", "xe", "xet", "xot"))
        block = ctx.enter_context(nc.Block())

        @block.sync
        def _(sp):
            sp.dma_start(XIN[:, :, :], x.rearrange("b s d -> s b d")).then_inc(x_in, 16)
            sp.dma_start(CTXS[:, :, :], ctx_in.rearrange("b s d -> s b d")).then_inc(c_in, 16)
            sp.dma_start(WQ[:, :, :], Wq.rearrange("(c p) n -> p c n", p=P)).then_inc(w_in, 16)
            sp.dma_start(WK[:, :], Wk).then_inc(w_in, 16)
            sp.dma_start(WV[:, :], Wv).then_inc(w_in, 16)
            sp.dma_start(WOX[:, :, :], Wo.rearrange("(c p) n -> p c n", p=P)).then_inc(w_in, 16)
            sp.dma_start(BQ[:, :], bq.rearrange("(c p) -> p c", p=P), allow_slow_non_contiguous=True).then_inc(bias_in, 16)
            sp.dma_start(BK[:, :], bk.rearrange("(c p) -> p c", p=P), allow_slow_non_contiguous=True).then_inc(bias_in, 16)
            sp.dma_start(BV[:, :], bv.unsqueeze(0).to_broadcast([P, D])).then_inc(bias_in, 16)
            sp.dma_start(BOX[:, :], bo.unsqueeze(0).to_broadcast([P, D])).then_inc(bias_in, 16)

        @block.gpsimd
        def _(pool):
            nc.gpsimd.memset(HALF[:, :], -0.5).then_inc(set0, 1)
            nc.gpsimd.memset(MASK[:, :, :], 1.0).then_inc(set0, 1)
            nc.gpsimd.memset(V1[:, :, :, XK:XK + 1], 1.0).then_inc(ones_set, 1)
            pool.wait_ge(set0, 2)
            nc.gpsimd.affine_select(out=MASK[:, :, :], in_=MASK[:, :, :], compare_op=ALU.is_ge, fill=0.0, base=0,
                                    pattern=[[-XK, CH], [0, SEQ]], channel_multiplier=1).then_inc(mask_set, 1)
            pool.wait_ge(mask_set, 1)
            nc.gpsimd.affine_select(out=MASK[:, :, :], in_=MASK[:, :, :], compare_op=ALU.is_ge, fill=0.0, base=XK - 1,
                                    pattern=[[XK, CH], [0, SEQ]], channel_multiplier=-1).then_inc(mask_set, 1)
            pool.wait_ge(prep, 3)
            nc.gpsimd.tensor_scalar(RSTD[:, :], MV[:, :, 1], 1e-5, None, ALU.add).then_inc(v0, 1)
            pool.wait_ge(v0, 1)
            nc.gpsimd.tensor_tensor(RSTD[:, :], RSTD[:, :], HALF[:, :], ALU.pow).then_inc(r0, 1)
            pool.wait_ge(mask_set, 2)

            def apart(i, j, c):
                u = (2 * i + j) * KD + c
                pool.wait_ge(kt, 2 * i + (j + 1))
                if not (type(i) is int and u < 2):
                    pool.wait_ge(s_mm, u - 1)
                nc.gpsimd.tensor_tensor(KX[:, c, :, :], bcast(KT[:, j, c, :], CH), MASK[:, :, :], ALU.mult).then_inc(kx, 1)

            for j in range(2):
                for c in range(KD):
                    apart(0, j, c)
            with pool.Fori(1, SEQS // 2, 1) as i:
                for j in range(2):
                    for c in range(KD):
                        apart(i, j, c)

        def step(i, j):
            b = 2 * i + j
            known = type(i) is int
            return b, not (known and b == 0), not (known and b >= SEQS - 1), not (known and b >= SEQS - 2)

        def steps(engine, run):
            for j in range(2):
                run(0, j)
            with engine.Fori(1, SEQS // 2 - 1, 1) as i:
                for j in range(2):
                    run(i, j)
            for j in range(2):
                run(SEQS // 2 - 1, j)

        @block.tensor
        def _(pe):
            def turn_inputs(b, j):
                pe.wait_ge(z, b + 1)
                if not (type(b) is int and b == 0):
                    pe.wait_ge(v1, b)
                for kc in range(KD):
                    nc.tensor.transpose(A[:, kc * P:(kc + 1) * P], Z[:, j, kc * P:(kc + 1) * P], ident[:, :])
                nc.tensor.transpose(A[:, 2 * P:3 * P], CSEQ[:, j, :], ident[:, :]).then_inc(zct_mm, 1)

            def make_qk(b, j):
                pe.wait_ge(zct, b + 1)
                for c in range(KD):
                    ins = nc.tensor.matmul(A[:, (2 + c) * P:(3 + c) * P], WK[:, c * P:(c + 1) * P], CT[:, j, :],
                                           start=True, stop=True)
                for c in range(KD):
                    for kc in range(KD):
                        ins = nc.tensor.matmul(A[:, c * P:(c + 1) * P], WQ[:, kc, c * P:(c + 1) * P], ZT[:, j, kc, :],
                                               start=(kc == 0), stop=(kc == KD - 1))
                ins.then_inc(qk_mm, 1)

            def make_v(b, j):
                pe.wait_ge(qt, b + 1)
                pe.wait_ge(kt, b + 1)
                nc.tensor.matmul(A[:, 0:D], CT[:, j, :], WV[:, :], start=True, stop=True).then_inc(v_mm, 1)

            def scores(b, j, c):
                u = b * KD + c
                pe.wait_ge(kx, u + 1)
                if not (type(b) is int and u < 2):
                    pe.wait_ge(sh, u - 1)
                for hf in range(2):
                    ins = nc.tensor.matmul(S[:, c, hf * 512:(hf + 1) * 512], QT[:, j, c, :],
                                           KX[:, c, hf * 4:(hf + 1) * 4, :].rearrange("p h s -> p (h s)"),
                                           start=True, stop=True)
                ins.then_inc(s_mm, 1)

            def turn_weights(b, j, c):
                u = b * KD + c
                pe.wait_ge(e, u + 1)
                if not (type(b) is int and u < 1):
                    pe.wait_ge(et, u)
                for h in range(CH):
                    ins = nc.tensor.transpose(PT[:, h * SEQ:(h + 1) * SEQ], E[:, c, h, :], ident[:, :])
                ins.then_inc(pt_mm, 1)

            def weigh(b, j, c):
                u = b * KD + c
                pe.wait_ge(et, u + 1)
                pe.wait_ge(v1, b + 1)
                if not (type(b) is int and u < 1):
                    pe.wait_ge(o, u)
                for h in range(CH):
                    ins = nc.tensor.matmul(B[:, h * (XK + 1):(h + 1) * (XK + 1)], ET[:, c, h, :], V1[:, j, c * CH + h, :],
                                           start=True, stop=True)
                ins.then_inc(pv_mm, 1)

            def turn_output(b, j, outputs):
                pe.wait_ge(o, outputs)
                for kc in range(KD):
                    ins = nc.tensor.transpose(B[:, 256 + kc * P:256 + (kc + 1) * P], O[:, j, kc * P:(kc + 1) * P],
                                              ident[:, :])
                ins.then_inc(ot_mm, 1)

            def project(b, j):
                pe.wait_ge(ot, b + 1)
                for kc in range(KD):
                    ins = nc.tensor.matmul(B[:, 256:512], OT[:, j, kc, :], WOX[:, kc, :], start=(kc == 0),
                                           stop=(kc == KD - 1))
                ins.then_inc(p_mm, 1)

            def run(i, j):
                b, before, after, after2 = step(i, j)
                k = 1 - j
                scores(b, j, 1)
                turn_weights(b, j, 0)
                if after:
                    make_qk(b + 1, k)
                weigh(b, j, 0)
                if after:
                    make_v(b + 1, k)
                turn_weights(b, j, 1)
                if before:
                    turn_output(b - 1, k, b * KD + 1)
                if after:
                    scores(b + 1, k, 0)
                if before:
                    project(b - 1, k)
                if after2:
                    turn_inputs(b + 2, j)
                if before:
                    pe.wait_ge(upd, b)
                weigh(b, j, 1)

            pe.wait_ge(w_in, 64)
            pe.wait_ge(ones_set, 1)
            turn_inputs(0, 0)
            make_qk(0, 0)
            make_v(0, 0)
            turn_inputs(1, 1)
            scores(0, 0, 0)
            steps(pe, run)
            turn_output(SEQS - 1, 1, SEQS * KD)
            project(SEQS - 1, 1)

        @block.scalar
        def _(act):
            def inputs(b, j):
                act.wait_ge(zct_mm, b + 1)
                nc.scalar.copy(ZT[:, j, :, :], A[:, 0:2 * P].rearrange("p (c t) -> p c t", c=KD))
                nc.scalar.copy(CT[:, j, :], A[:, 2 * P:3 * P]).then_inc(zct, 1)

            def qk(b, j):
                act.wait_ge(qk_mm, b + 1)
                for c in range(KD):
                    ins = nc.scalar.activation(KT[:, j, c, :], A[:, (2 + c) * P:(3 + c) * P], ACT.Identity,
                                               bias=BK[:, c:c + 1])
                ins.then_inc(kt, 1)
                for c in range(KD):
                    ins = nc.scalar.activation(QT[:, j, c, :], A[:, c * P:(c + 1) * P], ACT.Identity, bias=BQ[:, c:c + 1])
                ins.then_inc(qt, 1)

            def weights(b, c):
                act.wait_ge(sh, b * KD + (c + 1))
                nc.scalar.activation(E[:, c, :, :], E[:, c, :, :], ACT.Exp, scale=XK ** -0.5).then_inc(e, 1)

            def turned_weights(b, c):
                act.wait_ge(pt_mm, b * KD + (c + 1))
                nc.scalar.copy(ET[:, c, :, :], PT[:, :].rearrange("p (h s) -> p h s", h=CH)).then_inc(et, 1)

            def turned_output(b, j):
                act.wait_ge(ot_mm, b + 1)
                nc.scalar.copy(OT[:, j, :, :], B[:, 256:512].rearrange("p (c t) -> p c t", c=KD)).then_inc(ot, 1)

            def run(i, j):
                b, before, after, after2 = step(i, j)
                k = 1 - j
                turned_weights(b, 0)
                if after:
                    qk(b + 1, k)
                weights(b, 1)
                turned_weights(b, 1)
                if before:
                    turned_output(b - 1, k)
                if after:
                    weights(b + 1, 0)
                if after2:
                    inputs(b + 2, j)

            act.wait_ge(bias_in, 64)
            inputs(0, 0)
            qk(0, 0)
            inputs(1, 1)
            weights(0, 0)
            steps(act, run)
            turned_output(SEQS - 1, 1)

        @block.vector
        def _(dve):
            def normed(b, j):
                if not (type(b) is int and b < 2):
                    dve.wait_ge(zct_mm, b - 1)
                nc.vector.tensor_copy(CSEQ[:, j, :], CTXS[:, b, :])
                nc.vector.tensor_scalar(Z[:, j, :], X[:, b, :], MV[:, b, 0:1], RSTD[:, bass.ds(b, 1)], ALU.subtract,
                                        ALU.mult).then_inc(z, 1)

            def values(b, j):
                dve.wait_ge(v_mm, b + 1)
                nc.vector.tensor_tensor(V1[:, j, :, 0:XK], A[:, 0:D].rearrange("p (h k) -> p h k", h=XH),
                                        BV[:, :].rearrange("p (h k) -> p h k", h=XH), ALU.add).then_inc(v1, 1)

            def shifted(b, c):
                u = b * KD + c
                dve.wait_ge(s_mm, u + 1)
                scores = S[:, c, :].rearrange("p (h s) -> p h s", h=CH)
                nc.vector.tensor_reduce(MX[:, c, :], scores, AX.X, ALU.max).then_inc(mx, 1)
                dve.wait_ge(mx, u + 1)
                nc.vector.tensor_tensor(E[:, c, :, :], scores, spread(MX[:, c, :], SEQ), ALU.subtract).then_inc(sh, 1)

            def output(b, j, c):
                u = b * KD + c
                dve.wait_ge(pv_mm, u + 1)
                out = B[:, 0:CH * (XK + 1)].rearrange("p (h k) -> p h k", h=CH)
                nc.vector.reciprocal(RD[:, c, :], out[:, :, XK]).then_inc(rd, 1)
                dve.wait_ge(rd, u + 1)
                nc.vector.tensor_tensor(O[:, j, c * P:(c + 1) * P].rearrange("p (h k) -> p h k", h=CH),
                                        out[:, :, 0:XK], spread(RD[:, c, :], XK), ALU.mult).then_inc(o, 1)

            def update(b):
                dve.wait_ge(p_mm, b + 1)
                dve.wait_ge(ob, b + 1)
                nc.vector.tensor_tensor(X[:, b, :], X[:, b, :], B[:, 256:512], ALU.add).then_inc(upd, 1)

            def run(i, j):
                b, before, after, after2 = step(i, j)
                k = 1 - j
                nc.vector.tensor_tensor(X[:, b, :], X[:, b, :], BOX[:, :], ALU.add).then_inc(ob, 1)
                shifted(b, 1)
                output(b, j, 0)
                if after:
                    values(b + 1, k)
                if after2:
                    normed(b + 2, j)
                if before:
                    update(b - 1)
                if after:
                    shifted(b + 1, 0)
                output(b, j, 1)

            dve.wait_ge(x_in, 16)
            nc.vector.tensor_tensor(X[:, :, :], X[:, :, :], XIN[:, :, :], ALU.add).then_inc(prep, 1)
            dve.wait_ge(prep, 1)
            for b in range(SEQS):
                ins = nc.vector.bn_stats(ST[:, b, :], X[:, b, :])
            ins.then_inc(prep, 1)
            dve.wait_ge(prep, 2)
            for b in range(SEQS):
                ins = nc.vector.bn_aggr(MV[:, b, :], ST[:, b, :])
            ins.then_inc(prep, 1)
            dve.wait_ge(r0, 1)
            dve.wait_ge(prep, 3)
            dve.wait_ge(bias_in, 64)
            dve.wait_ge(c_in, 16)
            normed(0, 0)
            normed(1, 1)
            values(0, 0)
            shifted(0, 0)
            steps(dve, run)
            update(SEQS - 1)


E, FF = 8, 512
FC = FF // P
RT = SEQS + E - 1
ROWS = RT * P


def mixture(nc, X, ident, out, gate_w, shared, routed):
    rows_in = nc.dram_tensor("rows_in", (ROWS, D), F32, kind="Internal").ap()
    rows_out = nc.dram_tensor("rows_out", (ROWS, D), F32, kind="Internal").ap()
    with ExitStack() as ctx:
        def sb(name, shape, dt=F32):
            return ctx.enter_context(nc.sbuf_tensor(name, shape, dt))

        WGU = sb("WGU", [P, E, 2, KD, FF])
        WD = sb("WD", [P, E, FC, D])
        EID = sb("EID", [P, RT], I32)
        ROW = sb("ROW", [P, SEQS], U32)
        PSX = ctx.enter_context(nc.psum_tensor("PSX", [P, 8, 512], F32))
        route(nc, X, ident, gate_w, shared, routed, rows_in, WGU, WD, EID, ROW, PSX)
        experts(nc, ident, rows_in, rows_out, WGU, WD, EID, PSX)
        combine(nc, X, rows_out, ROW, out)


def route(nc, X, ident, gate_w, shared, routed, rows_in, WGU, WD, EID, ROW, PSX):
    with ExitStack() as ctx:
        def sb(name, shape, dt=F32):
            return ctx.enter_context(nc.sbuf_tensor(name, shape, dt))

        def sem(name):
            return ctx.enter_context(nc.semaphore(name))

        RAW = sb("RAW", [P, 3, 1024])
        ZERO = sb("ZERO", [P, D])
        ZN = sb("ZN", [P, SEQS, D])
        ZG = sb("ZG", [P, TILES, KD, TOK])
        SGU = sb("SGU", [P, 2, KD, FF])
        SD = sb("SD", [P, FC, D])
        SGS = sb("SGS", [P, 2, TOK])
        HS = sb("HS", [P, FC, TOK])
        GW = sb("GW", [E, D])
        GT = sb("GT", [P, KD, E])
        ST = sb("RST", [P, SEQS, 6])
        MV = sb("RMV", [P, SEQS, 2])
        RSTD = sb("RRSTD", [P, SEQS])
        HALF = sb("RHALF", [P, SEQS])
        BEFORE = sb("BEFORE", [P, P])
        ONES = sb("RONES", [P, P])
        IOTE = sb("IOTE", [P, SEQS, E])
        IOT128 = sb("IOT128", [P, E, SEQS])
        IOTU = sb("IOTU", [P, RT, E])
        LG = sb("LG", [P, SEQS, E])
        MXL = sb("MXL", [P, SEQS])
        SC = sb("SC", [P, SEQS])
        PICK = sb("PICK", [P, SEQS, E])
        IDX = sb("IDX", [P, SEQS])
        OH = sb("OH", [P, SEQS, E])
        TOTS = sb("TOTS", [P, SEQS, E])
        BASE = sb("BASE", [P, SEQS + 1, E])
        MORE = sb("MORE", [P, E, SEQS])
        NT = sb("NT", [P, E])
        START = sb("START", [P, E + 1])
        PAST = sb("PAST", [P, RT, E])
        EIDF = sb("EIDF", [P, RT])
        RB = sb("RB", [P, E])
        POS = sb("POS", [P, SEQS, E])
        POSF = sb("POSF", [P, SEQS])

        raw_in = [sem(f"raw_in{i}") for i in range(3)]
        gw_in, zeroed, scattered = (sem(n) for n in ("gw_in", "zeroed", "scattered"))
        consts, zero_set, before_set, v0, r0 = (sem(n) for n in ("rconsts", "zero_set", "before_set", "rv0", "rr0"))
        gt_mm, zt_mm, lg_mm, pre_mm = (sem(n) for n in ("gt_mm", "rzt_mm", "lg_mm", "pre_mm"))
        w_mm = [sem(f"w_mm{i}") for i in range(3)]
        w_sb = [sem(f"w_sb{i}") for i in range(3)]
        g_mm, u_mm, o_mm = (sem(n) for n in ("rg_mm", "ru_mm", "ro_mm"))
        gt, zg, sc, sg = (sem(n) for n in ("gt", "zg", "sc", "rsg"))
        prep, zn, step, oh, row, mxl, hs, upd = (
            sem(n) for n in ("rprep", "rzn", "rstep", "roh", "rrow", "rmxl", "rhs", "rupd"))
        xs = sem("rxs")
        block = ctx.enter_context(nc.Block())

        @block.sync
        def _(sp):
            def load(k, mats):
                for i, w in enumerate(mats):
                    if not (type(k) is int and k == 0):
                        sp.wait_ge(w_mm[i], k)
                    sp.dma_start(RAW[:, i, :].rearrange("p (c n) -> p c n", n=w.shape[1]),
                                 w.rearrange("(c p) n -> p c n", p=P)).then_inc(raw_in[i], 16)

            sp.dma_start(GW[:, :], gate_w).then_inc(gw_in, 16)
            load(0, shared)
            sp.wait_ge(zero_set, 1)
            sp.dma_start(rows_in[:, :].rearrange("(u p) d -> p u d", p=P), bcast(ZERO[:, :], RT)).then_inc(zeroed, 16)
            with sp.Fori(0, E, 1) as e:
                load(e + 1, [w[e, :, :] for w in routed])
            sp.wait_ge(zeroed, 16)

        @block.gpsimd
        def _(pool):
            nc.gpsimd.memset(ZERO[:, :], 0.0).then_inc(zero_set, 1)
            nc.gpsimd.memset(HALF[:, :], -0.5)
            nc.gpsimd.memset(ONES[:, :], 1.0)
            nc.gpsimd.memset(BASE[:, 0, :], 0.0)
            nc.gpsimd.memset(START[:, 0:1], 0.0)
            nc.gpsimd.iota(IOTE[:, :, :], pattern=[[0, SEQS], [1, E]], base=0, channel_multiplier=0,
                           allow_small_or_imprecise_dtypes=True)
            nc.gpsimd.iota(IOT128[:, :, :], pattern=[[0, E], [P, SEQS]], base=0, channel_multiplier=0,
                           allow_small_or_imprecise_dtypes=True)
            nc.gpsimd.iota(IOTU[:, :, :], pattern=[[1, RT], [0, E]], base=0, channel_multiplier=0,
                           allow_small_or_imprecise_dtypes=True)
            nc.gpsimd.memset(BEFORE[:, :], 1.0).then_inc(consts, 1)
            pool.wait_ge(consts, 1)
            nc.gpsimd.affine_select(out=BEFORE[:, :], in_=BEFORE[:, :], compare_op=ALU.is_ge, fill=0.0, base=-1,
                                    pattern=[[1, P]], channel_multiplier=-1).then_inc(before_set, 1)
            pool.wait_ge(prep, 2)
            nc.gpsimd.tensor_scalar(RSTD[:, :], MV[:, :, 1], 1e-5, None, ALU.add).then_inc(v0, 1)
            pool.wait_ge(v0, 1)
            nc.gpsimd.tensor_tensor(RSTD[:, :], RSTD[:, :], HALF[:, :], ALU.pow).then_inc(r0, 1)
            pool.wait_ge(sc, 1)
            pool.wait_ge(zt_mm, TILES)
            for b in range(SEQS):
                ins = nc.gpsimd.tensor_tensor(ZN[:, b, :], ZN[:, b, :], SC[:, b:b + 1].to_broadcast([P, D]), ALU.mult)
            ins.then_inc(xs, 1)
            pool.wait_ge(xs, 1)
            pool.wait_ge(row, 1)
            pool.wait_ge(zeroed, 16)
            for b in range(SEQS):
                pool.indirect_dma_start(out=rows_in[:, :], out_offset=bass.IndirectOffsetOnAxis(ROW[:, b:b + 1], 0),
                                        in_=ZN[:, b, :], in_offset=None).then_inc(scattered, 16)
            pool.wait_ge(scattered, 16 * SEQS)

        def turned(i, out_chunks, in_chunks):
            return [(c, n, (n * in_chunks + c) * P) for n in range(out_chunks) for c in range(in_chunks)]

        @block.tensor
        def _(pe):
            def logits(q):
                pe.wait_ge(zg, q + 1)
                for b in range(TS):
                    s = q * TS + b
                    for kc in range(KD):
                        ins = nc.tensor.matmul(PSX[:, 6, s * E:(s + 1) * E], ZG[:, q, kc, b * P:(b + 1) * P],
                                               GT[:, kc, :], start=(kc == 0), stop=(kc == KD - 1))
                return ins

            def matrix(k, i):
                oc, icn = (KD, FC) if i < 2 else (FC, KD)
                pe.wait_ge(raw_in[i], 16 * k + 16)
                if i > 0:
                    pe.wait_ge(w_sb[i - 1], k + 1)
                elif not (type(k) is int and k == 0):
                    pe.wait_ge(w_sb[2], k)
                width = oc * P
                dst = PSX[:, 0:2, :].rearrange("p b n -> p (b n)")
                for c, n, at in turned(i, oc, icn):
                    ins = nc.tensor.transpose(dst[:, at:at + P], RAW[:, i, c * width + n * P:c * width + (n + 1) * P],
                                              ident[:, :])
                ins.then_inc(w_mm[i], 1)

            def hidden(q, c):
                n = q * FC + c
                for m, (done, read) in enumerate(((g_mm, sg), (u_mm, hs))):
                    if not (type(n) is int and n < 2):
                        pe.wait_ge(read, n - 1)
                    for kc in range(KD):
                        ins = nc.tensor.matmul(PSX[:, 2 + 2 * (c % 2) + m, :], SGU[:, m, kc, c * P:(c + 1) * P],
                                               ZG[:, q, kc, :], start=(kc == 0), stop=(kc == KD - 1))
                    ins.then_inc(done, 1)

            def down(q):
                pe.wait_ge(hs, (q + 1) * FC)
                if not (type(q) is int and q == 0):
                    pe.wait_ge(upd, q)
                for b in range(TS):
                    for c in range(FC):
                        ins = nc.tensor.matmul(PSX[:, 6 + b // 2, b % 2 * D:(b % 2 + 1) * D],
                                               HS[:, c, b * P:(b + 1) * P], SD[:, c, :], start=(c == 0),
                                               stop=(c == FC - 1))
                ins.then_inc(o_mm, 1)

            def tile(q):
                for c in range(FC):
                    hidden(q, c)
                    if c < 3:
                        matrix(2 * q + 1, c)
                matrix(2 * q + 2, 0)
                matrix(2 * q + 2, 1)
                down(q)
                matrix(2 * q + 2, 2)

            pe.wait_ge(gw_in, 16)
            for kc in range(KD):
                ins = nc.tensor.transpose(PSX[:, 7, kc * E:(kc + 1) * E], GW[:, kc * P:(kc + 1) * P], ident[0:E, 0:E])
            ins.then_inc(gt_mm, 1)
            for i in range(3):
                matrix(0, i)
            for q in range(TILES):
                pe.wait_ge(zn, q + 1)
                if q >= 2:
                    pe.wait_ge(zg, q - 1)
                for kc in range(KD):
                    for b in range(TS):
                        ins = nc.tensor.transpose(PSX[:, 2 + 2 * (q % 2) + kc, b * P:(b + 1) * P],
                                                  ZN[:, q * TS + b, kc * P:(kc + 1) * P], ident[:, :])
                ins.then_inc(zt_mm, 1)
                if q == 0:
                    pe.wait_ge(gt, 1)
                if q > 0:
                    logits(q - 1)
            logits(TILES - 1).then_inc(lg_mm, 1)
            pe.wait_ge(w_sb[2], 1)
            hidden(0, 0)
            pe.wait_ge(before_set, 1)
            pe.wait_ge(oh, 1)
            ohs = OH[:, :, :].rearrange("p b e -> p (b e)")
            nc.tensor.matmul(PSX[:, 7, 0:P], BEFORE[:, :], ohs, start=True, stop=True)
            nc.tensor.matmul(PSX[:, 7, P:2 * P], ONES[:, :], ohs, start=True, stop=True).then_inc(pre_mm, 1)
            matrix(1, 0)
            for c in range(1, FC):
                hidden(0, c)
                if c < 3:
                    matrix(1, c)
            matrix(2, 0)
            matrix(2, 1)
            pe.wait_ge(row, 1)
            down(0)
            matrix(2, 2)
            with pe.Fori(1, TILES, 1) as q:
                tile(q)

        @block.scalar
        def _(act):
            def matrix(k, gate_up, down, i):
                act.wait_ge(w_mm[i], k + 1)
                src = PSX[:, 0:2, :].rearrange("p b n -> p (b n)")
                dst = (gate_up[:, i, :, :] if i < 2 else down).rearrange("p c n -> p (c n)")
                nc.scalar.copy(dst, src).then_inc(w_sb[i], 1)

            def routed_matrix(k, i):
                matrix(k, WGU[:, k - 1, :, :, :], WD[:, k - 1, :, :], i)

            def silu(q, c):
                n = q * FC + c
                act.wait_ge(g_mm, n + 1)
                if not (type(n) is int and n < 2):
                    act.wait_ge(hs, n - 1)
                nc.scalar.activation(SGS[:, c % 2, :], PSX[:, 2 + 2 * (c % 2), :], ACT.Silu).then_inc(sg, 1)

            def tile(q):
                for c in range(FC):
                    silu(q, c)
                    if c < 3:
                        routed_matrix(2 * q + 1, c)
                for i in range(3):
                    routed_matrix(2 * q + 2, i)

            act.wait_ge(gt_mm, 1)
            nc.scalar.copy(GT[:, :, :], PSX[:, 7, 0:KD * E].rearrange("p (c e) -> p c e", c=KD)).then_inc(gt, 1)
            for i in range(3):
                matrix(0, SGU, SD[:, :, :], i)
            for q in range(TILES):
                act.wait_ge(zt_mm, q + 1)
                nc.scalar.copy(ZG[:, q, :, :], PSX[:, 2 + 2 * (q % 2):4 + 2 * (q % 2), :]).then_inc(zg, 1)
            act.wait_ge(mxl, 1)
            nc.scalar.activation(SC[:, :], MXL[:, :], ACT.Sigmoid).then_inc(sc, 1)
            tile(0)
            with act.Fori(1, TILES, 1) as q:
                tile(q)

        @block.vector
        def _(dve):
            for b in range(SEQS):
                ins = nc.vector.bn_stats(ST[:, b, :], X[:, b, :])
            ins.then_inc(prep, 1)
            dve.wait_ge(prep, 1)
            for b in range(SEQS):
                ins = nc.vector.bn_aggr(MV[:, b, :], ST[:, b, :])
            ins.then_inc(prep, 1)
            dve.wait_ge(r0, 1)
            dve.wait_ge(prep, 2)
            for q in range(TILES):
                for b in range(q * TS, (q + 1) * TS):
                    ins = nc.vector.tensor_scalar(ZN[:, b, :], X[:, b, :], MV[:, b, 0:1], RSTD[:, b:b + 1], ALU.subtract,
                                                  ALU.mult)
                ins.then_inc(zn, 1)
            steps = [0]

            def then(ins):
                steps[0] += 1
                ins.then_inc(step, 1)
                dve.wait_ge(step, steps[0])

            dve.wait_ge(consts, 1)
            dve.wait_ge(lg_mm, 1)
            then(nc.vector.tensor_copy(LG[:, :, :], PSX[:, 6, 0:P].rearrange("p (b e) -> p b e", e=E)))
            nc.vector.tensor_reduce(MXL[:, :], LG[:, :, :], AX.X, ALU.max).then_inc(mxl, 1)
            dve.wait_ge(mxl, 1)
            then(nc.vector.tensor_tensor(PICK[:, :, :], LG[:, :, :], spread(MXL[:, :], E), ALU.is_lt))
            then(nc.vector.scalar_tensor_tensor(PICK[:, :, :], PICK[:, :, :], float(E), IOTE[:, :, :], ALU.mult, ALU.add))
            then(nc.vector.tensor_reduce(IDX[:, :], PICK[:, :, :], AX.X, ALU.min))
            nc.vector.tensor_tensor(OH[:, :, :], IOTE[:, :, :], spread(IDX[:, :], E), ALU.is_equal).then_inc(oh, 1)
            dve.wait_ge(pre_mm, 1)
            then(nc.vector.tensor_copy(TOTS[:, :, :], PSX[:, 7, P:2 * P].rearrange("p (b e) -> p b e", e=E)))
            for b in range(SEQS):
                then(nc.vector.tensor_tensor(BASE[:, b + 1, :], BASE[:, b, :], TOTS[:, b, :], ALU.add))
            then(nc.vector.tensor_tensor(MORE[:, :, :], spread(BASE[:, SEQS, :], SEQS), IOT128[:, :, :], ALU.is_gt))
            then(nc.vector.tensor_reduce(NT[:, :], MORE[:, :, :], AX.X, ALU.add))
            for e in range(E):
                then(nc.vector.tensor_tensor(START[:, e + 1:e + 2], START[:, e:e + 1], NT[:, e:e + 1], ALU.add))
            then(nc.vector.tensor_tensor(PAST[:, :, :], bcast(START[:, 1:E + 1], RT), IOTU[:, :, :], ALU.is_le))
            then(nc.vector.tensor_reduce(EIDF[:, :], PAST[:, :, :], AX.X, ALU.add))
            then(nc.vector.tensor_scalar(EID[:, :], EIDF[:, :], float(E - 1), None, ALU.min))
            then(nc.vector.tensor_scalar(RB[:, :], START[:, 0:E], float(P), None, ALU.mult))
            then(nc.vector.tensor_tensor(POS[:, :, :], BASE[:, 0:SEQS, :], bcast(RB[:, :], SEQS), ALU.add))
            then(nc.vector.tensor_tensor(POS[:, :, :], POS[:, :, :], PSX[:, 7, 0:P].rearrange("p (b e) -> p b e", e=E),
                                         ALU.add))
            dve.wait_ge(oh, 1)
            then(nc.vector.tensor_tensor(POS[:, :, :], POS[:, :, :], OH[:, :, :], ALU.mult))
            then(nc.vector.tensor_reduce(POSF[:, :], POS[:, :, :], AX.X, ALU.add))
            nc.vector.tensor_copy(ROW[:, :], POSF[:, :]).then_inc(row, 1)

            def shared_tile(q):
                for c in range(FC):
                    n = q * FC + c
                    dve.wait_ge(sg, n + 1)
                    dve.wait_ge(u_mm, n + 1)
                    if c == 0 and not (type(q) is int and q == 0):
                        dve.wait_ge(o_mm, q)
                    nc.vector.tensor_tensor(HS[:, c, :], SGS[:, c % 2, :], PSX[:, 3 + 2 * (c % 2), :],
                                            ALU.mult).then_inc(hs, 1)
                dve.wait_ge(o_mm, q + 1)
                for b in range(2):
                    x2 = X[:, bass.ds(q * TS + 2 * b, 2), :]
                    ins = nc.vector.tensor_tensor(x2, x2, PSX[:, 6 + b, :].rearrange("p (s d) -> p s d", s=2), ALU.add)
                ins.then_inc(upd, 1)

            shared_tile(0)
            with dve.Fori(1, TILES, 1) as q:
                shared_tile(q)


def experts(nc, ident, rows_in, rows_out, WGU, WD, EID, PSX):
    with ExitStack() as ctx:
        def sb(name, shape, dt=F32):
            return ctx.enter_context(nc.sbuf_tensor(name, shape, dt))

        def sem(name):
            return ctx.enter_context(nc.semaphore(name))

        XU = sb("XU", [P, 2, D])
        XTU = sb("XTU", [P, 2, KD, P])
        SG = sb("SG", [P, 2, FF])
        AC = sb("AC", [P, 2, FF])
        AT = sb("AT", [P, 2, FC, P])
        OU = sb("OU", [P, 2, D])
        xu_in = [sem(f"xu_in{j}") for j in range(2)]
        stored = [sem(f"stored{j}") for j in range(2)]
        xt_mm, g_mm, u_mm, at_mm, o_mm = (sem(n) for n in ("uxt_mm", "g_mm", "u_mm", "at_mm", "o_mm"))
        xt, sg, ac, at, ou = (sem(n) for n in ("uxt", "sg", "ac", "at", "ou"))
        PAIRS = RT // 2
        block = ctx.enter_context(nc.Block())

        @block.sync
        def _(sp):
            def load(i, j):
                u = 2 * i + j
                if not (type(i) is int and i == 0):
                    sp.wait_ge(xt_mm, u - 1)
                sp.dma_start(XU[:, j, :], rows_in[bass.ds(u * P, P), :]).then_inc(xu_in[j], 16)

            for j in range(2):
                load(0, j)
            with sp.Fori(1, PAIRS, 1) as i:
                for j in range(2):
                    load(i, j)
            load(PAIRS, 0)

        @block.gpsimd
        def _(pool):
            def store(i, j):
                u = 2 * i + j
                pool.wait_ge(ou, u + 1)
                pool.dma_start(rows_out[bass.ds(u * P, P), :], OU[:, j, :]).then_inc(stored[j], 16)

            with pool.Fori(0, PAIRS, 1) as i:
                for j in range(2):
                    store(i, j)
            store(PAIRS, 0)
            pool.wait_ge(stored[0], 16 * (PAIRS + 1))
            pool.wait_ge(stored[1], 16 * PAIRS)

        @block.tensor
        def _(pe):
            def turn_input(i, j):
                u = 2 * i + j
                pe.wait_ge(xu_in[j], 16 * i + 16)
                if not (type(i) is int and u == 0):
                    pe.wait_ge(xt, u)
                for kc in range(KD):
                    ins = nc.tensor.transpose(PSX[:, 6, kc * P:(kc + 1) * P], XU[:, j, kc * P:(kc + 1) * P], ident[:, :])
                ins.then_inc(xt_mm, 1)

            def gate_up(i, j):
                u = 2 * i + j
                e = nc.tensor.value_load(EID[0:1, bass.ds(u, 1)], min_val=0, max_val=E - 1)
                pe.wait_ge(xt, u + 1)
                for m, done in enumerate((g_mm, u_mm)):
                    if not (type(i) is int and i == 0):
                        pe.wait_ge((sg, ac)[m], u - 1)
                    for kc in range(KD):
                        ins = nc.tensor.matmul(PSX[:, 2 * m + j, :], XTU[:, j, kc, :], WGU[:, e, m, kc, :],
                                               start=(kc == 0), stop=(kc == KD - 1))
                    ins.then_inc(done, 1)

            def turn_hidden(i, j):
                u = 2 * i + j
                pe.wait_ge(ac, u + 1)
                if not (type(i) is int and u == 0):
                    pe.wait_ge(at, u)
                for c in range(FC):
                    ins = nc.tensor.transpose(PSX[:, 4, c * P:(c + 1) * P], AC[:, j, c * P:(c + 1) * P], ident[:, :])
                ins.then_inc(at_mm, 1)

            def down(i, j):
                u = 2 * i + j
                e = nc.tensor.value_load(EID[0:1, bass.ds(u, 1)], min_val=0, max_val=E - 1)
                pe.wait_ge(at, u + 1)
                if not (type(i) is int and i == 0):
                    pe.wait_ge(ou, u - 1)
                for c in range(FC):
                    ins = nc.tensor.matmul(PSX[:, 5 + 2 * j, 0:D], AT[:, j, c, :], WD[:, e, c, :], start=(c == 0),
                                           stop=(c == FC - 1))
                ins.then_inc(o_mm, 1)

            def pair(i, more):
                turn_hidden(i, 0)
                gate_up(i, 1)
                turn_input(i + 1, 0)
                down(i, 0)
                turn_hidden(i, 1)
                gate_up(i + 1, 0)
                if more:
                    turn_input(i + 1, 1)
                down(i, 1)

            turn_input(0, 0)
            turn_input(0, 1)
            gate_up(0, 0)
            pair(0, True)
            with pe.Fori(1, PAIRS - 1, 1) as i:
                pair(i, True)
            pair(PAIRS - 1, False)
            turn_hidden(PAIRS, 0)
            down(PAIRS, 0)

        @block.scalar
        def _(act):
            def evac_input(i, j):
                act.wait_ge(xt_mm, 2 * i + (j + 1))
                nc.scalar.copy(XTU[:, j, :, :], PSX[:, 6, 0:D].rearrange("p (c t) -> p c t", c=KD)).then_inc(xt, 1)

            def silu(i, j):
                u = 2 * i + j
                act.wait_ge(g_mm, u + 1)
                nc.scalar.activation(SG[:, j, :], PSX[:, j, :], ACT.Silu).then_inc(sg, 1)

            def evac_hidden(i, j):
                act.wait_ge(at_mm, 2 * i + (j + 1))
                nc.scalar.copy(AT[:, j, :, :], PSX[:, 4, :].rearrange("p (c t) -> p c t", c=FC)).then_inc(at, 1)

            def pair(i, more):
                evac_hidden(i, 0)
                silu(i, 1)
                evac_input(i + 1, 0)
                evac_hidden(i, 1)
                silu(i + 1, 0)
                if more:
                    evac_input(i + 1, 1)

            evac_input(0, 0)
            evac_input(0, 1)
            silu(0, 0)
            with act.Fori(0, PAIRS - 1, 1) as i:
                pair(i, True)
            pair(PAIRS - 1, False)
            evac_hidden(PAIRS, 0)

        @block.vector
        def _(dve):
            def product(i, j):
                u = 2 * i + j
                dve.wait_ge(sg, u + 1)
                dve.wait_ge(u_mm, u + 1)
                nc.vector.tensor_tensor(AC[:, j, :], SG[:, j, :], PSX[:, 2 + j, :], ALU.mult).then_inc(ac, 1)

            def result(i, j, first):
                u = 2 * i + j
                dve.wait_ge(o_mm, u + 1)
                if not first:
                    dve.wait_ge(stored[j], 16 * i)
                nc.vector.tensor_copy(OU[:, j, :], PSX[:, 5 + 2 * j, 0:D]).then_inc(ou, 1)

            def pair(i, first):
                product(i, 1)
                result(i, 0, first)
                product(i + 1, 0)
                result(i, 1, first)

            product(0, 0)
            pair(0, True)
            with dve.Fori(1, PAIRS, 1) as i:
                pair(i, False)
            result(PAIRS, 0, False)


def combine(nc, X, rows_out, ROW, out):
    with ExitStack() as ctx:
        def sem(name):
            return ctx.enter_context(nc.semaphore(name))

        RO = ctx.enter_context(nc.sbuf_tensor("RO", [P, SEQS, D], F32))
        ro_in = [sem(f"ro_in{h}") for h in range(2)]
        ready, written = sem("ready"), sem("written")
        block = ctx.enter_context(nc.Block())

        @block.sync
        def _(sp):
            for t in range(TILES):
                sp.wait_ge(ready, t + 1)
                sp.dma_start(out[t * TS:(t + 1) * TS, :, :].rearrange("b s d -> s b d"),
                             X[:, t * TS:(t + 1) * TS, :]).then_inc(written, 16)
            sp.wait_ge(written, 16 * TILES)

        @block.gpsimd
        def _(pool):
            for b in range(SEQS):
                pool.indirect_dma_start(out=RO[:, b, :], out_offset=None, in_=rows_out[:, :],
                                        in_offset=bass.IndirectOffsetOnAxis(ROW[:, b:b + 1], 0)
                                        ).then_inc(ro_in[b // (SEQS // 2)], 16)

        @block.vector
        def _(dve):
            for t in range(TILES):
                bs = slice(t * TS, (t + 1) * TS)
                dve.wait_ge(ro_in[t // 2], 16 * SEQS // 2)
                nc.vector.tensor_tensor(X[:, bs, :], X[:, bs, :], RO[:, bs, :], ALU.add).then_inc(ready, 1)


def decoder(nc, a, out):
    with ExitStack() as ctx:
        X = ctx.enter_context(nc.sbuf_tensor("X", [P, SEQS, D], F32))
        ident = ctx.enter_context(nc.sbuf_tensor("ident", [P, P], F32))
        ident_set = ctx.enter_context(nc.semaphore("ident_set"))
        with nc.Block() as block:
            @block.gpsimd
            def _(pool):
                nc.gpsimd.memset(ident[:, :], 0.0).then_inc(ident_set, 1)
                pool.wait_ge(ident_set, 1)
                nc.gpsimd.affine_select(out=ident[:, :], in_=ident[:, :], compare_op=ALU.not_equal, fill=1.0, base=0,
                                        pattern=[[-1, P]], channel_multiplier=1).then_inc(ident_set, 1)
                pool.wait_ge(ident_set, 2)
        attention_stack(nc, X, ident, a["x"], *(a["L0_attn_" + n] for n in (
            "Wq", "bq", "Wk", "bk", "Wv", "bv", "Wo", "bo", "ln1_s", "ln1_b", "W1", "b1", "W2", "b2", "ln2_s", "ln2_b")))
        cross_attention(nc, X, ident, a["x"], a["ctx_512"], *(a["L0_xattn_" + n] for n in (
            "Wq", "bq", "Wk", "bk", "Wv", "bv", "Wo", "bo")))
        mixture(nc, X, ident, out, a["L0_ffn_gate_w"], [a["L0_ffn_shared_" + n] for n in ("gate", "up", "down")],
                [a["L0_ffn_r_" + n] for n in ("gate", "up", "down")])


def kernel(**inputs):
    import numpy as np
    from concourse import bacc
    from concourse.bass_utils import run_bass_kernel_spmd

    nc = bacc.Bacc("TRN2", target_bir_lowering=False, num_devices=1)
    arrays = {name: np.ascontiguousarray(a) for name, a in inputs.items()}
    aps = {name: nc.dram_tensor(name, a.shape, mybir.dt.from_np(a.dtype), kind="ExternalInput").ap()
           for name, a in arrays.items()}
    out = nc.dram_tensor("out", (SEQS, SEQ, D), F32, kind="ExternalOutput").ap()
    decoder(nc, aps, out)
    return run_bass_kernel_spmd(nc, [arrays], core_ids=[0]).results[0]["out"]
```
